# Optimizing a Trainium2 kernel written in Bass

```python
import numpy as np
import jax
import jax.numpy as jnp

def _softmax(x, axis=-1):
    return jax.nn.softmax(x, axis=axis)

def _gelu(x):
    return jax.nn.gelu(x, approximate=True)

def _silu(x):
    return jax.nn.silu(x)

def _sigmoid(x):
    return jax.nn.sigmoid(x)

def _layernorm(x, axis=-1, eps=1e-05):
    m = jnp.mean(x, axis=axis, keepdims=True)
    v = jnp.var(x, axis=axis, keepdims=True)
    return (x - m) / jnp.sqrt(v + eps)

def _scatter_add(tgt, idx, src, axis=0):
    return tgt.at[idx].add(src)

def _segment_sum(src, seg, n):
    return jax.ops.segment_sum(src, seg, n)
kernel_name = 'mk_gnn_resnorm_d4_gnn_r8_85ea5b'

def setup_inputs(seed: int=0):
    np.random.seed(seed)
    _w = jnp.asarray

    def _rec_inputs():
        import jax
        import jax.numpy as jnp
        _gk = jax.random.key(seed)
        x = -0.000202 + 1 * jax.random.normal(jax.random.fold_in(_gk, 1), (6250, 64), jnp.float32)
        _s = jax.random.randint(jax.random.fold_in(_gk, 2), (100000,), 0, 6250, jnp.int32)
        _d = jax.random.randint(jax.random.fold_in(_gk, 3), (100000,), 0, 6250, jnp.int32)
        _loop = jnp.arange(6250, dtype=jnp.int32)
        src = jnp.concatenate([_s, _d, _loop])
        dst = jnp.concatenate([_d, _s, _loop])
        _o = jnp.argsort(dst, stable=True)
        src = src[_o]
        dst = dst[_o]
        edge_attr_64 = -5.16925e-05 + 1.00005 * jax.random.normal(jax.random.fold_in(_gk, 12), (206250, 64), jnp.float32)
        return (x, src, dst, edge_attr_64)
    x, src, dst, edge_attr_64 = _rec_inputs()

    def _L0_gnn_setup():
        import jax, jax.numpy as jnp
        import numpy as np
        N = 12500
        E = 200000
        D = 64
        H = 128
        EPS = 1e-05
        NEG_SLOPE = 0.01

        def _xavier(key, shape):
            fan_in, fan_out = (shape[0], shape[1])
            limit = float(np.sqrt(6.0 / (fan_in + fan_out)))
            return jax.random.uniform(key, shape, jnp.float32, -limit, limit)

        def _bn(h, gamma, beta):
            mean = jnp.mean(h, axis=0)
            var = jnp.mean(jnp.square(h - mean), axis=0)
            return (h - mean) * jax.lax.rsqrt(var + EPS) * gamma + beta
        key = jax.random.key(seed)
        ks = jax.random.split(key, 10)
        x = jax.random.normal(ks[0], (N, D), jnp.float32)
        edge_index = jax.random.randint(ks[1], (2, E), 0, N, jnp.int64)
        edge_attr = jax.random.normal(ks[2], (E, D), jnp.float32)
        u = jax.random.normal(ks[3], (1, 16), jnp.float32)
        batch = jnp.zeros((N,), jnp.int64)
        b_init = jnp.float32(0.01)
        params = {'W1': _xavier(ks[4], (2 * D, H)), 'b1': jnp.full((H,), b_init), 'g1': jnp.ones((H,), jnp.float32), 'be1': jnp.zeros((H,), jnp.float32), 'W2': _xavier(ks[5], (H, H)), 'b2': jnp.full((H,), b_init), 'W3': _xavier(ks[6], (H + D, H)), 'b3': jnp.full((H,), b_init), 'g2': jnp.ones((H,), jnp.float32), 'be2': jnp.zeros((H,), jnp.float32), 'W4': _xavier(ks[7], (H, D)), 'b4': jnp.full((D,), b_init)}
        return {'x': x, 'edge_index': edge_index, 'edge_attr': edge_attr, 'u': u, 'batch': batch, **params}
    _L0_gnn_all = _L0_gnn_setup()
    _L0_gnn_in = {k: v for k, v in _L0_gnn_all.items() if k in ('u', 'W1', 'b1', 'g1', 'be1', 'W2', 'b2', 'W3', 'b3', 'g2', 'be2', 'W4', 'b4')}
    del _L0_gnn_all

    def _L1_gnn_setup():
        import jax, jax.numpy as jnp
        import numpy as np
        N = 6250
        E = 100000
        D_IN = 64
        D_HID = 64
        D_OUT = 64

        def _glorot(key, shape):
            lim = np.sqrt(6.0 / (shape[0] + shape[1]))
            return jax.random.uniform(key, shape, jnp.float32, -lim, lim)

        def _gcn_conv(x, W, b, src, dst, normalize, n):
            h = x @ W.T
            if normalize:
                loop = jnp.arange(n, dtype=src.dtype)
                s = jnp.concatenate([src, loop])
                d = jnp.concatenate([dst, loop])
                deg = jax.ops.segment_sum(jnp.ones_like(s, dtype=h.dtype), d, num_segments=n)
                dinv = jnp.where(deg > 0, jax.lax.rsqrt(deg), jnp.zeros_like(deg))
                norm = dinv[s] * dinv[d]
                out = jax.ops.segment_sum(h[s] * norm[:, None], d, num_segments=n)
            else:
                out = jax.ops.segment_sum(h[src], dst, num_segments=n)
            return out + b
        key = jax.random.key(seed)
        ks = jax.random.split(key, 8)
        edge_index = jax.random.randint(ks[0], (2, E), 0, N, dtype=jnp.int64)
        x_init = jax.random.normal(ks[1], (N, D_IN), jnp.float32)
        return {'edge_index': edge_index, 'x_init': x_init, 'W1': _glorot(ks[2], (D_HID, D_IN)), 'b1': jnp.zeros((D_HID,), jnp.float32), 'W2': _glorot(ks[3], (D_HID, D_HID)), 'b2': jnp.zeros((D_HID,), jnp.float32), 'W3': _glorot(ks[4], (D_OUT, D_HID)), 'b3': jnp.zeros((D_OUT,), jnp.float32)}
    _L1_gnn_all = _L1_gnn_setup()
    _L1_gnn_in = {k: v for k, v in _L1_gnn_all.items() if k in ('W1', 'b1', 'W2', 'b2', 'W3', 'b3')}
    del _L1_gnn_all

    def _L2_gnn_setup():
        import jax, jax.numpy as jnp
        import numpy as np
        N_NODES = 12500
        N_EDGES = 156250
        D_IN, D_HID = (64, 128)
        key = jax.random.key(seed)
        k_x, k_e, k_w1, k_w2 = jax.random.split(key, 4)
        x = jax.random.normal(k_x, (N_NODES, D_IN), dtype=jnp.float32)
        edge_index = jax.random.randint(k_e, (2, N_EDGES), 0, N_NODES, dtype=jnp.int64)
        W1 = jax.random.normal(k_w1, (D_IN, D_HID), dtype=jnp.float32) / np.sqrt(D_IN)
        b1 = jnp.zeros((D_HID,), dtype=jnp.float32)
        W2 = jax.random.normal(k_w2, (D_HID, D_IN), dtype=jnp.float32) / np.sqrt(D_HID)
        b2 = jnp.zeros((D_IN,), dtype=jnp.float32)
        return {'x': x, 'edge_index': edge_index, 'W1': W1, 'b1': b1, 'W2': W2, 'b2': b2}
    _L2_gnn_all = _L2_gnn_setup()
    _L2_gnn_in = {k: v for k, v in _L2_gnn_all.items() if k in ('W1', 'b1', 'W2', 'b2')}
    del _L2_gnn_all

    def _L3_gnn_setup():
        import jax, jax.numpy as jnp
        import numpy as np
        N_NODES = 6250
        N_EDGES = 100000
        D_NODE = 64
        HID = 64
        N_TGT = 64

        def _init_linear(key, fan_in, fan_out):
            kw, kb = jax.random.split(key)
            bound = 1.0 / np.sqrt(fan_in)
            W = jax.random.uniform(kw, (fan_in, fan_out), minval=-bound, maxval=bound, dtype=jnp.float32)
            b = jax.random.uniform(kb, (fan_out,), minval=-bound, maxval=bound, dtype=jnp.float32)
            return (W, b)
        key = jax.random.key(seed)
        ks = jax.random.split(key, 8)
        x = jax.random.normal(ks[0], (N_NODES, D_NODE), dtype=jnp.float32)
        edge_index = jax.random.randint(ks[1], (2, N_EDGES), 0, N_NODES, dtype=jnp.int64)
        edge_attr = jax.random.normal(ks[2], (N_EDGES, HID), dtype=jnp.float32)
        u = jax.random.normal(ks[3], (1, 16), dtype=jnp.float32)
        batch = jnp.zeros((N_NODES,), dtype=jnp.int64)
        W1a, b1a = _init_linear(ks[4], D_NODE + HID, HID)
        W1b, b1b = _init_linear(ks[5], HID, HID)
        W2a, b2a = _init_linear(ks[6], D_NODE + HID, HID)
        W2b, b2b = _init_linear(ks[7], HID, N_TGT)
        return {'x': x, 'edge_index': edge_index, 'edge_attr': edge_attr, 'u': u, 'batch': batch, 'W1a': W1a, 'b1a': b1a, 'W1b': W1b, 'b1b': b1b, 'W2a': W2a, 'b2a': b2a, 'W2b': W2b, 'b2b': b2b}
    _L3_gnn_all = _L3_gnn_setup()
    _L3_gnn_in = {k: v for k, v in _L3_gnn_all.items() if k in ('u', 'W1a', 'b1a', 'W1b', 'b1b', 'W2a', 'b2a', 'W2b', 'b2b')}
    del _L3_gnn_all
    return {'x': x, 'src': src, 'dst': dst, 'edge_attr_64': edge_attr_64, 'L0_gnn_u': _L0_gnn_in['u'], 'L0_gnn_W1': _L0_gnn_in['W1'], 'L0_gnn_b1': _L0_gnn_in['b1'], 'L0_gnn_g1': _L0_gnn_in['g1'], 'L0_gnn_be1': _L0_gnn_in['be1'], 'L0_gnn_W2': _L0_gnn_in['W2'], 'L0_gnn_b2': _L0_gnn_in['b2'], 'L0_gnn_W3': _L0_gnn_in['W3'], 'L0_gnn_b3': _L0_gnn_in['b3'], 'L0_gnn_g2': _L0_gnn_in['g2'], 'L0_gnn_be2': _L0_gnn_in['be2'], 'L0_gnn_W4': _L0_gnn_in['W4'], 'L0_gnn_b4': _L0_gnn_in['b4'], 'L1_gnn_W1': _L1_gnn_in['W1'], 'L1_gnn_b1': _L1_gnn_in['b1'], 'L1_gnn_W2': _L1_gnn_in['W2'], 'L1_gnn_b2': _L1_gnn_in['b2'], 'L1_gnn_W3': _L1_gnn_in['W3'], 'L1_gnn_b3': _L1_gnn_in['b3'], 'L2_gnn_W1': _L2_gnn_in['W1'], 'L2_gnn_b1': _L2_gnn_in['b1'], 'L2_gnn_W2': _L2_gnn_in['W2'], 'L2_gnn_b2': _L2_gnn_in['b2'], 'L3_gnn_u': _L3_gnn_in['u'], 'L3_gnn_W1a': _L3_gnn_in['W1a'], 'L3_gnn_b1a': _L3_gnn_in['b1a'], 'L3_gnn_W1b': _L3_gnn_in['W1b'], 'L3_gnn_b1b': _L3_gnn_in['b1b'], 'L3_gnn_W2a': _L3_gnn_in['W2a'], 'L3_gnn_b2a': _L3_gnn_in['b2a'], 'L3_gnn_W2b': _L3_gnn_in['W2b'], 'L3_gnn_b2b': _L3_gnn_in['b2b']}

def reference(x, src, dst, edge_attr_64, L0_gnn_u, L0_gnn_W1, L0_gnn_b1, L0_gnn_g1, L0_gnn_be1, L0_gnn_W2, L0_gnn_b2, L0_gnn_W3, L0_gnn_b3, L0_gnn_g2, L0_gnn_be2, L0_gnn_W4, L0_gnn_b4, L1_gnn_W1, L1_gnn_b1, L1_gnn_W2, L1_gnn_b2, L1_gnn_W3, L1_gnn_b3, L2_gnn_W1, L2_gnn_b1, L2_gnn_W2, L2_gnn_b2, L3_gnn_u, L3_gnn_W1a, L3_gnn_b1a, L3_gnn_W1b, L3_gnn_b1b, L3_gnn_W2a, L3_gnn_b2a, L3_gnn_W2b, L3_gnn_b2b):
    import jax
    import jax.numpy as jnp

    def _L0_gnn_ref(x, edge_index, edge_attr, u, batch, W1, b1, g1, be1, W2, b2, W3, b3, g2, be2, W4, b4):
        import jax, jax.numpy as jnp
        import numpy as np
        N = 12500
        E = 200000
        D = 64
        H = 128
        EPS = 1e-05
        NEG_SLOPE = 0.01

        def _xavier(key, shape):
            fan_in, fan_out = (shape[0], shape[1])
            limit = float(np.sqrt(6.0 / (fan_in + fan_out)))
            return jax.random.uniform(key, shape, jnp.float32, -limit, limit)

        def _bn(h, gamma, beta):
            mean = jnp.mean(h, axis=0)
            var = jnp.mean(jnp.square(h - mean), axis=0)
            return (h - mean) * jax.lax.rsqrt(var + EPS) * gamma + beta
        row, col = (edge_index[0], edge_index[1])
        h = jnp.concatenate([x[row], edge_attr], axis=1)
        h = jax.nn.leaky_relu(h @ W1 + b1, NEG_SLOPE)
        h = _bn(h, g1, be1)
        h = h @ W2 + b2
        agg = jax.ops.segment_sum(h, col, num_segments=x.shape[0])
        h2 = jnp.concatenate([x, agg], axis=1)
        h2 = jax.nn.leaky_relu(h2 @ W3 + b3, NEG_SLOPE)
        h2 = _bn(h2, g2, be2)
        return h2 @ W4 + b4

    def _L1_gnn_ref(edge_index, x_init, W1, b1, W2, b2, W3, b3):
        import jax, jax.numpy as jnp
        import numpy as np
        N = 6250
        E = 100000
        D_IN = 64
        D_HID = 64
        D_OUT = 64

        def _glorot(key, shape):
            lim = np.sqrt(6.0 / (shape[0] + shape[1]))
            return jax.random.uniform(key, shape, jnp.float32, -lim, lim)

        def _gcn_conv(x, W, b, src, dst, normalize, n):
            h = x @ W.T
            if normalize:
                loop = jnp.arange(n, dtype=src.dtype)
                s = jnp.concatenate([src, loop])
                d = jnp.concatenate([dst, loop])
                deg = jax.ops.segment_sum(jnp.ones_like(s, dtype=h.dtype), d, num_segments=n)
                dinv = jnp.where(deg > 0, jax.lax.rsqrt(deg), jnp.zeros_like(deg))
                norm = dinv[s] * dinv[d]
                out = jax.ops.segment_sum(h[s] * norm[:, None], d, num_segments=n)
            else:
                out = jax.ops.segment_sum(h[src], dst, num_segments=n)
            return out + b
        src, dst = (edge_index[0], edge_index[1])
        n = x_init.shape[0]
        x = jax.nn.relu(_gcn_conv(x_init, W1, b1, src, dst, False, n))
        x = jax.nn.relu(_gcn_conv(x, W2, b2, src, dst, True, n))
        x = _gcn_conv(x, W3, b3, src, dst, False, n)
        return x

    def _L2_gnn_ref(x, edge_index, W1, b1, W2, b2):
        import jax, jax.numpy as jnp
        import numpy as np
        N_NODES = 12500
        N_EDGES = 156250
        D_IN, D_HID = (64, 128)
        row, col = (edge_index[0], edge_index[1])
        agg = jax.ops.segment_sum(x[col], row, num_segments=x.shape[0])
        out = agg + x
        h = jax.nn.relu(out @ W1 + b1)
        return h @ W2 + b2

    def _L3_gnn_ref(x, edge_index, edge_attr, u, batch, W1a, b1a, W1b, b1b, W2a, b2a, W2b, b2b):
        import jax, jax.numpy as jnp
        import numpy as np
        N_NODES = 6250
        N_EDGES = 100000
        D_NODE = 64
        HID = 64
        N_TGT = 64

        def _init_linear(key, fan_in, fan_out):
            kw, kb = jax.random.split(key)
            bound = 1.0 / np.sqrt(fan_in)
            W = jax.random.uniform(kw, (fan_in, fan_out), minval=-bound, maxval=bound, dtype=jnp.float32)
            b = jax.random.uniform(kb, (fan_out,), minval=-bound, maxval=bound, dtype=jnp.float32)
            return (W, b)
        row, col = (edge_index[0], edge_index[1])
        msg = jnp.concatenate([x[col], edge_attr], axis=1)
        msg = jnp.maximum(msg @ W1a + b1a, 0.0) @ W1b + b1b
        summed = jax.ops.segment_sum(msg, row, num_segments=x.shape[0])
        counts = jax.ops.segment_sum(jnp.ones((row.shape[0],), msg.dtype), row, num_segments=x.shape[0])
        agg = summed / jnp.maximum(counts, 1.0)[:, None]
        h = jnp.concatenate([x, agg], axis=1)
        out = jnp.maximum(h @ W2a + b2a, 0.0) @ W2b + b2b
        return out
    edge_index = jnp.stack([src, dst])
    batch0 = jnp.zeros((6250,), jnp.int32)
    x = _layernorm(x + _L0_gnn_ref(x, edge_index, edge_attr_64, L0_gnn_u, batch0, L0_gnn_W1, L0_gnn_b1, L0_gnn_g1, L0_gnn_be1, L0_gnn_W2, L0_gnn_b2, L0_gnn_W3, L0_gnn_b3, L0_gnn_g2, L0_gnn_be2, L0_gnn_W4, L0_gnn_b4), axis=-1)
    x = _layernorm(x + _L1_gnn_ref(edge_index, x, L1_gnn_W1, L1_gnn_b1, L1_gnn_W2, L1_gnn_b2, L1_gnn_W3, L1_gnn_b3), axis=-1)
    x = _layernorm(x + _L2_gnn_ref(x, edge_index, L2_gnn_W1, L2_gnn_b1, L2_gnn_W2, L2_gnn_b2), axis=-1)
    x = _layernorm(x + _L3_gnn_ref(x, edge_index, edge_attr_64, L3_gnn_u, batch0, L3_gnn_W1a, L3_gnn_b1a, L3_gnn_W1b, L3_gnn_b1b, L3_gnn_W2a, L3_gnn_b2a, L3_gnn_W2b, L3_gnn_b2b), axis=-1)
    return x

_drawn_inputs = setup_inputs


def setup_inputs(seed=0):
    import zlib

    import numpy as np

    out = dict(_drawn_inputs(seed))
    spreads = {'L0_gnn_b1': (0.009999999776482582, 0.6),
     'L0_gnn_g1': (1.0, 0.6),
     'L0_gnn_be1': (0.0, 0.1),
     'L0_gnn_b2': (0.009999999776482582, 0.6),
     'L0_gnn_b3': (0.009999999776482582, 0.6),
     'L0_gnn_g2': (1.0, 0.2),
     'L0_gnn_be2': (0.0, 0.1),
     'L0_gnn_b4': (0.009999999776482582, 0.6),
     'L1_gnn_b1': (0.0, 0.485),
     'L1_gnn_b2': (0.0, 0.1),
     'L1_gnn_b3': (0.0, 2.0),
     'L2_gnn_b1': (0.0, 2.0),
     'L2_gnn_b2': (0.0, 0.8)}
    factors = {'L3_gnn_W1a': 2.907, 'L3_gnn_b1a': 8.0, 'L3_gnn_b1b': 4.113}
    for name, (base, spread) in spreads.items():
        noise = np.random.default_rng([zlib.crc32(name.encode()), seed]).standard_normal(out[name].shape)
        drawn = base * np.exp(spread * noise) if base else spread * noise
        out[name] = jnp.asarray(drawn.astype(out[name].dtype))
    for name, factor in factors.items():
        out[name] = (out[name] * factor).astype(out[name].dtype)
    return out
```

```python
from contextlib import ExitStack

import concourse.bass as bass
from concourse import mybir

P = 128
N, E, D, H = 6250, 206250, 64, 128
T = 8
GE = T * P
NG = (E + GE - 1) // GE
LAST = E - (NG - 1) * GE
NB = (N + P - 1) // P
NP = NB * P
LB = N - (NB - 1) * P
WIN = 64
NA = NP + P
CH = 7
NCH = NB // CH
CW = CH * P // 2
EPS = 1e-5
SLOPE = 0.01
assert NG % 2 == 0 and NB % CH == 0 and (2 * NP) % (2 * CW) == 0

F32, I32, U32 = mybir.dt.float32, mybir.dt.int32, mybir.dt.uint32
ALU, ACT, AX = mybir.AluOpType, mybir.ActivationFunctionType, mybir.AxisListType


def build(nc, x, src, dst, edge_attr, W, out):
    ctx = ExitStack()
    with ctx:
        def sb(name, shape, dt=F32):
            return ctx.enter_context(nc.sbuf_tensor(name, shape, dt))

        def sem(name):
            return ctx.enter_context(nc.semaphore(name))

        def dram(name, shape, dt=F32):
            return nc.dram_tensor(name, shape, dt, kind="Internal").ap()

        tab_pre0 = dram("tab_pre0", (NP, H))
        tab = [dram(f"tab_{n}", (NP, D)) for n in ("conv1", "conv2", "conv3", "gin", "pre3")]
        acc_gin = [dram(f"acc_gin{c}", (NA, D)) for c in range(T)]
        acc_mean = [dram(f"acc_mean{c}", (NA, D + 1)) for c in range(T)]
        span_d = dram("span_d", (2, NG), I32)

        ident = sb("ident", [P, P])
        lower = sb("lower", [P, P])
        ones = sb("ones", [P, P])
        iota_i = sb("iota_i", [P, WIN], I32)
        iota_w = sb("iota_w", [P, WIN])
        trash_i = sb("trash_i", [P, 1], I32)
        trash = sb("trash", [P, 1])
        src_i = sb("src_i", [P, NG, T], I32)
        dst_i = sb("dst_i", [P, NG, T], I32)
        src_f = sb("src_f", [P, NG, T])
        dst_rel = sb("dst_rel", [P, NG, T])
        scat_i = sb("scat_i", [P, NG, T], I32)
        span_row = sb("span_row", [1, 2, NG], I32)
        acc = sb("acc", [P, 2, NA])
        nodes_t = sb("nodes_t", [D + 1, NA])
        node_x = sb("node_x", [P, NB, D])
        node_y = sb("node_y", [P, NB, D + 1])
        node_z = sb("node_z", [P, NB, D + 1])
        dinv = sb("dinv", [P, NB])
        ln = sb("ln", [P, 4, NB])
        gath = sb("gath", [P, 2, T, H])
        eattr = sb("eattr", [P, 2, T, D])
        eattr_t = sb("eattr_t", [P, 2, T // 2, P])
        hid = sb("hid", [P, 2, T, H])
        onehot = sb("onehot", [P, T, WIN])
        drel = sb("drel", [P, T])
        idx_g = sb("idx_g", [P, 2, T], I32)
        idx_s = sb("idx_s", [P, 2, T], I32)
        same = sb("same", [P, T, P])
        earlier = sb("earlier", [P, T, P])
        dup = sb("dup", [P, 3, T])
        addend = sb("addend", [P, 2, T, D + 1])
        zero_w = sb("zero_w", [P, H])
        src_s = sb("src_s", [P, 2, T])
        stage = sb("stage", [P, 2, CW])
        col = sb("col", [P, 24])
        bc = sb("bc", [P, 5, H])
        w0x = sb("w0x", [D, H])
        w0e = sb("w0e", [P, H])
        w0b = sb("w0b", [H, H])
        w0cx = sb("w0cx", [D, H])
        w0ca = sb("w0ca", [H, H])
        w0d = sb("w0d", [H, D])
        wc_in = sb("wc_in", [D, 3, D])
        wc = sb("wc", [D + 1, 3, D])
        wg1 = sb("wg1", [D, H])
        wg2 = sb("wg2", [H, D])
        w3x = sb("w3x", [D, D])
        w3e = sb("w3e", [P, D])
        w3b = sb("w3b", [D + 1, D])
        w3cx = sb("w3cx", [D, D])
        w3ca = sb("w3ca", [D, D])
        w3d = sb("w3d", [D, D])

        banks = [ctx.enter_context(nc.psum_tensor(f"bank{i}", [P, 512], F32)) for i in range(8)]

        def node_rows(t):
            return t.rearrange("(b p) f -> p b f", p=P)

        def row_bc(v):
            return v.rearrange("(a f) -> a f", a=1).to_broadcast([P, v.shape[0]])

        def column(v):
            return v.rearrange("(f a) -> f a", a=1)

        GB1, GBE1, B2, B3, G2, BE2, BG1, B3A2 = range(8)
        M1, V1, SC1, SH1, S1, Q1, M2, V2, SC2, SH2, NM2 = range(8, 19)

        s_fill = sem("s_fill")
        s_par = sem("s_par")
        s_idx = sem("s_idx")
        s_cst = sem("s_cst")
        s_spn = sem("s_spn")
        s_sp0 = sem("s_sp0")
        s_span = sem("s_span")
        s_zero = sem("s_zero")
        s_gm = sem("s_gm")
        with nc.Block() as block:
            zeros = acc[:, 0, 0:(NA // P) * (D + 1)]
            ends = acc[:, 1, 0:2 * GE].bitcast(I32)
            QG = NG // 2
            mn, mx = ln[0:QG, 0, 0:2].bitcast(I32), ln[0:QG, 1, 0:2].bitcast(I32)
            base_bc = hid[:, 0, 0:2, :].rearrange("p a b -> p (a b)")[:, 0:NG].bitcast(I32)
            n_param = [0]

            @block.sync
            def _(sp):
                tail = (NG - 2) * GE
                sp.dma_start(ends[0:QG - 1, :], dst[0:tail].rearrange("(q e) -> q e", q=QG - 1)).then_inc(s_gm, 16)
                sp.dma_start(ends[QG - 1:QG, 0:GE + LAST], dst[tail:E].rearrange("(q e) -> q e", q=1)).then_inc(s_gm, 16)
                sp.dma_start(ends[QG - 1:QG, GE + LAST:2 * GE],
                             dst[E - GE + LAST:E].rearrange("(q e) -> q e", q=1)).then_inc(s_gm, 16)
                sp.wait_ge(s_fill, 2)
                full, part = LAST // T, LAST % T
                for t, d in ((src_i, src), (dst_i, dst)):
                    sp.dma_start(t[:, 0:NG - 1, :],
                                 d[0:(NG - 1) * GE].rearrange("(g p c) -> p g c", p=P, c=T)).then_inc(s_idx, 16)
                    sp.dma_start(t[0:full, NG - 1, :],
                                 d[(NG - 1) * GE:(NG - 1) * GE + full * T].rearrange("(p c) -> p c", c=T)).then_inc(s_idx, 16)
                    if part:
                        sp.dma_start(t[full:full + 1, NG - 1, 0:part],
                                     d[(NG - 1) * GE + full * T:E].rearrange("(p c) -> p c", p=1)).then_inc(s_idx, 16)
                sp.wait_ge(s_spn, 1)
                sp.dma_start(span_d[0, :].rearrange("(q r) -> q r", r=2), mn).then_inc(s_sp0, 16)
                sp.dma_start(span_d[1, :].rearrange("(q r) -> q r", r=2), mx).then_inc(s_sp0, 16)
                sp.wait_ge(s_sp0, 32)
                sp.dma_start(span_row[:, :, :], span_d.rearrange("(a t) g -> a t g", a=1)).then_inc(s_span, 16)
                sp.dma_start(base_bc, span_d[0:1, :].to_broadcast([P, NG])).then_inc(s_span, 16)
                sp.wait_ge(s_span, 32)

            @block.scalar
            def _(act):
                def load(dst_ap, src_ap):
                    act.dma_start(dst_ap, src_ap).then_inc(s_par, 16)
                    n_param[0] += 1

                act.wait_ge(s_fill, 3)
                load(node_x[:, 0:NB - 1, :], node_rows(x[0:(NB - 1) * P, :]))
                load(node_x[0:LB, NB - 1, :], x[(NB - 1) * P:N, :])
                load(w0x[:, :], W["L0_gnn_W1"][0:D, :])
                load(w0e[0:D, :], W["L0_gnn_W1"][D:2 * D, :])
                load(w0e[D:P, :], W["L0_gnn_W1"][D:2 * D, :])
                load(w0b[:, :], W["L0_gnn_W2"])
                load(w0cx[:, :], W["L0_gnn_W3"][0:D, :])
                load(w0ca[:, :], W["L0_gnn_W3"][D:D + H, :])
                load(w0d[:, :], W["L0_gnn_W4"])
                for i in range(3):
                    load(wc_in[:, i, :], W[f"L1_gnn_W{i + 1}"])
                    load(wc[D:D + 1, i, :], W[f"L1_gnn_b{i + 1}"].rearrange("(a f) -> a f", a=1))
                load(wg1[:, :], W["L2_gnn_W1"])
                load(wg2[:, :], W["L2_gnn_W2"])
                load(w3x[:, :], W["L3_gnn_W1a"][0:D, :])
                load(w3e[0:D, :], W["L3_gnn_W1a"][D:2 * D, :])
                load(w3e[D:P, :], W["L3_gnn_W1a"][D:2 * D, :])
                load(w3b[0:D, :], W["L3_gnn_W1b"])
                load(w3b[D:D + 1, :], W["L3_gnn_b1b"].rearrange("(a f) -> a f", a=1))
                load(w3cx[:, :], W["L3_gnn_W2a"][0:D, :])
                load(w3ca[:, :], W["L3_gnn_W2a"][D:2 * D, :])
                load(w3d[:, :], W["L3_gnn_W2b"])
                for c, name in ((GB1, "L0_gnn_g1"), (GBE1, "L0_gnn_be1"), (B2, "L0_gnn_b2"), (B3, "L0_gnn_b3"),
                                (G2, "L0_gnn_g2"), (BE2, "L0_gnn_be2"), (BG1, "L2_gnn_b1")):
                    load(col[:, c:c + 1], column(W[name]))
                load(col[0:D, B3A2:B3A2 + 1], column(W["L3_gnn_b2a"]))
                for r, name in enumerate(("L0_gnn_b1", "L0_gnn_b4", "L1_gnn_b2", "L2_gnn_b2", "L3_gnn_b1a")):
                    load(bc[:, r, 0:W[name].shape[0]], row_bc(W[name]))
                load(bc[:, 1, D:2 * D], row_bc(W["L3_gnn_b2b"]))
                act.wait_ge(s_fill, 4)
                for c in range(T):
                    act.dma_start(acc_gin[c].rearrange("(p r) f -> p (r f)", p=P),
                                  zeros[:, 0:(NA // P) * D]).then_inc(s_zero, 16)
                    act.dma_start(acc_mean[c].rearrange("(p r) f -> p (r f)", p=P), zeros).then_inc(s_zero, 16)
                act.wait_ge(s_par, 16 * n_param[0])
                act.wait_ge(s_zero, 32 * T)

            @block.gpsimd
            def _(pool):
                nc.gpsimd.memset(src_i[:, NG - 1, :], N).then_inc(s_fill, 1)
                nc.gpsimd.memset(dst_i[:, NG - 1, :], N).then_inc(s_fill, 1)
                nc.gpsimd.memset(node_x[:, NB - 1, :], 0.0).then_inc(s_fill, 1)
                nc.gpsimd.memset(zeros, 0.0).then_inc(s_fill, 1)
                nc.gpsimd.memset(zero_w[:, :], 0.0)
                nc.gpsimd.memset(ones[:, :], 1.0).then_inc(s_cst, 1)
                pool.wait_ge(s_cst, 1)
                nc.gpsimd.affine_select(out=ident[:, :], in_=ones[:, :], compare_op=ALU.is_equal, fill=0.0, base=0,
                                        pattern=[[-1, P]], channel_multiplier=1).then_inc(s_cst, 1)
                nc.gpsimd.affine_select(out=lower[:, :], in_=ones[:, :], compare_op=ALU.is_gt, fill=0.0, base=0,
                                        pattern=[[-1, P]], channel_multiplier=1).then_inc(s_cst, 1)
                nc.gpsimd.iota(iota_i[:, :], [[1, WIN]], base=0, channel_multiplier=0).then_inc(s_cst, 1)
                nc.gpsimd.iota(trash_i[:, :], [[0, 1]], base=N, channel_multiplier=1).then_inc(s_cst, 1)

            @block.vector
            def _(dve):
                s_d = sem("s_d0")
                dve.wait_ge(s_gm, 48)
                e3 = ends[0:QG, :].rearrange("q (r e) -> q r e", r=2)
                nc.vector.tensor_reduce(mn, e3, AX.X, ALU.min).then_inc(s_d, 1)
                nc.vector.tensor_reduce(mx, e3, AX.X, ALU.max).then_inc(s_d, 1)
                dve.wait_ge(s_d, 2)
                nc.vector.tensor_tensor(mx, mx, mn, ALU.subtract).then_inc(s_d, 1)
                dve.wait_ge(s_d, 3)
                nc.vector.tensor_scalar(mx, mx, WIN.bit_length() - 1, None, ALU.arith_shift_right).then_inc(s_d, 1)
                dve.wait_ge(s_d, 4)
                nc.vector.tensor_scalar(mx, mx, 1, None, ALU.add).then_inc(s_spn, 1)
                dve.wait_ge(s_cst, 5)
                nc.vector.tensor_copy(iota_w[:, :], iota_i[:, :])
                nc.vector.tensor_copy(trash[:, :], trash_i[:, :])
                dve.wait_ge(s_idx, 16 * (6 if LAST % T else 4))
                nc.vector.tensor_copy(src_f[:, :, :], src_i[:, :, :])
                dve.wait_ge(s_span, 32)
                nc.vector.tensor_tensor(dst_rel[:, :, :], dst_i[:, :, :],
                                        base_bc.unsqueeze(2).to_broadcast([P, NG, T]), ALU.subtract).then_inc(s_d, 1)
                dve.wait_ge(s_d, 5)
                nc.vector.scalar_tensor_tensor(out=dst_rel[:, NG - 1, :], in0=dst_i[:, NG - 1, :], scalar=float(N),
                                               in1=dst_rel[:, NG - 1, :], op0=ALU.is_lt, op1=ALU.mult).then_inc(s_d, 1)
                dve.wait_ge(s_d, 6)
                nc.vector.scalar_tensor_tensor(out=dst_rel[:, NG - 1, :], in0=dst_i[:, NG - 1, :], scalar=float(N),
                                               in1=dst_rel[:, NG - 1, :], op0=ALU.is_ge,
                                               op1=ALU.subtract).then_inc(s_d, 1)
                dve.wait_ge(s_d, 7)
                nc.vector.tensor_scalar(dst_rel[:, NG - 1, :], dst_rel[:, NG - 1, :], -1.0, None, ALU.mult)

        def to_features(pe, dst_t, source, width, s_tr, s_ev, src_ready=None):
            for q in range((NB + 3) // 4):
                if q >= 2:
                    pe.wait_ge(s_ev, q - 1)
                for k in range(min(4, NB - 4 * q)):
                    last = nc.tensor.transpose(banks[q % 2][0:width, k * P:(k + 1) * P],
                                               source[:, 4 * q + k, 0:width], ident[:, :])
                last.then_inc(s_tr, 1)

        def to_features_copy(act, dst_t, width, s_tr, s_ev):
            for q in range((NB + 3) // 4):
                act.wait_ge(s_tr, q + 1)
                n = min(4, NB - 4 * q) * P
                nc.scalar.copy(dst_t[0:width, 4 * q * P:4 * q * P + n], banks[q % 2][0:width, 0:n]).then_inc(s_ev, 1)

        def layer_norm(dve, chain, y):
            step, s_var, s_std = chain
            b3 = lambda t: t.unsqueeze(2).to_broadcast([P, NB, D])
            step(nc.vector.tensor_reduce(ln[:, 0, :], y, AX.X, ALU.add))
            step(nc.vector.tensor_scalar(ln[:, 0, :], ln[:, 0, :], 1.0 / D, None, ALU.mult))
            step(nc.vector.tensor_tensor(y, y, b3(ln[:, 0, :]), ALU.subtract))
            step(nc.vector.tensor_tensor(node_z[:, :, 0:D], y, y, ALU.mult))
            step(nc.vector.tensor_reduce(ln[:, 1, :], node_z[:, :, 0:D], AX.X, ALU.add))
            nc.vector.tensor_scalar(ln[:, 1, :], ln[:, 1, :], 1.0 / D, EPS, ALU.mult, ALU.add).then_inc(s_var, 1)
            dve.wait_ge(s_std, 1)
            step(nc.vector.reciprocal(ln[:, 3, :], ln[:, 2, :]))
            step(nc.vector.tensor_tensor(node_x[:, :, :], y, b3(ln[:, 3, :]), ALU.mult))

        def layer_norm_root(act, s_var, s_std):
            act.wait_ge(s_var, 1)
            nc.scalar.activation(ln[:, 2, :], ln[:, 1, :], ACT.Sqrt).then_inc(s_std, 1)

        def stepper(dve, name):
            s = sem(name)
            count = [0]

            def step(ins):
                count[0] += 1
                ins.then_inc(s, 1)
                dve.wait_ge(s, count[0])
            return step

        s_t, s_e, s_m, s_a, s_w, s_wt, s_wv = (sem(f"pre_{k}") for k in "temawuv")
        pre = acc[:, 0, 0:NB * H].rearrange("p (b f) -> p b f", f=H)
        with nc.Block() as block:
            @block.tensor
            def _(pe):
                to_features(pe, nodes_t, node_x, D, s_t, s_e)
                for i in range(3):
                    last = nc.tensor.transpose(banks[4][0:D, i * D:(i + 1) * D], wc_in[:, i, :], ident[0:D, 0:D])
                last.then_inc(s_wt, 1)
                pe.wait_ge(s_e, (NB + 3) // 4)
                for q in range((NB + 3) // 4):
                    if q >= 2:
                        pe.wait_ge(s_a, q - 1)
                    for k in range(min(4, NB - 4 * q)):
                        b = 4 * q + k
                        last = nc.tensor.matmul(banks[2 + q % 2][:, k * H:(k + 1) * H], nodes_t[0:D, b * P:(b + 1) * P],
                                                w0x[:, :], start=True, stop=True)
                    last.then_inc(s_m, 1)

            @block.scalar
            def _(act):
                to_features_copy(act, nodes_t, D, s_t, s_e)
                act.wait_ge(s_wt, 1)
                nc.scalar.copy(wc[0:D, :, :], banks[4][0:D, 0:3 * D].rearrange("p (i f) -> p i f", i=3))

            @block.vector
            def _(dve):
                for q in range((NB + 3) // 4):
                    dve.wait_ge(s_m, q + 1)
                    n = min(4, NB - 4 * q)
                    nc.vector.tensor_tensor(pre[:, 4 * q:4 * q + n, :],
                                            banks[2 + q % 2][:, 0:n * H].rearrange("p (b f) -> p b f", f=H),
                                            bc[:, 0, :].unsqueeze(1).to_broadcast([P, n, H]), ALU.add).then_inc(s_a, 1)

            @block.sync
            def _(sp):
                sp.wait_ge(s_a, (NB + 3) // 4)
                sp.dma_start(node_rows(tab_pre0[0:(NB - 1) * P, :]), pre[:, 0:NB - 1, :]).then_inc(s_w, 16)
                sp.dma_start(tab_pre0[(NB - 1) * P:N, :], pre[0:LB, NB - 1, :]).then_inc(s_w, 16)
                sp.dma_start(tab_pre0[N:NP, :], zero_w[0:NP - N, :]).then_inc(s_w, 16)
                sp.wait_ge(s_w, 48)

        def both(eng, body, end=NG // 2):
            body(0, 0, 0)
            body(0, 1, 1)
            with eng.Fori(1, end) as it:
                for s in range(2):
                    body(it, s, it * 2 + s)

        def wait(eng, semaphore, value):
            if not isinstance(value, int) or value > 0:
                eng.wait_ge(semaphore, value)

        def send_indices(sp, it, s, g, table, gathered, here):
            wait(sp, gathered[s], 16 * T * it)
            sp.dma_start(idx_g[:, s, :], table[:, bass.ds(g, 1), :].rearrange("p a c -> p (a c)")).then_inc(here[s], 16)

        def send_attributes(sp, it, s, g, turned, there):
            wait(sp, turned[s], it)
            sp.dma_start(eattr[:, s, :, :], edge_attr[bass.ds(g * GE, GE), :].rearrange(
                "(p c) f -> p c f", p=P)).then_inc(there[s], 16)

        def send_last_attributes(sp, turned, there):
            sp.wait_ge(turned[1], NG // 2 - 1)
            full, part = LAST // T, LAST % T
            e0 = (NG - 1) * GE
            rows = eattr[:, 1, :, :].rearrange("p c f -> p (c f)")
            n = 1
            sp.dma_start(rows[0:full, :], edge_attr[e0:e0 + full * T, :].rearrange(
                "(p c) f -> p (c f)", c=T)).then_inc(there[1], 16)
            if part:
                sp.dma_start(rows[full:full + 1, 0:part * D], edge_attr[e0 + full * T:E, :].rearrange(
                    "(p c) f -> p (c f)", p=1)).then_inc(there[1], 16)
                sp.dma_start(rows[full:full + 1, part * D:T * D], zeros_d[0:T - part, :].rearrange(
                    "(p c) f -> p (c f)", p=1)).then_inc(there[1], 16)
                n = 3
            first = full + (part > 0)
            sp.dma_start(rows[first:P, :], zeros_d[0:(P - first) * T, :].rearrange(
                "(p c) f -> p (c f)", c=T)).then_inc(there[1], 16)
            return n + 1

        N_LAST = (3 if LAST % T else 1) + 1

        def gather_rows(pool, it, s, table, width, here, free, gathered, begun):
            indices, used = pool.snap(16 * (it + 1)), pool.snap(it)
            pool.wait_ge(here[s], indices)
            wait(pool, free[s], used)
            pool.sem_inc(begun, 1)
            for c in range(T):
                pool.indirect_dma_start(gath[:, s, c, 0:width], None, table[:, :], bass.IndirectOffsetOnAxis(
                    ap=idx_g[:, s, c:c + 1].bitcast(U32), axis=0)).then_inc(gathered[s], 16)

        def turn_attributes(pe, it, s, there, turned, copied, last=False):
            pe.wait_ge(there[s], 16 * it + 16 * (N_LAST if last else 1))
            wait(pe, copied[1 - s], it if s == 0 else it + 1)
            for q in range(T // 2):
                ins = nc.tensor.transpose(banks[6][:, q * P:(q + 1) * P],
                                          eattr[:, s, 2 * q:2 * q + 2, :].rearrange("p c f -> p (c f)"), ident[:, :])
            ins.then_inc(turned[s], 1)

        def copy_attributes(act, it, s, turned, copied, joined):
            wait(act, joined[s], it)
            act.wait_ge(turned[s], it + 1)
            nc.scalar.copy(eattr_t[:, s, :, :], banks[6][:, :].rearrange("p (q e) -> p q e", e=P)).then_inc(copied[s], 1)

        def join_attributes(pe, it, s, out_of, weights, copied, summed, joined, shared=False):
            pe.wait_ge(copied[s], it + 1)
            if shared:
                wait(pe, summed[1 - s], it if s == 0 else it + 1)
            else:
                wait(pe, summed[s], it)
            for c in range(T):
                h = D * (c % 2)
                ins = nc.tensor.matmul(out_of(s, c), eattr_t[h:h + D, s, c // 2, :], weights[h:h + D, :],
                                       start=True, stop=True)
            ins.then_inc(joined[s], 1)

        edge_sems = []

        def edge_sem(name):
            edge_sems.append(nc.alloc_semaphore(name=name))
            return edge_sems[-1]

        def slots(name):
            return [edge_sem(f"{name}0"), edge_sem(f"{name}1")]

        def retire(pool):
            nc.clear_and_free_semaphores(edge_sems)
            edge_sems.clear()

        def window_stage(name, table, mlp0):
            width = H if mlp0 else D
            here, gathered, free = (slots(f"{name}_{k}") for k in ("here", "gathered", "free"))
            s_oh, s_win, s_add, s_rel = (edge_sem(f"{name}_{k}") for k in ("oh", "win", "add", "rel"))
            if mlp0:
                there, turned, copied, joined, summed, ready = (
                    slots(f"{name}_{k}") for k in ("there", "turned", "copied", "joined", "summed", "ready"))
            begun = edge_sem(f"{name}_begun")
            rows = hid if mlp0 else gath
            sums, gram = banks[4], banks[5]
            product = lambda s, c: banks[2 * s + c % 2][:, (c // 2) * H:(c // 2 + 1) * H]
            with nc.Block() as block:
                @block.sync
                def _(sp):
                    def group(it, s, g):
                        send_indices(sp, it, s, g, src_i, gathered, here)
                        if mlp0:
                            send_attributes(sp, it, s, g, turned, there)
                    both(sp, group, NG // 2 - 1)
                    group(NG // 2 - 1, 0, NG - 2)
                    send_indices(sp, NG // 2 - 1, 1, NG - 1, src_i, gathered, here)
                    if mlp0:
                        send_last_attributes(sp, turned, there)

                @block.gpsimd
                def _(pool):
                    both(pool, lambda it, s, g: gather_rows(pool, it, s, table, width, here, free, gathered, begun))

                @block.scalar
                def _(act):
                    if mlp0:
                        both(act, lambda it, s, g: copy_attributes(act, it, s, turned, copied, joined))

                @block.tensor
                def _(pe):
                    count = pe.alloc_register(f"{name}_pe_windows")
                    pe.reg_mov(count, 0)

                    def group(it, s, g, final=False):
                        nxt = (it, 1) if s == 0 else (it + 1, 0)
                        if mlp0:
                            if not (final and s == 1):
                                turn_attributes(pe, *nxt, there, turned, copied, last=final)
                            pe.wait_ge(ready[s], it + 1)
                            for c in range(T):
                                nc.tensor.matmul(gram[:, 0:H], hid[:, s, c, :], hid[:, s, c, :], start=False,
                                                 stop=False, skip_group_check=True)
                            if not (final and s == 1):
                                join_attributes(pe, *nxt, product, w0e, copied, summed, joined)
                        else:
                            pe.wait_ge(gathered[s], 16 * T * (it + 1))
                        windows = pe.value_load(span_row[0:1, 1, bass.ds(g, 1)], min_val=1, max_val=N // WIN + 1)
                        with pe.Fori(0, windows) as w:
                            k = pe.snap(count, min_val=0, max_val=2 ** 20)
                            pe.wait_ge(s_oh, k + 1)
                            for c in range(T):
                                ins = nc.tensor.matmul(sums[0:width, 0:WIN], rows[:, s, c, 0:width], onehot[:, c, :],
                                                       start=(c == 0), stop=(c == T - 1))
                            if mlp0:
                                for c in range(T):
                                    ins = nc.tensor.matmul(sums[:, WIN:2 * WIN], ones[:, :], onehot[:, c, :],
                                                           start=(c == 0), stop=(c == T - 1))
                            ins.then_inc(s_win, 1)
                            pe.reg_add(count, count, 1)

                    if mlp0:
                        nc.tensor.matmul(gram[:, 0:H], zero_w[:, :], zero_w[:, :], start=True, stop=False,
                                         skip_group_check=True)
                        turn_attributes(pe, 0, 0, there, turned, copied)
                        join_attributes(pe, 0, 0, product, w0e, copied, summed, joined)
                    both(pe, group, NG // 2 - 1)
                    group(NG // 2 - 1, 0, NG - 2, final=True)
                    group(NG // 2 - 1, 1, NG - 1, final=True)
                    if mlp0:
                        nc.tensor.matmul(gram[:, 0:H], zero_w[:, :], zero_w[:, :], start=False, stop=True,
                                         skip_group_check=True)

                @block.vector
                def _(dve):
                    count = dve.alloc_register(f"{name}_dve_windows")
                    dve.reg_mov(count, 0)
                    start = dve.alloc_register(f"{name}_dve_start")
                    n_acc = 2 if mlp0 else 1
                    if mlp0:
                        nc.vector.memset(acc[:, :, :], 0.0).then_inc(s_add, 1)
                    elif name != "conv2":
                        nc.vector.memset(acc[D:D + 1, 0, :], 1.0)
                        nc.vector.memset(acc[0:D, 0, :], 0.0).then_inc(s_add, 1)
                    else:
                        nc.vector.memset(acc[0:D, 0, NP:NA], 0.0).then_inc(s_add, 1)

                    def group(it, s, g):
                        if mlp0:
                            dve.wait_ge(joined[s], it + 1)
                            dve.wait_ge(gathered[s], 16 * T * (it + 1))
                            for q in range(2):
                                ins = nc.vector.tensor_tensor(
                                    hid[:, s, q:T:2, :], banks[2 * s + q][:, :].rearrange("p (c f) -> p c f", f=H),
                                    gath[:, s, q:T:2, :], ALU.add)
                            ins.then_inc(summed[s], 1)
                            dve.wait_ge(summed[s], it + 1)
                            nc.vector.scalar_tensor_tensor(out=hid[:, s, :, :], in0=hid[:, s, :, :], scalar=SLOPE,
                                                           in1=hid[:, s, :, :], op0=ALU.mult,
                                                           op1=ALU.max).then_inc(ready[s], 1)
                        base = dve.value_load(span_row[0:1, 0, bass.ds(g, 1)], min_val=0, max_val=N - 1)
                        windows = dve.value_load(span_row[0:1, 1, bass.ds(g, 1)], min_val=1, max_val=N // WIN + 1)
                        if not isinstance(g, int) or g > 0:
                            dve.wait_ge(s_rel, dve.snap(count, min_val=0, max_val=2 ** 20) + g)
                        nc.vector.tensor_copy(drel[:, :], dst_rel[:, bass.ds(g, 1), :].rearrange(
                            "p a c -> p (a c)")).then_inc(s_rel, 1)
                        dve.reg_mov(start, base)
                        with dve.Fori(0, windows) as w:
                            k = dve.snap(count, min_val=0, max_val=2 ** 20)
                            first = dve.snap(start, min_val=0, max_val=NA - WIN)
                            dve.wait_ge(s_rel, k + g + 1)
                            nc.vector.tensor_tensor(onehot[:, :, :], iota_w[:, :].unsqueeze(1).to_broadcast([P, T, WIN]),
                                                    drel[:, :].unsqueeze(2).to_broadcast([P, T, WIN]),
                                                    ALU.is_equal).then_inc(s_oh, 1)
                            dve.wait_ge(s_win, k + 1)
                            nc.vector.tensor_scalar(drel[:, :], drel[:, :], float(WIN), None,
                                                    ALU.subtract).then_inc(s_rel, 1)
                            dve.wait_ge(s_add, k + 1)
                            at = acc[0:width, 0:n_acc, bass.ds(first, WIN)]
                            nc.vector.tensor_tensor(at, at, sums[0:width, 0:n_acc * WIN].rearrange(
                                "p (a n) -> p a n", a=n_acc), ALU.add).then_inc(s_add, 1)
                            dve.reg_add(count, count, 1)
                            dve.reg_add(start, start, WIN)
                        dve.sem_inc(free[s], 1)
                    both(dve, group)

        def scatter_stage(name, table, accs, mlp3):
            width = D + 1 if mlp3 else D
            here, gathered, free, added, row_in, equal, totalled, index, addable, spread = (
                slots(f"{name}_{k}") for k in ("here", "gathered", "free", "added", "row_in", "equal", "totalled",
                                               "index", "addable", "spread"))
            if mlp3:
                there, turned, copied, joined, summed, ready = (
                    slots(f"{name}_{k}") for k in ("there", "turned", "copied", "joined", "summed", "ready"))
                rows = hid[:, :, :, 0:D + 1]
            else:
                s_dup = edge_sem(f"{name}_dup")
                rows = gath[:, :, :, 0:D]
            begun = edge_sem(f"{name}_begun")
            spreads = [banks[0], banks[1]]
            totals = [banks[2], banks[3]]
            product = lambda s, c: banks[4 + c % 2][:, (c // 2) * D:(c // 2 + 1) * D]
            with nc.Block() as block:
                @block.sync
                def _(sp):
                    def group(it, s, g):
                        send_indices(sp, it, s, g, dst_i, gathered, here)
                        if mlp3:
                            send_attributes(sp, it, s, g, turned, there)
                    both(sp, group, NG // 2 - 1)
                    group(NG // 2 - 1, 0, NG - 2)
                    send_indices(sp, NG // 2 - 1, 1, NG - 1, dst_i, gathered, here)
                    if mlp3:
                        send_last_attributes(sp, turned, there)

                @block.gpsimd
                def _(pool):
                    def gather(it, s):
                        gather_rows(pool, it, s, table, D, here, free, gathered, begun)

                    def scatter(it, s):
                        now, before = pool.snap(it + 1), pool.snap(16 * T * (it if s == 0 else it + 1))
                        pool.wait_ge(index[s], now)
                        pool.wait_ge(addable[s], now)
                        wait(pool, added[1 - s], before)
                        pool.sem_inc(begun, 1)
                        for c in range(T):
                            pool.indirect_dma_start(accs[c][:, :], bass.IndirectOffsetOnAxis(
                                ap=idx_s[:, s, c:c + 1].bitcast(U32), axis=0), addend[:, s, c, 0:width], None,
                                bounds_check=NA - 1, compute_op=ALU.add).then_inc(added[s], 16)

                    def four(it):
                        gather(it, 1)
                        scatter(it, 0)
                        gather(it + 1, 0)
                        scatter(it, 1)
                    gather(0, 0)
                    four(0)
                    with pool.Fori(1, NG // 2 - 1) as it:
                        four(it)
                    gather(NG // 2 - 1, 1)
                    scatter(NG // 2 - 1, 0)
                    scatter(NG // 2 - 1, 1)
                    for s in range(2):
                        pool.wait_ge(added[s], 16 * T * (NG // 2))

                @block.scalar
                def _(act):
                    def group(it, s, g, final=False):
                        wait(act, equal[s], it)
                        nc.scalar.copy(src_s[:, s, :], src_f[:, bass.ds(g, 1), :].rearrange(
                            "p a c -> p (a c)")).then_inc(row_in[s], 1)
                        if mlp3 and not (final and s == 1):
                            copy_attributes(act, *((it, 1) if s == 0 else (it + 1, 0)), turned, copied, joined)
                        act.wait_ge(totalled[s], it + 1)
                        wait(act, added[s], 16 * T * it)
                        for q in range(2):
                            ins = nc.scalar.copy(addend[:, s, 4 * q:4 * q + 4, 0:width],
                                                 totals[q][:, 0:4 * width].rearrange("p (c f) -> p c f", c=4))
                        ins.then_inc(addable[s], 1)
                    if mlp3:
                        copy_attributes(act, 0, 0, turned, copied, joined)
                    both(act, group, NG // 2 - 1)
                    group(NG // 2 - 1, 0, NG - 2, final=True)
                    group(NG // 2 - 1, 1, NG - 1, final=True)

                @block.tensor
                def _(pe):
                    def group(it, s, g, final=False):
                        pe.wait_ge(row_in[s], it + 1)
                        wait(pe, equal[1 - s], it if s == 0 else it + 1)
                        for c in range(T):
                            ins = nc.tensor.transpose(spreads[c // 4][:, (c % 4) * P:(c % 4 + 1) * P],
                                                      src_s[:, s, c:c + 1].to_broadcast([P, P]), ident[:, :])
                        ins.then_inc(spread[s], 1)
                        if mlp3:
                            if not (final and s == 1):
                                nxt = (it, 1) if s == 0 else (it + 1, 0)
                                turn_attributes(pe, *nxt, there, turned, copied, last=final)
                                join_attributes(pe, *nxt, product, w3e, copied, summed, joined, shared=True)
                            pe.wait_ge(ready[s], it + 1)
                        else:
                            pe.wait_ge(gathered[s], 16 * T * (it + 1))
                        pe.wait_ge(equal[s], it + 1)
                        wait(pe, addable[1 - s], it if s == 0 else it + 1)
                        for c in range(T):
                            ins = nc.tensor.matmul(totals[c // 4][:, (c % 4) * width:(c % 4 + 1) * width],
                                                   same[:, c, :], rows[:, s, c, :], start=True, stop=True)
                        ins.then_inc(totalled[s], 1)
                    if mlp3:
                        turn_attributes(pe, 0, 0, there, turned, copied)
                        join_attributes(pe, 0, 0, product, w3e, copied, summed, joined, shared=True)
                    both(pe, group, NG // 2 - 1)
                    group(NG // 2 - 1, 0, NG - 2, final=True)
                    group(NG // 2 - 1, 1, NG - 1, final=True)

                @block.vector
                def _(dve):
                    if mlp3:
                        nc.vector.memset(hid[:, :, :, D:D + 1], 1.0)

                    def group(it, s, g):
                        dve.wait_ge(spread[s], it + 1)
                        wait(dve, totalled[1 - s], it if s == 0 else it + 1)
                        src_now = src_s[:, s, :]
                        for q in range(2):
                            ins = nc.vector.tensor_tensor(
                                same[:, 4 * q:4 * q + 4, :], spreads[q][:, :].rearrange("p (c e) -> p c e", c=4),
                                src_now[:, 4 * q:4 * q + 4].unsqueeze(2).to_broadcast([P, 4, P]), ALU.is_equal)
                        if mlp3:
                            ins.then_inc(equal[s], 1)
                            dve.wait_ge(joined[s], it + 1)
                            dve.wait_ge(gathered[s], 16 * T * (it + 1))
                            for q in range(2):
                                ins = nc.vector.tensor_tensor(
                                    hid[:, s, q:T:2, 0:D],
                                    banks[4 + q][:, 0:4 * D].rearrange("p (c f) -> p c f", f=D),
                                    gath[:, s, q:T:2, 0:D], ALU.add)
                            ins.then_inc(summed[s], 1)
                            dve.wait_ge(summed[s], it + 1)
                            nc.vector.tensor_scalar(hid[:, s, :, 0:D], hid[:, s, :, 0:D], 0.0, None,
                                                    ALU.max).then_inc(ready[s], 1)
                            dve.sem_inc(free[s], 1)
                            wait(dve, added[s], 16 * T * it)
                            nc.vector.tensor_copy(idx_s[:, s, :], scat_i[:, bass.ds(g, 1), :].rearrange(
                                "p a c -> p (a c)")).then_inc(index[s], 1)
                            return
                        ins.then_inc(s_dup, 1)
                        dve.wait_ge(s_dup, g * 5 + 1)
                        nc.vector.tensor_tensor(earlier[:, :, :], same[:, :, :],
                                                lower[:, :].unsqueeze(1).to_broadcast([P, T, P]),
                                                ALU.mult).then_inc(s_dup, 1)
                        dve.wait_ge(s_dup, g * 5 + 2)
                        nc.vector.tensor_reduce(dup[:, 0, :], earlier[:, :, :], AX.X, ALU.max).then_inc(s_dup, 1)
                        nc.vector.tensor_scalar(dup[:, 1, :], src_now, -1.0, trash[:, 0:1], ALU.mult,
                                                ALU.add).then_inc(s_dup, 1)
                        dve.wait_ge(s_dup, g * 5 + 4)
                        nc.vector.tensor_tensor(dup[:, 0, :], dup[:, 0, :], dup[:, 1, :], ALU.mult).then_inc(s_dup, 1)
                        dve.wait_ge(s_dup, g * 5 + 5)
                        nc.vector.tensor_tensor(scat_i[:, bass.ds(g, 1), :].rearrange("p a c -> p (a c)"),
                                                dup[:, 0, :], src_now, ALU.add)
                        wait(dve, added[s], 16 * T * it)
                        nc.vector.tensor_tensor(idx_s[:, s, :], dup[:, 0, :], src_now, ALU.add).then_inc(index[s], 1)
                        dve.sem_inc(equal[s], 1)
                        dve.wait_ge(totalled[s], it + 1)
                        dve.sem_inc(free[s], 1)
                    both(dve, group)

        def node_products(pe, lhs_t, rhs, s_m, s_a, first=0):
            for q in range(NCH):
                if q >= 2:
                    pe.wait_ge(s_a, q - 1)
                for k in range(CH):
                    b = CH * q + k
                    ins = nc.tensor.matmul(banks[first + q % 2][:, k * D:(k + 1) * D], lhs_t[:, b * P:(b + 1) * P], rhs,
                                           start=True, stop=True)
                ins.then_inc(s_m, 1)

        def chunk(q, first=0):
            return banks[first + q % 2][:, 0:CH * D].rearrange("p (b f) -> p b f", f=D), slice(CH * q, CH * (q + 1))

        def over_nodes(row):
            return row.unsqueeze(1).to_broadcast([P, CH, D])

        def add_accumulators(sp_or_dve, accs, width, s_ld, s_sm, load):
            size = NB * width
            part = lambda c: acc[:, c % 4 // 2, (c % 2) * (NA // 2):(c % 2) * (NA // 2) + size].rearrange(
                "p (b f) -> p b f", f=width)
            y = node_y[:, :, 0:width]
            if load:
                for c in range(T):
                    if c >= 4:
                        sp_or_dve.wait_ge(s_sm, c - 3)
                    sp_or_dve.dma_start(part(c), node_rows(accs[c][0:NP, :])).then_inc(s_ld[c], 16)
                return
            for c in range(T):
                sp_or_dve.wait_ge(s_ld[c], 16)
                if c == 0:
                    nc.vector.tensor_copy(y, part(0)).then_inc(s_sm, 1)
                else:
                    sp_or_dve.wait_ge(s_sm, c)
                    nc.vector.tensor_tensor(y, y, part(c), ALU.add).then_inc(s_sm, 1)
            sp_or_dve.wait_ge(s_sm, T)

        zeros_d = acc_gin[0]
        window_stage("mlp0", tab_pre0, mlp0=True)

        C = lambda i: col[:, i:i + 1]
        s_c, s_sq, s_rt, s_scaled, s_a1, s_st, s_b1, s_lk, s_lk2, s_ms, s_sqs, s_norm, s_m3, s_e3, s_dg, s_dgr, s_di, \
            s_y, s_var, s_std, s_wr, s_gd = (sem(f"bn_{k}") for k in (
                "c sq rt scaled a1 st b1 lk lk2 ms sqs norm m3 e3 dg dgr di y var std wr gd").split())
        with nc.Block() as block:
            @block.tensor
            def _(pe):
                for b in range(NB):
                    ins = nc.tensor.matmul(banks[7][:, b:b + 1], acc[0:1, 1, b * P:(b + 1) * P], ones[0:1, 0:1],
                                           start=True, stop=True)
                ins.then_inc(s_dg, 1)
                pe.wait_ge(s_scaled, 1)
                for j in range(2 * NCH):
                    cols = slice(j * CW, (j + 1) * CW)
                    if j >= 2:
                        pe.wait_ge(s_st, j - 1)
                    nc.tensor.matmul(banks[j % 2][:, 0:CW], w0b[:, :], acc[:, 0, cols], start=True,
                                     stop=True).then_inc(s_a1, 1)
                    pe.wait_ge(s_st, j + 1)
                    if j >= 2:
                        pe.wait_ge(s_lk, j - 1)
                    nc.tensor.matmul(banks[2 + j % 2][:, 0:CW], w0cx[:, :], nodes_t[0:D, cols], start=True, stop=False)
                    nc.tensor.matmul(banks[2 + j % 2][:, 0:CW], w0ca[:, :], stage[:, j % 2, :], start=False,
                                     stop=True).then_inc(s_b1, 1)
                pe.wait_ge(s_norm, 1)
                node_products(pe, acc[:, 0, :], w0d[:, :], s_m3, s_e3)

            @block.scalar
            def _(act):
                act.wait_ge(s_sq, 1)
                nc.scalar.activation(C(S1), C(V1), ACT.Sqrt).then_inc(s_rt, 1)
                act.wait_ge(s_dgr, 1)
                nc.scalar.activation(dinv[:, :], ln[:, 0, :], ACT.Sqrt).then_inc(s_di, 1)
                for j in range(2 * NCH):
                    act.wait_ge(s_b1, j + 1)
                    nc.scalar.activation(acc[:, 0, j * CW:(j + 1) * CW], banks[2 + j % 2][:, 0:CW], ACT.Identity,
                                         bias=C(B3)).then_inc(s_lk, 1)
                act.wait_ge(s_ms, 1)
                nc.scalar.activation(acc[:, 1, 0:N], acc[:, 0, 0:N], ACT.Square, bias=C(NM2),
                                     accum_out=C(Q1)).then_inc(s_sqs, 1)
                act.wait_ge(s_sq, 2)
                nc.scalar.activation(C(S1), C(V2), ACT.Sqrt).then_inc(s_rt, 1)
                layer_norm_root(act, s_var, s_std)

            @block.vector
            def _(dve):
                step = stepper(dve, "bn_chain")
                step(nc.vector.tensor_reduce(C(M1), acc[:, 0, 0:N], AX.X, ALU.add))
                step(nc.vector.tensor_scalar(C(M1), C(M1), 1.0 / E, None, ALU.mult))
                step(nc.vector.tensor_tensor(stage[:, 0, 0:H], banks[5][:, 0:H], ident[:, :], ALU.mult))
                step(nc.vector.tensor_reduce(C(V1), stage[:, 0, 0:H], AX.X, ALU.add))
                step(nc.vector.tensor_tensor(C(Q1), C(M1), C(M1), ALU.mult))
                step(nc.vector.tensor_scalar(C(V1), C(V1), 1.0 / E, C(Q1), ALU.mult, ALU.subtract))
                step(nc.vector.tensor_scalar(C(V1), C(V1), 0.0, EPS, ALU.max, ALU.add))
                dve.sem_inc(s_sq, 1)
                dve.wait_ge(s_rt, 1)
                step(nc.vector.reciprocal(C(SC1), C(S1)))
                step(nc.vector.tensor_tensor(C(SC1), C(SC1), C(GB1), ALU.mult))
                step(nc.vector.tensor_tensor(C(SH1), C(M1), C(SC1), ALU.mult))
                step(nc.vector.tensor_tensor(C(SH1), C(GBE1), C(SH1), ALU.subtract))
                step(nc.vector.tensor_scalar(acc[:, 0, 0:NP], acc[:, 0, 0:NP], C(SC1), None, ALU.mult))
                nc.vector.scalar_tensor_tensor(out=acc[:, 0, 0:NP], in0=acc[:, 1, 0:NP], scalar=C(SH1),
                                               in1=acc[:, 0, 0:NP], op0=ALU.mult, op1=ALU.add).then_inc(s_scaled, 1)
                dve.wait_ge(s_dg, 1)
                step(nc.vector.tensor_scalar(ln[:, 0, :], banks[7][:, 0:NB], 1.0, None, ALU.add))
                dve.sem_inc(s_dgr, 1)
                for j in range(2 * NCH):
                    dve.wait_ge(s_a1, j + 1)
                    if j >= 2:
                        dve.wait_ge(s_b1, j - 1)
                    nc.vector.scalar_tensor_tensor(out=stage[:, j % 2, :], in0=acc[:, 1, j * CW:(j + 1) * CW],
                                                   scalar=C(B2), in1=banks[j % 2][:, 0:CW], op0=ALU.mult,
                                                   op1=ALU.add).then_inc(s_st, 1)
                dve.wait_ge(s_di, 1)
                step(nc.vector.reciprocal(dinv[:, :], dinv[:, :]))
                dve.wait_ge(s_lk, 2 * NCH)
                step(nc.vector.scalar_tensor_tensor(out=acc[:, 0, 0:NP], in0=acc[:, 0, 0:NP], scalar=SLOPE,
                                                    in1=acc[:, 0, 0:NP], op0=ALU.mult, op1=ALU.max))
                step(nc.vector.tensor_reduce(C(M2), acc[:, 0, 0:N], AX.X, ALU.add))
                step(nc.vector.tensor_scalar(C(M2), C(M2), 1.0 / N, None, ALU.mult))
                nc.vector.tensor_scalar(C(NM2), C(M2), -1.0, None, ALU.mult).then_inc(s_ms, 1)
                dve.wait_ge(s_sqs, 1)
                nc.vector.tensor_scalar(C(V2), C(Q1), 1.0 / N, EPS, ALU.mult, ALU.add).then_inc(s_sq, 1)
                dve.wait_ge(s_rt, 2)
                step(nc.vector.reciprocal(C(SC2), C(S1)))
                step(nc.vector.tensor_tensor(C(SC2), C(SC2), C(G2), ALU.mult))
                step(nc.vector.tensor_tensor(C(SH2), C(M2), C(SC2), ALU.mult))
                step(nc.vector.tensor_tensor(C(SH2), C(BE2), C(SH2), ALU.subtract))
                nc.vector.tensor_scalar(acc[:, 0, 0:NP], acc[:, 0, 0:NP], C(SC2), C(SH2), ALU.mult,
                                        ALU.add).then_inc(s_norm, 1)
                for q in range(NCH):
                    dve.wait_ge(s_m3, q + 1)
                    got, bl = chunk(q)
                    nc.vector.tensor_tensor(node_y[:, bl, 0:D], got, over_nodes(bc[:, 1, 0:D]), ALU.add).then_inc(s_e3, 1)
                dve.wait_ge(s_e3, NCH)
                y = node_y[:, :, 0:D]
                step(nc.vector.tensor_tensor(y, y, node_x[:, :, :], ALU.add))
                layer_norm(dve, (step, s_var, s_std), y)
                dve.sem_inc(s_y, 1)

            @block.sync
            def _(sp):
                sp.wait_ge(s_y, 1)
                sp.dma_start(node_rows(tab[0]), node_x[:, :, :]).then_inc(s_wr, 16)
                sp.wait_ge(s_wr, 16)

            @block.gpsimd
            def _(pool):
                retire(pool)

        window_stage("conv1", tab[0], mlp0=False)
        s_m, s_r, s_x, s_y, s_tr, s_ev, s_wr = (sem(f"c1_{k}") for k in "m r x y tr ev wr".split())
        with nc.Block() as block:
            @block.tensor
            def _(pe):
                node_products(pe, acc[0:D + 1, 0, :], wc[:, 0, :], s_m, s_r)
                pe.wait_ge(s_y, 1)
                pe.wait_ge(s_r, NCH)
                to_features(pe, acc[:, 0, :], node_y, D, s_tr, s_ev)

            @block.scalar
            def _(act):
                for q in range(NCH):
                    act.wait_ge(s_m, q + 1)
                    got, bl = chunk(q)
                    nc.scalar.activation(node_y[:, bl, 0:D], got, ACT.Relu).then_inc(s_r, 1)
                to_features_copy(act, acc[:, 0, :], D, s_tr, s_ev)

            @block.vector
            def _(dve):
                dve.wait_ge(s_r, NCH)
                nc.vector.tensor_tensor(node_y[:, :, 0:D], node_y[:, :, 0:D],
                                        dinv[:, :].unsqueeze(2).to_broadcast([P, NB, D]), ALU.mult).then_inc(s_y, 1)

            @block.sync
            def _(sp):
                sp.wait_ge(s_y, 1)
                sp.dma_start(node_rows(tab[1]), node_y[:, :, 0:D]).then_inc(s_wr, 16)
                sp.wait_ge(s_wr, 16)

            @block.gpsimd
            def _(pool):
                retire(pool)

        window_stage("conv2", tab[1], mlp0=False)
        s_m2, s_r2, s_y2, s_wr2 = (sem(f"c2_{k}") for k in "m r y wr".split())
        with nc.Block() as block:
            @block.tensor
            def _(pe):
                node_products(pe, acc[0:D, 0, :], wc[0:D, 1, :], s_m2, s_r2)

            @block.vector
            def _(dve):
                step = stepper(dve, "c2_chain")
                for q in range(NCH):
                    dve.wait_ge(s_m2, q + 1)
                    got, bl = chunk(q)
                    nc.vector.tensor_tensor(node_y[:, bl, 0:D], got, dinv[:, bl].unsqueeze(2).to_broadcast([P, CH, D]),
                                            ALU.mult).then_inc(s_r2, 1)
                dve.wait_ge(s_r2, NCH)
                y = node_y[:, :, 0:D]
                step(nc.vector.tensor_tensor(y, y, bc[:, 2, 0:D].unsqueeze(1).to_broadcast([P, NB, D]), ALU.add))
                nc.vector.tensor_scalar(y, y, 0.0, None, ALU.max).then_inc(s_y2, 1)

            @block.sync
            def _(sp):
                sp.wait_ge(s_y2, 1)
                sp.dma_start(node_rows(tab[2]), node_y[:, :, 0:D]).then_inc(s_wr2, 16)
                sp.wait_ge(s_wr2, 16)

            @block.gpsimd
            def _(pool):
                retire(pool)

        window_stage("conv3", tab[2], mlp0=False)
        s_m4, s_r4, s_y4, s_var4, s_std4, s_wr4 = (sem(f"c3_{k}") for k in "m r y var std wr".split())
        with nc.Block() as block:
            @block.tensor
            def _(pe):
                node_products(pe, acc[0:D + 1, 0, :], wc[:, 2, :], s_m4, s_r4)

            @block.scalar
            def _(act):
                layer_norm_root(act, s_var4, s_std4)

            @block.vector
            def _(dve):
                step = stepper(dve, "c3_chain")
                for q in range(NCH):
                    dve.wait_ge(s_m4, q + 1)
                    got, bl = chunk(q)
                    nc.vector.tensor_tensor(node_y[:, bl, 0:D], got, node_x[:, bl, :], ALU.add).then_inc(s_r4, 1)
                dve.wait_ge(s_r4, NCH)
                layer_norm(dve, (step, s_var4, s_std4), node_y[:, :, 0:D])
                dve.sem_inc(s_y4, 1)

            @block.sync
            def _(sp):
                sp.wait_ge(s_y4, 1)
                sp.dma_start(node_rows(tab[3]), node_x[:, :, :]).then_inc(s_wr4, 16)
                sp.wait_ge(s_wr4, 16)

            @block.gpsimd
            def _(pool):
                retire(pool)

        scatter_stage("gin", tab[3], acc_gin, mlp3=False)
        s_ld5 = [sem(f"g_ld{c}") for c in range(T)]
        s_sm5, s_in5, s_tr5, s_ev5, s_a5, s_h5, s_m5, s_r5, s_var5, s_std5, s_x5, s_tr6, s_ev6, s_m6, s_r6, s_wr5 = (
            sem(f"g_{k}") for k in "sm in tr ev a h m r var std x tr6 ev6 m6 r6 wr".split())
        with nc.Block() as block:
            @block.sync
            def _(sp):
                add_accumulators(sp, acc_gin, D, s_ld5, s_sm5, load=True)
                sp.wait_ge(s_r6, NCH)
                sp.dma_start(node_rows(tab[4]), node_y[:, :, 0:D]).then_inc(s_wr5, 16)
                sp.wait_ge(s_wr5, 16)

            @block.tensor
            def _(pe):
                pe.wait_ge(s_in5, 1)
                to_features(pe, nodes_t, node_y, D, s_tr5, s_ev5)
                pe.wait_ge(s_ev5, (NB + 3) // 4)
                for j in range(2 * NCH):
                    if j >= 2:
                        pe.wait_ge(s_h5, j - 1)
                    nc.tensor.matmul(banks[2 + j % 2][:, 0:CW], wg1[:, :], nodes_t[0:D, j * CW:(j + 1) * CW], start=True,
                                     stop=True).then_inc(s_a5, 1)
                pe.wait_ge(s_h5, 2 * NCH)
                node_products(pe, acc[:, 0, :], wg2[:, :], s_m5, s_r5, first=4)
                pe.wait_ge(s_x5, 1)
                to_features(pe, nodes_t, node_x, D, s_tr6, s_ev6)
                pe.wait_ge(s_ev6, (NB + 3) // 4)
                node_products(pe, nodes_t[0:D, :], w3x[:, :], s_m6, s_r6, first=6)

            @block.scalar
            def _(act):
                to_features_copy(act, nodes_t, D, s_tr5, s_ev5)
                for j in range(2 * NCH):
                    act.wait_ge(s_a5, j + 1)
                    nc.scalar.activation(acc[:, 0, j * CW:(j + 1) * CW], banks[2 + j % 2][:, 0:CW], ACT.Relu,
                                         bias=C(BG1)).then_inc(s_h5, 1)
                layer_norm_root(act, s_var5, s_std5)
                to_features_copy(act, nodes_t, D, s_tr6, s_ev6)

            @block.vector
            def _(dve):
                step = stepper(dve, "g_chain")
                add_accumulators(dve, acc_gin, D, s_ld5, s_sm5, load=False)
                y = node_y[:, :, 0:D]
                nc.vector.tensor_tensor(y, y, node_x[:, :, :], ALU.add).then_inc(s_in5, 1)
                dve.wait_ge(s_tr5, (NB + 3) // 4)
                for q in range(NCH):
                    dve.wait_ge(s_m5, q + 1)
                    got, bl = chunk(q, 4)
                    nc.vector.tensor_tensor(node_y[:, bl, 0:D], got, over_nodes(bc[:, 3, 0:D]), ALU.add).then_inc(s_r5, 1)
                dve.wait_ge(s_r5, NCH)
                step(nc.vector.tensor_tensor(y, y, node_x[:, :, :], ALU.add))
                layer_norm(dve, (step, s_var5, s_std5), y)
                dve.sem_inc(s_x5, 1)
                for q in range(NCH):
                    dve.wait_ge(s_m6, q + 1)
                    got, bl = chunk(q, 6)
                    nc.vector.tensor_tensor(node_y[:, bl, 0:D], got, over_nodes(bc[:, 4, 0:D]), ALU.add).then_inc(s_r6, 1)

            @block.gpsimd
            def _(pool):
                retire(pool)

        scatter_stage("mean", tab[4], acc_mean, mlp3=True)
        s_ld7 = [sem(f"m_ld{c}") for c in range(T)]
        s_sm7, s_in7, s_tr7, s_ev7, s_a7, s_st7, s_b7, s_h7, s_m7, s_r7, s_var7, s_std7, s_x7, s_out = (
            sem(f"m_{k}") for k in "sm in tr ev a st b h m r var std x out".split())
        with nc.Block() as block:
            @block.sync
            def _(sp):
                add_accumulators(sp, acc_mean, D + 1, s_ld7, s_sm7, load=True)
                sp.wait_ge(s_x7, 1)
                sp.dma_start(node_rows(out[0:(NB - 1) * P, :]), node_x[:, 0:NB - 1, :]).then_inc(s_out, 16)
                sp.dma_start(out[(NB - 1) * P:N, :], node_x[0:LB, NB - 1, :]).then_inc(s_out, 16)
                sp.wait_ge(s_out, 32)

            @block.tensor
            def _(pe):
                pe.wait_ge(s_in7, 1)
                to_features(pe, acc[:, 0, :], node_y, D + 1, s_tr7, s_ev7)
                pe.wait_ge(s_ev7, (NB + 3) // 4)
                for j in range(2 * NCH):
                    cols = slice(j * CW, (j + 1) * CW)
                    if j >= 2:
                        pe.wait_ge(s_st7, j - 1)
                    nc.tensor.matmul(banks[2 + j % 2][0:D, 0:CW], w3b[:, :], acc[0:D + 1, 0, cols], start=True,
                                     stop=True).then_inc(s_a7, 1)
                    pe.wait_ge(s_st7, j + 1)
                    if j >= 2:
                        pe.wait_ge(s_h7, j - 1)
                    nc.tensor.matmul(banks[4 + j % 2][0:D, 0:CW], w3cx[:, :], nodes_t[0:D, cols], start=True, stop=False)
                    nc.tensor.matmul(banks[4 + j % 2][0:D, 0:CW], w3ca[:, :], stage[0:D, j % 2, :], start=False,
                                     stop=True).then_inc(s_b7, 1)
                pe.wait_ge(s_h7, 2 * NCH)
                node_products(pe, acc[0:D, 1, :], w3d[:, :], s_m7, s_r7, first=6)

            @block.scalar
            def _(act):
                to_features_copy(act, acc[:, 0, :], D + 1, s_tr7, s_ev7)
                for j in range(2 * NCH):
                    act.wait_ge(s_a7, j + 1)
                    nc.scalar.copy(stage[0:D, j % 2, :], banks[2 + j % 2][0:D, 0:CW]).then_inc(s_st7, 1)
                    act.wait_ge(s_b7, j + 1)
                    nc.scalar.activation(acc[0:D, 1, j * CW:(j + 1) * CW], banks[4 + j % 2][0:D, 0:CW], ACT.Relu,
                                         bias=col[0:D, B3A2:B3A2 + 1]).then_inc(s_h7, 1)
                layer_norm_root(act, s_var7, s_std7)

            @block.vector
            def _(dve):
                step = stepper(dve, "m_chain")
                add_accumulators(dve, acc_mean, D + 1, s_ld7, s_sm7, load=False)
                count = ln[:, 0, :].unsqueeze(2)
                step(nc.vector.tensor_scalar(count, node_y[:, :, D:D + 1], 1.0, None, ALU.max))
                step(nc.vector.reciprocal(ln[:, 1, :], ln[:, 0, :]))
                nc.vector.tensor_tensor(node_y[:, :, :], node_y[:, :, :],
                                        ln[:, 1, :].unsqueeze(2).to_broadcast([P, NB, D + 1]),
                                        ALU.mult).then_inc(s_in7, 1)
                for q in range(NCH):
                    dve.wait_ge(s_m7, q + 1)
                    got, bl = chunk(q, 6)
                    nc.vector.tensor_tensor(node_y[:, bl, 0:D], got, over_nodes(bc[:, 1, D:2 * D]),
                                            ALU.add).then_inc(s_r7, 1)
                dve.wait_ge(s_r7, NCH)
                y = node_y[:, :, 0:D]
                step(nc.vector.tensor_tensor(y, y, node_x[:, :, :], ALU.add))
                layer_norm(dve, (step, s_var7, s_std7), y)
                dve.sem_inc(s_x7, 1)

            @block.gpsimd
            def _(pool):
                retire(pool)


WEIGHTS = ["L0_gnn_W1", "L0_gnn_b1", "L0_gnn_g1", "L0_gnn_be1", "L0_gnn_W2", "L0_gnn_b2", "L0_gnn_W3", "L0_gnn_b3",
           "L0_gnn_g2", "L0_gnn_be2", "L0_gnn_W4", "L0_gnn_b4", "L1_gnn_W1", "L1_gnn_b1", "L1_gnn_W2", "L1_gnn_b2",
           "L1_gnn_W3", "L1_gnn_b3", "L2_gnn_W1", "L2_gnn_b1", "L2_gnn_W2", "L2_gnn_b2", "L3_gnn_W1a", "L3_gnn_b1a",
           "L3_gnn_W1b", "L3_gnn_b1b", "L3_gnn_W2a", "L3_gnn_b2a", "L3_gnn_W2b", "L3_gnn_b2b"]


def kernel(**inputs):
    import numpy as np
    import concourse.bacc as bacc
    from concourse.bass_utils import run_bass_kernel_spmd

    nc = bacc.Bacc("TRN2", target_bir_lowering=False, num_devices=1)
    arrays, handles = {}, {}
    for name in ["x", "src", "dst", "edge_attr_64"] + WEIGHTS:
        a = np.ascontiguousarray(inputs[name])
        arrays[f"in_{name}"] = a
        handles[name] = nc.dram_tensor(f"in_{name}", a.shape, mybir.dt.from_np(a.dtype), kind="ExternalInput").ap()
    out = nc.dram_tensor("out", (N, D), F32, kind="ExternalOutput").ap()
    build(nc, handles["x"], handles["src"], handles["dst"], handles["edge_attr_64"], {k: handles[k] for k in WEIGHTS}, out)
    return run_bass_kernel_spmd(nc, [arrays], core_ids=[0]).results[0]["out"]
```

```python
from contextlib import ExitStack

import concourse.bass as bass
from concourse import mybir

P = 128
N, E, D, H = 6250, 206250, 64, 128
T = 8
GE = T * P
NG = (E + GE - 1) // GE
LAST = E - (NG - 1) * GE
NB = (N + P - 1) // P
NP = NB * P
LB = N - (NB - 1) * P
WIN = 64
NA = NP + P
CH = 7
NCH = NB // CH
CW = CH * P // 2
EPS = 1e-5
SLOPE = 0.01
assert NG % 2 == 0 and NB % CH == 0 and (2 * NP) % (2 * CW) == 0

F32, I32, U32, BF16 = mybir.dt.float32, mybir.dt.int32, mybir.dt.uint32, mybir.dt.bfloat16
ALU, ACT, AX = mybir.AluOpType, mybir.ActivationFunctionType, mybir.AxisListType


def build(nc, x, src, dst, edge_attr, W, out):
    ctx = ExitStack()
    with ctx:
        def sb(name, shape, dt=F32):
            return ctx.enter_context(nc.sbuf_tensor(name, shape, dt))

        def sem(name):
            return ctx.enter_context(nc.semaphore(name))

        def dram(name, shape, dt=F32):
            return nc.dram_tensor(name, shape, dt, kind="Internal").ap()

        tab_pre0 = dram("tab_pre0", (NP, H))
        tab = [dram(f"tab_{n}", (NP, D)) for n in ("conv1", "conv2", "conv3")]
        tab_gin = dram("tab_gin", (NA, D + 1))
        tab_pre3 = dram("tab_pre3", (NA, D))
        acc_gin = [dram(f"acc_gin{c}", (NA, D + 1)) for c in range(T)]
        acc_mean = [dram(f"acc_mean{c}", (NA, D)) for c in range(T)]
        span_d = dram("span_d", (2, NG), I32)

        ident = sb("ident", [P, P])
        lower = sb("lower", [P, P])
        ones = sb("ones", [P, P])
        iota_i = sb("iota_i", [P, WIN], I32)
        iota_w = sb("iota_w", [P, WIN])
        trash_i = sb("trash_i", [P, 1], I32)
        trash = sb("trash", [P, 1])
        src_i = sb("src_i", [P, NG, T], I32)
        dst_i = sb("dst_i", [P, NG, T], I32)
        src_f = sb("src_f", [P, NG, T])
        dst_rel = sb("dst_rel", [P, NG, T])
        scat_i = dst_i
        span_row = sb("span_row", [1, 2, NG], I32)
        acc = sb("acc", [P, 2, NA])
        nodes_t = sb("nodes_t", [D + 1, NA])
        node_x = sb("node_x", [P, NB, D])
        node_y = sb("node_y", [P, NB, D + 1])
        node_z = sb("node_z", [P, NB, D + 1])
        dinv = sb("dinv", [P, NB])
        ln = sb("ln", [P, 4, NB])
        count = sb("count", [P, NB])
        gath = sb("gath", [P, 2, T, H])
        eattr = sb("eattr", [P, 2, T, D])
        eattr_t = sb("eattr_t", [P, 2, T // 2, P])
        hid = sb("hid", [P, 2, T, H])
        squares = sb("squares", [P, T, H])
        sq_sum = sb("sq_sum", [P, T, H])
        onehot = sb("onehot", [P, 2, T, WIN])
        onehot_b = sb("onehot_b", [P, 2, T, WIN], BF16)
        onehot_x = node_z[:, :, :].rearrange("p b f -> p (b f)")[:, 0:T * WIN].rearrange("p (c n) -> p c n", c=T)
        onehot_xb = sb("onehot_xb", [P, T, WIN], BF16)
        drel = sb("drel", [P, T])
        idx_g = sb("idx_g", [P, 2, T], I32)
        idx_s = sb("idx_s", [P, 2, T], I32)
        same = sb("same", [P, 2, T, P], BF16)
        dup = sb("dup", [P, 2, T])
        addend = node_y[:, :, :].rearrange("p b f -> p (b f)")[:, 0:2 * T * (D + 1)].rearrange(
            "p (s c f) -> p s c f", s=2, c=T)
        zero_w = sb("zero_w", [P, H])
        zero_b = sb("zero_b", [P, H], BF16)
        ones_b = sb("ones_b", [P, P], BF16)
        earlier = sb("earlier", [P, T, P], BF16)
        lower_b = sb("lower_b", [P, P], BF16)
        src_s = sb("src_s", [P, 2, T])
        lhs3 = sb("lhs3", [P, 3, D])
        win_x = sb("win_x", [P, 3, D + 1])
        wnode = sb("wnode", [P, 2])
        stage = sb("stage", [P, 2, CW])
        col = sb("col", [P, 24])
        bc = sb("bc", [P, 5, H])
        w0x = sb("w0x", [D, H])
        w0e = sb("w0e", [P, 2 * H])
        w0b = sb("w0b", [H, H])
        w0cx = sb("w0cx", [D, H])
        w0ca = sb("w0ca", [H, H])
        w0d = sb("w0d", [H, D])
        wc_in = sb("wc_in", [D, 3, D])
        wc = sb("wc", [D + 1, 3, D])
        wg1 = sb("wg1", [D, H])
        wg2 = sb("wg2", [H, D])
        w3x = sb("w3x", [D, D])
        w3b = sb("w3b", [D + 1, D])
        w3cx = sb("w3cx", [D, D])
        w3ca = sb("w3ca", [D, D])
        w3d = sb("w3d", [D, D])

        banks = [ctx.enter_context(nc.psum_tensor(f"bank{i}", [P, 512], F32)) for i in range(8)]

        def node_rows(t):
            return t.rearrange("(b p) f -> p b f", p=P)

        def row_bc(v):
            return v.rearrange("(a f) -> a f", a=1).to_broadcast([P, v.shape[0]])

        def column(v):
            return v.rearrange("(f a) -> f a", a=1)

        GB1, GBE1, B2, B3, G2, BE2, BG1, B3A2 = range(8)
        M1, V1, SC1, SH1, S1, Q1, M2, V2, SC2, SH2, NM2 = range(8, 19)

        s_fill = sem("s_fill")
        s_par = sem("s_par")
        s_idx = sem("s_idx")
        s_cst = sem("s_cst")
        s_spn = sem("s_spn")
        s_sp0 = sem("s_sp0")
        s_span = sem("s_span")
        s_zero = sem("s_zero")
        s_gm = sem("s_gm")
        with nc.Block() as block:
            zeros = acc[:, 0, 0:(NA // P) * (D + 1)]
            ends = acc[:, 1, 0:2 * GE].bitcast(I32)
            QG = NG // 2
            mn, mx = ln[0:QG, 0, 0:2].bitcast(I32), ln[0:QG, 1, 0:2].bitcast(I32)
            base_bc = hid[:, 0, 0:2, :].rearrange("p a b -> p (a b)")[:, 0:NG].bitcast(I32)
            n_param = [0]

            @block.sync
            def _(sp):
                tail = (NG - 2) * GE
                sp.dma_start(ends[0:QG - 1, :], dst[0:tail].rearrange("(q e) -> q e", q=QG - 1)).then_inc(s_gm, 16)
                sp.dma_start(ends[QG - 1:QG, 0:GE + LAST], dst[tail:E].rearrange("(q e) -> q e", q=1)).then_inc(s_gm, 16)
                sp.dma_start(ends[QG - 1:QG, GE + LAST:2 * GE],
                             dst[E - GE + LAST:E].rearrange("(q e) -> q e", q=1)).then_inc(s_gm, 16)
                sp.wait_ge(s_fill, 2)
                full, part = LAST // T, LAST % T
                for t, d in ((src_i, src), (dst_i, dst)):
                    sp.dma_start(t[:, 0:NG - 1, :],
                                 d[0:(NG - 1) * GE].rearrange("(g p c) -> p g c", p=P, c=T)).then_inc(s_idx, 16)
                    sp.dma_start(t[0:full, NG - 1, :],
                                 d[(NG - 1) * GE:(NG - 1) * GE + full * T].rearrange("(p c) -> p c", c=T)).then_inc(s_idx, 16)
                    if part:
                        sp.dma_start(t[full:full + 1, NG - 1, 0:part],
                                     d[(NG - 1) * GE + full * T:E].rearrange("(p c) -> p c", p=1)).then_inc(s_idx, 16)
                sp.wait_ge(s_spn, 1)
                sp.dma_start(span_d[0, :].rearrange("(q r) -> q r", r=2), mn).then_inc(s_sp0, 16)
                sp.dma_start(span_d[1, :].rearrange("(q r) -> q r", r=2), mx).then_inc(s_sp0, 16)
                sp.wait_ge(s_sp0, 32)
                sp.dma_start(span_row[:, :, :], span_d.rearrange("(a t) g -> a t g", a=1)).then_inc(s_span, 16)
                sp.dma_start(base_bc, span_d[0:1, :].to_broadcast([P, NG])).then_inc(s_span, 16)
                sp.wait_ge(s_span, 32)

            @block.scalar
            def _(act):
                def load(dst_ap, src_ap):
                    act.dma_start(dst_ap, src_ap).then_inc(s_par, 16)
                    n_param[0] += 1

                act.wait_ge(s_fill, 4)
                load(node_x[:, 0:NB - 1, :], node_rows(x[0:(NB - 1) * P, :]))
                load(node_x[0:LB, NB - 1, :], x[(NB - 1) * P:N, :])
                load(w0x[:, :], W["L0_gnn_W1"][0:D, :])
                load(w0e[0:D, 0:H], W["L0_gnn_W1"][D:2 * D, :])
                load(w0e[D:P, H:2 * H], W["L0_gnn_W1"][D:2 * D, :])
                load(w0b[:, :], W["L0_gnn_W2"])
                load(w0cx[:, :], W["L0_gnn_W3"][0:D, :])
                load(w0ca[:, :], W["L0_gnn_W3"][D:D + H, :])
                load(w0d[:, :], W["L0_gnn_W4"])
                for i in range(3):
                    load(wc_in[:, i, :], W[f"L1_gnn_W{i + 1}"])
                    load(wc[D:D + 1, i, :], W[f"L1_gnn_b{i + 1}"].rearrange("(a f) -> a f", a=1))
                load(wg1[:, :], W["L2_gnn_W1"])
                load(wg2[:, :], W["L2_gnn_W2"])
                load(w3x[:, :], W["L3_gnn_W1a"][0:D, :])
                for s in range(2):
                    load(lhs3[0:D, s, :], W["L3_gnn_W1a"][D:2 * D, :])
                load(w3b[0:D, :], W["L3_gnn_W1b"])
                load(w3b[D:D + 1, :], W["L3_gnn_b1b"].rearrange("(a f) -> a f", a=1))
                load(w3cx[:, :], W["L3_gnn_W2a"][0:D, :])
                load(w3ca[:, :], W["L3_gnn_W2a"][D:2 * D, :])
                load(w3d[:, :], W["L3_gnn_W2b"])
                for c, name in ((GB1, "L0_gnn_g1"), (GBE1, "L0_gnn_be1"), (B2, "L0_gnn_b2"), (B3, "L0_gnn_b3"),
                                (G2, "L0_gnn_g2"), (BE2, "L0_gnn_be2"), (BG1, "L2_gnn_b1")):
                    load(col[:, c:c + 1], column(W[name]))
                load(col[0:D, B3A2:B3A2 + 1], column(W["L3_gnn_b2a"]))
                for r, name in enumerate(("L0_gnn_b1", "L0_gnn_b4", "L1_gnn_b2", "L2_gnn_b2", "L3_gnn_b1a")):
                    load(bc[:, r, 0:W[name].shape[0]], row_bc(W[name]))
                load(bc[:, 1, D:2 * D], row_bc(W["L3_gnn_b2b"]))
                act.wait_ge(s_fill, 5)
                for c in range(T):
                    act.dma_start(acc_mean[c].rearrange("(p r) f -> p (r f)", p=P),
                                  zeros[:, 0:(NA // P) * D]).then_inc(s_zero, 16)
                    act.dma_start(acc_gin[c].rearrange("(p r) f -> p (r f)", p=P), zeros).then_inc(s_zero, 16)
                act.dma_start(tab_gin[NP:NA, :], zeros[:, 0:D + 1]).then_inc(s_zero, 16)
                act.dma_start(tab_pre3[NP:NA, :], zeros[:, 0:D]).then_inc(s_zero, 16)
                act.wait_ge(s_par, 16 * n_param[0])
                act.wait_ge(s_zero, 32 * T + 32)

            @block.gpsimd
            def _(pool):
                nc.gpsimd.memset(src_i[:, NG - 1, :], N).then_inc(s_fill, 1)
                nc.gpsimd.memset(dst_i[:, NG - 1, :], N).then_inc(s_fill, 1)
                nc.gpsimd.memset(node_x[:, NB - 1, :], 0.0).then_inc(s_fill, 1)
                nc.gpsimd.memset(w0e[:, :], 0.0).then_inc(s_fill, 1)
                nc.gpsimd.memset(zeros, 0.0).then_inc(s_fill, 1)
                nc.gpsimd.memset(zero_w[:, :], 0.0)
                nc.gpsimd.memset(zero_b[:, :], 0.0)
                nc.gpsimd.memset(ones_b[:, :], 1.0)
                nc.gpsimd.memset(lhs3[:, 2, :], 0.0)
                nc.gpsimd.memset(ones[:, :], 1.0).then_inc(s_cst, 1)
                pool.wait_ge(s_cst, 1)
                nc.gpsimd.affine_select(out=ident[:, :], in_=ones[:, :], compare_op=ALU.is_equal, fill=0.0, base=0,
                                        pattern=[[-1, P]], channel_multiplier=1).then_inc(s_cst, 1)
                nc.gpsimd.affine_select(out=lower[:, :], in_=ones[:, :], compare_op=ALU.is_gt, fill=0.0, base=0,
                                        pattern=[[-1, P]], channel_multiplier=1).then_inc(s_cst, 1)
                nc.gpsimd.iota(iota_i[:, :], [[1, WIN]], base=0, channel_multiplier=0).then_inc(s_cst, 1)
                nc.gpsimd.iota(trash_i[:, :], [[0, 1]], base=N, channel_multiplier=1).then_inc(s_cst, 1)

            @block.vector
            def _(dve):
                s_d = sem("s_d0")
                dve.wait_ge(s_gm, 48)
                e3 = ends[0:QG, :].rearrange("q (r e) -> q r e", r=2)
                nc.vector.tensor_reduce(mn, e3, AX.X, ALU.min).then_inc(s_d, 1)
                nc.vector.tensor_reduce(mx, e3, AX.X, ALU.max).then_inc(s_d, 1)
                dve.wait_ge(s_d, 2)
                nc.vector.tensor_tensor(mx, mx, mn, ALU.subtract).then_inc(s_d, 1)
                dve.wait_ge(s_d, 3)
                nc.vector.tensor_scalar(mx, mx, WIN.bit_length() - 1, None, ALU.arith_shift_right).then_inc(s_d, 1)
                dve.wait_ge(s_d, 4)
                nc.vector.tensor_scalar(mx, mx, 1, None, ALU.add).then_inc(s_spn, 1)
                dve.wait_ge(s_cst, 5)
                nc.vector.tensor_copy(iota_w[:, :], iota_i[:, :])
                nc.vector.tensor_copy(trash[:, :], trash_i[:, :]).then_inc(s_d, 1)
                nc.vector.tensor_copy(lower_b[:, :], lower[:, :])
                dve.wait_ge(s_d, 5)
                nc.vector.tensor_scalar(wnode[:, 0:1], trash[:, :], -float(N + D), None, ALU.add)
                dve.wait_ge(s_idx, 16 * (6 if LAST % T else 4))
                nc.vector.tensor_copy(src_f[:, :, :], src_i[:, :, :])
                dve.wait_ge(s_span, 32)
                nc.vector.tensor_tensor(dst_rel[:, :, :], dst_i[:, :, :],
                                        base_bc.unsqueeze(2).to_broadcast([P, NG, T]), ALU.subtract).then_inc(s_d, 1)
                dve.wait_ge(s_d, 6)
                nc.vector.scalar_tensor_tensor(out=dst_rel[:, NG - 1, :], in0=dst_i[:, NG - 1, :], scalar=float(N),
                                               in1=dst_rel[:, NG - 1, :], op0=ALU.is_lt, op1=ALU.mult).then_inc(s_d, 1)
                dve.wait_ge(s_d, 7)
                nc.vector.scalar_tensor_tensor(out=dst_rel[:, NG - 1, :], in0=dst_i[:, NG - 1, :], scalar=float(N),
                                               in1=dst_rel[:, NG - 1, :], op0=ALU.is_ge,
                                               op1=ALU.subtract).then_inc(s_d, 1)
                dve.wait_ge(s_d, 8)
                nc.vector.tensor_scalar(dst_rel[:, NG - 1, :], dst_rel[:, NG - 1, :], -1.0, None, ALU.mult)

        def to_features(pe, dst_t, source, width, s_tr, s_ev, src_ready=None):
            for q in range((NB + 3) // 4):
                if q >= 2:
                    pe.wait_ge(s_ev, q - 1)
                for k in range(min(4, NB - 4 * q)):
                    last = nc.tensor.transpose(banks[q % 2][0:width, k * P:(k + 1) * P],
                                               source[:, 4 * q + k, 0:width], ident[:, :])
                last.then_inc(s_tr, 1)

        def to_features_copy(act, dst_t, width, s_tr, s_ev):
            for q in range((NB + 3) // 4):
                act.wait_ge(s_tr, q + 1)
                n = min(4, NB - 4 * q) * P
                nc.scalar.copy(dst_t[0:width, 4 * q * P:4 * q * P + n], banks[q % 2][0:width, 0:n]).then_inc(s_ev, 1)

        def layer_norm(dve, chain, y):
            step, s_var, s_std = chain
            b3 = lambda t: t.unsqueeze(2).to_broadcast([P, NB, D])
            step(nc.vector.tensor_reduce(ln[:, 0, :], y, AX.X, ALU.add))
            step(nc.vector.tensor_scalar(ln[:, 0, :], ln[:, 0, :], 1.0 / D, None, ALU.mult))
            step(nc.vector.tensor_tensor(y, y, b3(ln[:, 0, :]), ALU.subtract))
            step(nc.vector.tensor_tensor(node_z[:, :, 0:D], y, y, ALU.mult))
            step(nc.vector.tensor_reduce(ln[:, 1, :], node_z[:, :, 0:D], AX.X, ALU.add))
            nc.vector.tensor_scalar(ln[:, 1, :], ln[:, 1, :], 1.0 / D, EPS, ALU.mult, ALU.add).then_inc(s_var, 1)
            dve.wait_ge(s_std, 1)
            step(nc.vector.reciprocal(ln[:, 3, :], ln[:, 2, :]))
            step(nc.vector.tensor_tensor(node_x[:, :, :], y, b3(ln[:, 3, :]), ALU.mult))

        def layer_norm_root(act, s_var, s_std):
            act.wait_ge(s_var, 1)
            nc.scalar.activation(ln[:, 2, :], ln[:, 1, :], ACT.Sqrt).then_inc(s_std, 1)

        def stepper(dve, name):
            s = sem(name)
            count = [0]

            def step(ins):
                count[0] += 1
                ins.then_inc(s, 1)
                dve.wait_ge(s, count[0])
            return step

        s_t, s_e, s_m, s_a, s_w, s_wt, s_wv = (sem(f"pre_{k}") for k in "temawuv")
        pre = acc[:, 0, 0:NB * H].rearrange("p (b f) -> p b f", f=H)
        with nc.Block() as block:
            @block.tensor
            def _(pe):
                to_features(pe, nodes_t, node_x, D, s_t, s_e)
                for i in range(3):
                    last = nc.tensor.transpose(banks[4][0:D, i * D:(i + 1) * D], wc_in[:, i, :], ident[0:D, 0:D])
                last.then_inc(s_wt, 1)
                pe.wait_ge(s_e, (NB + 3) // 4)
                for q in range((NB + 3) // 4):
                    if q >= 2:
                        pe.wait_ge(s_a, q - 1)
                    for k in range(min(4, NB - 4 * q)):
                        b = 4 * q + k
                        last = nc.tensor.matmul(banks[2 + q % 2][:, k * H:(k + 1) * H], nodes_t[0:D, b * P:(b + 1) * P],
                                                w0x[:, :], start=True, stop=True)
                    last.then_inc(s_m, 1)

            @block.scalar
            def _(act):
                to_features_copy(act, nodes_t, D, s_t, s_e)
                act.wait_ge(s_wt, 1)
                nc.scalar.copy(wc[0:D, :, :], banks[4][0:D, 0:3 * D].rearrange("p (i f) -> p i f", i=3))

            @block.vector
            def _(dve):
                for q in range((NB + 3) // 4):
                    dve.wait_ge(s_m, q + 1)
                    n = min(4, NB - 4 * q)
                    nc.vector.tensor_tensor(pre[:, 4 * q:4 * q + n, :],
                                            banks[2 + q % 2][:, 0:n * H].rearrange("p (b f) -> p b f", f=H),
                                            bc[:, 0, :].unsqueeze(1).to_broadcast([P, n, H]), ALU.add).then_inc(s_a, 1)

            @block.sync
            def _(sp):
                sp.wait_ge(s_a, (NB + 3) // 4)
                sp.dma_start(node_rows(tab_pre0[0:(NB - 1) * P, :]), pre[:, 0:NB - 1, :]).then_inc(s_w, 16)
                sp.dma_start(tab_pre0[(NB - 1) * P:N, :], pre[0:LB, NB - 1, :]).then_inc(s_w, 16)
                sp.dma_start(tab_pre0[N:NP, :], zero_w[0:NP - N, :]).then_inc(s_w, 16)
                sp.wait_ge(s_w, 48)

        def both(eng, body, end=NG // 2):
            body(0, 0, 0)
            body(0, 1, 1)
            with eng.Fori(1, end) as it:
                for s in range(2):
                    body(it, s, it * 2 + s)

        def wait(eng, semaphore, value):
            if not isinstance(value, int) or value > 0:
                eng.wait_ge(semaphore, value)

        def send_indices(sp, it, s, g, table, gathered, here):
            wait(sp, gathered[s], 16 * T * it)
            sp.dma_start(idx_g[:, s, :], table[:, bass.ds(g, 1), :].rearrange("p a c -> p (a c)")).then_inc(here[s], 16)

        def send_attributes(sp, it, s, g, at, turned, there):
            wait(sp, turned[s], it)
            sp.dma_start(at, edge_attr[bass.ds(g * GE, GE), :].rearrange("(p c) f -> p c f", p=P)).then_inc(there[s], 16)

        def send_last_attributes(sp, at, filler, turned, there):
            sp.wait_ge(turned[1], NG // 2 - 1)
            full, part = LAST // T, LAST % T
            e0 = (NG - 1) * GE
            sp.dma_start(at[0:full, :, :], edge_attr[e0:e0 + full * T, :].rearrange(
                "(p c) f -> p c f", c=T)).then_inc(there[1], 16)
            if part:
                sp.dma_start(at[full:full + 1, 0:part, :], edge_attr[e0 + full * T:E, :].rearrange(
                    "(p c) f -> p c f", p=1)).then_inc(there[1], 16)
                sp.dma_start(at[full:full + 1, part:T, :], filler[0:T - part, :].rearrange(
                    "(p c) f -> p c f", p=1)).then_inc(there[1], 16)
            first = full + (part > 0)
            sp.dma_start(at[first:P, :, :], filler[0:(P - first) * T, :].rearrange(
                "(p c) f -> p c f", c=T)).then_inc(there[1], 16)

        N_LAST = (3 if LAST % T else 1) + 1

        def gather_rows(pool, it, s, table, width, here, free, gathered, begun):
            indices, used = pool.snap(16 * (it + 1)), pool.snap(it)
            pool.wait_ge(here[s], indices)
            wait(pool, free[s], used)
            pool.sem_inc(begun, 1)
            for c in range(T):
                pool.indirect_dma_start(gath[:, s, c, 0:width], None, table[:, :], bass.IndirectOffsetOnAxis(
                    ap=idx_g[:, s, c:c + 1].bitcast(U32), axis=0)).then_inc(gathered[s], 16)

        edge_sems = []

        def edge_sem(name):
            edge_sems.append(nc.alloc_semaphore(name=name))
            return edge_sems[-1]

        def slots(name):
            return [edge_sem(f"{name}0"), edge_sem(f"{name}1")]

        def retire(pool):
            nc.clear_and_free_semaphores(edge_sems)
            edge_sems.clear()

        def copy_attributes(act, it, s, turned, copied, joined):
            wait(act, joined[s], it)
            act.wait_ge(turned[s], it + 1)
            nc.scalar.copy(eattr_t[:, s, :, :], banks[6][:, :].rearrange("p (q e) -> p q e", e=P)).then_inc(copied[s], 1)

        def slot_after(it, s):
            return (it, 1) if s == 0 else (it + 1, 0)

        def before(it, s):
            return it if s == 0 else it + 1

        def base_of(eng, g):
            return eng.value_load(span_row[0:1, 0, bass.ds(g, 1)], min_val=0, max_val=N - 1)

        def further_windows(eng, g, seen, body, ahead=None):
            windows = eng.value_load(span_row[0:1, 1, bass.ds(g, 1)], min_val=1, max_val=N // WIN + 1)
            with eng.If(windows > 1):
                if ahead is not None:
                    ahead()
                with eng.Fori(1, windows) as w:
                    body(eng.snap(seen, min_val=0, max_val=2 ** 20))
                    eng.reg_add(seen, seen, 1)

        def register(eng, name, value=0):
            reg = eng.alloc_register(name)
            eng.reg_mov(reg, value)
            return reg

        def is_window(out_ap, rel):
            return nc.vector.tensor_tensor(out_ap, iota_w[:, :].unsqueeze(1).to_broadcast([P, T, WIN]),
                                           rel.unsqueeze(2).to_broadcast([P, T, WIN]), ALU.is_equal)

        def group_rel(g):
            return dst_rel[:, bass.ds(g, 1), :].rearrange("p a c -> p (a c)")

        def window_stage(name, table, mlp0):
            width = H if mlp0 else D
            n_acc = 2 if mlp0 else 1
            here, gathered, free, hot, won = (slots(f"{name}_{k}") for k in ("here", "gathered", "free", "hot", "won"))
            s_add, s_xhot, s_xwon = (edge_sem(f"{name}_{k}") for k in ("add", "xhot", "xwon"))
            if mlp0:
                there, turned, copied, joined, summed, ready, hot_b, squared, sq_added = (
                    slots(f"{name}_{k}") for k in ("there", "turned", "copied", "joined", "summed", "ready", "hotb",
                                                   "squared", "sqadded"))
                s_xhot_b = edge_sem(f"{name}_xhotb")
            begun = edge_sem(f"{name}_begun")
            rows = hid if mlp0 else gath
            sums = banks[4]
            with nc.Block() as block:
                @block.sync
                def _(sp):
                    def group(it, s, g):
                        send_indices(sp, it, s, g, src_i, gathered, here)
                        if mlp0:
                            send_attributes(sp, it, s, g, eattr[:, s, :, :], turned, there)
                    both(sp, group, NG // 2 - 1)
                    group(NG // 2 - 1, 0, NG - 2)
                    send_indices(sp, NG // 2 - 1, 1, NG - 1, src_i, gathered, here)
                    if mlp0:
                        send_last_attributes(sp, eattr[:, 1, :, :], acc_mean[0], turned, there)

                @block.gpsimd
                def _(pool):
                    both(pool, lambda it, s, g: gather_rows(pool, it, s, table, width, here, free, gathered, begun))

                @block.scalar
                def _(act):
                    if not mlp0:
                        return
                    seen = register(act, f"{name}_act_seen")

                    def group(it, s, g, final=False):
                        act.wait_ge(hot[s], it + 1)
                        nc.scalar.copy(onehot_b[:, s, :, :], onehot[:, s, :, :]).then_inc(hot_b[s], 1)
                        if not (final and s == 1):
                            copy_attributes(act, *slot_after(it, s), turned, copied, joined)
                        act.wait_ge(ready[s], it + 1)
                        wait(act, sq_added[1 - s], before(it, s))
                        nc.scalar.activation(squares[:, :, :], hid[:, s, :, :], ACT.Square).then_inc(squared[s], 1)

                        def window(k):
                            act.wait_ge(s_xhot, k + 1)
                            nc.scalar.copy(onehot_xb[:, :, :], onehot_x[:, :, :]).then_inc(s_xhot_b, 1)
                        further_windows(act, g, seen, window)
                    copy_attributes(act, 0, 0, turned, copied, joined)
                    both(act, group, NG // 2 - 1)
                    group(NG // 2 - 1, 0, NG - 2, final=True)
                    group(NG // 2 - 1, 1, NG - 1, final=True)

                @block.tensor
                def _(pe):
                    seen = register(pe, f"{name}_pe_seen")

                    def turn(it, s, last=False):
                        pe.wait_ge(there[s], 16 * it + 16 * (N_LAST if last else 1))
                        wait(pe, copied[1 - s], before(it, s))
                        for q in range(T // 2):
                            ins = nc.tensor.transpose(banks[6][:, q * P:(q + 1) * P],
                                                      eattr[:, s, 2 * q:2 * q + 2, :].rearrange("p c f -> p (c f)"),
                                                      ident[:, :])
                        ins.then_inc(turned[s], 1)

                    def join(it, s):
                        pe.wait_ge(copied[s], it + 1)
                        wait(pe, summed[s], it)
                        for q in range(T // 2):
                            ins = nc.tensor.matmul(banks[2 * s + q // 2][:, (q % 2) * 2 * H:(q % 2 + 1) * 2 * H],
                                                   eattr_t[:, s, q, :], w0e[:, :], start=True, stop=True)
                        ins.then_inc(joined[s], 1)

                    def window_sums(s, hots, hots_b):
                        for c in range(T):
                            ins = nc.tensor.matmul(sums[0:width, 0:WIN], rows[:, s, c, 0:width], hots[:, c, :],
                                                   start=(c == 0), stop=(c == T - 1))
                        if mlp0:
                            for c in range(T):
                                ins = nc.tensor.matmul(sums[:, WIN:2 * WIN], ones_b[:, :], hots_b[:, c, :],
                                                       start=(c == 0), stop=(c == T - 1))
                        return ins

                    def group(it, s, g, final=False):
                        if mlp0:
                            if not (final and s == 1):
                                turn(*slot_after(it, s), last=final)
                                join(*slot_after(it, s))
                            pe.wait_ge(hot_b[s], it + 1)
                            pe.wait_ge(ready[s], it + 1)
                        else:
                            pe.wait_ge(hot[s], it + 1)
                            pe.wait_ge(gathered[s], 16 * T * (it + 1))
                        pe.wait_ge(s_add, g + 1)
                        window_sums(s, onehot[:, s, :, :], onehot_b[:, s, :, :]).then_inc(won[s], 1)

                        def window(k):
                            if mlp0:
                                pe.wait_ge(s_xhot_b, k + 1)
                            pe.wait_ge(s_xhot, k + 1)
                            window_sums(s, onehot_x, onehot_xb).then_inc(s_xwon, 1)
                        further_windows(pe, g, seen, window)
                    if mlp0:
                        turn(0, 0)
                        join(0, 0)
                    both(pe, group, NG // 2 - 1)
                    group(NG // 2 - 1, 0, NG - 2, final=True)
                    group(NG // 2 - 1, 1, NG - 1, final=True)

                @block.vector
                def _(dve):
                    seen = register(dve, f"{name}_dve_seen")
                    start = register(dve, f"{name}_dve_start")
                    if mlp0:
                        nc.vector.memset(sq_sum[:, :, :], 0.0)
                        nc.vector.memset(acc[:, :, :], 0.0).then_inc(s_add, 1)
                    elif name != "conv2":
                        nc.vector.memset(acc[D:D + 1, 0, :], 1.0)
                        nc.vector.memset(acc[0:D, 0, :], 0.0).then_inc(s_add, 1)
                    else:
                        nc.vector.memset(acc[0:D, 0, NP:NA], 0.0).then_inc(s_add, 1)

                    def add_window(first):
                        at = acc[0:width, 0:n_acc, bass.ds(first, WIN)]
                        return nc.vector.tensor_tensor(at, at, sums[0:width, 0:n_acc * WIN].rearrange(
                            "p (a n) -> p a n", a=n_acc), ALU.add)

                    def group(it, s, g):
                        wait(dve, won[s], it)
                        is_window(onehot[:, s, :, :], group_rel(g)).then_inc(hot[s], 1)
                        if mlp0:
                            dve.wait_ge(joined[s], it + 1)
                            dve.wait_ge(gathered[s], 16 * T * (it + 1))
                            for q in range(2):
                                ins = nc.vector.tensor_tensor(
                                    hid[:, s, 4 * q:4 * q + 4, :],
                                    banks[2 * s + q][:, :].rearrange("p (c f) -> p c f", f=H),
                                    gath[:, s, 4 * q:4 * q + 4, :], ALU.add)
                            ins.then_inc(summed[s], 1)
                            dve.wait_ge(summed[s], it + 1)
                            nc.vector.scalar_tensor_tensor(out=hid[:, s, :, :], in0=hid[:, s, :, :], scalar=SLOPE,
                                                           in1=hid[:, s, :, :], op0=ALU.mult,
                                                           op1=ALU.max).then_inc(ready[s], 1)
                            dve.wait_ge(squared[s], it + 1)
                            nc.vector.tensor_tensor(sq_sum[:, :, :], sq_sum[:, :, :], squares[:, :, :],
                                                    ALU.add).then_inc(sq_added[s], 1)
                        base = base_of(dve, g)
                        dve.wait_ge(won[s], it + 1)
                        dve.wait_ge(s_add, g + 1)
                        add_window(base).then_inc(s_add, 1)
                        dve.reg_mov(start, base)

                        def second():
                            dve.drain()
                            nc.vector.tensor_scalar(drel[:, :], group_rel(g), float(WIN), None, ALU.subtract)

                        def window(k):
                            dve.drain()
                            is_window(onehot_x[:, :, :], drel[:, :]).then_inc(s_xhot, 1)
                            dve.reg_add(start, start, WIN)
                            dve.wait_ge(s_xwon, k + 1)
                            nc.vector.tensor_scalar(drel[:, :], drel[:, :], float(WIN), None, ALU.subtract)
                            add_window(dve.snap(start, min_val=0, max_val=NA - WIN))
                            dve.drain()
                        further_windows(dve, g, seen, window, ahead=second)
                        dve.sem_inc(free[s], 1)
                    both(dve, group)

        def add_rows(pool, it, s, accs, width, index, addable, added, begun):
            now = pool.snap(it + 1)
            before_now = pool.snap(16 * (T // 2) * before(it, s))
            pool.wait_ge(index[s], now)
            pool.wait_ge(addable[s], now)
            for h in range(2):
                wait(pool, added[1 - s][h], before_now)
                pool.sem_inc(begun, 1)
                for c in range(h * T // 2, (h + 1) * T // 2):
                    pool.indirect_dma_start(accs[c][:, :], bass.IndirectOffsetOnAxis(
                        ap=idx_s[:, s, c:c + 1].bitcast(U32), axis=0), addend[:, s, c, 0:width], None,
                        bounds_check=NA - 1, compute_op=ALU.add).then_inc(added[s][h], 16)

        def slot_added(eng, it, s, added):
            for h in range(2):
                wait(eng, added[s][h], 16 * (T // 2) * it)

        def all_added(pool, added):
            for s in range(2):
                for h in range(2):
                    pool.wait_ge(added[s][h], 16 * (T // 2) * (NG // 2))

        def spread_src(pe, it, s, row_in, equal, spread):
            pe.wait_ge(row_in[s], it + 1)
            wait(pe, equal[1 - s], before(it, s))
            for c in range(T):
                ins = nc.tensor.transpose(banks[c // 4][:, (c % 4) * P:(c % 4 + 1) * P],
                                          src_s[:, s, c:c + 1].to_broadcast([P, P]), ident[:, :])
            ins.then_inc(spread[s], 1)

        def equal_src(s, out):
            for q in range(2):
                ins = nc.vector.tensor_tensor(out[:, 4 * q:4 * q + 4, :],
                                              banks[q][:, :].rearrange("p (c e) -> p c e", c=4),
                                              src_s[:, s, 4 * q:4 * q + 4].unsqueeze(2).to_broadcast([P, 4, P]),
                                              ALU.is_equal)
            return ins

        def take_src(act, s, g, row_in):
            nc.scalar.copy(src_s[:, s, :], src_f[:, bass.ds(g, 1), :].rearrange("p a c -> p (a c)")).then_inc(row_in[s], 1)

        def window_rows(sp, table, width, at, first):
            return sp.dma_start(at, table[bass.ds(first, WIN), 0:width])

        def gin_stage():
            width = D + 1
            there, row_in, spread, equal, crossed, counted, totalled, addable, index, used = (
                slots(f"gin_{k}") for k in ("there", "rowin", "spread", "equal", "crossed", "counted", "totalled",
                                            "addable", "index", "used"))
            added = [slots(f"gin_added{s}") for s in range(2)]
            s_dup, s_xthere, s_xhot, s_xcross, s_xcount, s_xdone, begun = (
                edge_sem(f"gin_{k}") for k in ("dup", "xthere", "xhot", "xcross", "xcount", "xdone", "begun"))
            cross, xcross, totals = banks[2:4], banks[6:8], banks[4:6]
            counts = [squares[0:WIN, :, :], sq_sum[0:WIN, :, :]]
            counts_x = gath[0:WIN, 0, :, :]
            with nc.Block() as block:
                @block.sync
                def _(sp):
                    seen, start = register(sp, "gin_sp_seen"), register(sp, "gin_sp_start")

                    def group(it, s, g):
                        base = base_of(sp, g)
                        wait(sp, totalled[s], it)
                        window_rows(sp, tab_gin, width, win_x[0:WIN, s, :], base).then_inc(there[s], 16)
                        sp.reg_mov(start, base)

                        def window(k):
                            sp.reg_add(start, start, WIN)
                            sp.wait_ge(s_xdone, k + 1)
                            window_rows(sp, tab_gin, width, win_x[0:WIN, 2, :],
                                        sp.snap(start, min_val=0, max_val=NA - WIN)).then_inc(s_xthere, 16)
                        further_windows(sp, g, seen, window)
                    both(sp, group)

                @block.gpsimd
                def _(pool):
                    both(pool, lambda it, s, g: add_rows(pool, it, s, acc_gin, width, index, addable, added, begun))
                    all_added(pool, added)

                @block.scalar
                def _(act):
                    seen = register(act, "gin_act_seen")

                    def copy_counts(out, cross_banks):
                        for q in range(2):
                            ins = nc.scalar.copy(out[:, 4 * q:4 * q + 4, :],
                                                 cross_banks[q][0:WIN, :].rearrange("p (c e) -> p c e", c=4))
                        return ins

                    def group(it, s, g, final=False):
                        act.wait_ge(crossed[s], it + 1)
                        wait(act, totalled[s], it)
                        copy_counts(counts[s], cross).then_inc(counted[s], 1)

                        def window(k):
                            act.wait_ge(s_xcross, k + 1)
                            copy_counts(counts_x, xcross).then_inc(s_xcount, 1)
                        further_windows(act, g, seen, window)
                        act.wait_ge(totalled[s], it + 1)
                        slot_added(act, it, s, added)
                        for q in range(2):
                            ins = nc.scalar.copy(addend[:, s, 4 * q:4 * q + 4, 0:width],
                                                 totals[q][:, 0:4 * width].rearrange("p (c f) -> p c f", c=4))
                        ins.then_inc(addable[s], 1)
                        if not final:
                            act.wait_ge(used[s], it + 1)
                            take_src(act, s, g + 2, row_in)
                    take_src(act, 0, 0, row_in)
                    take_src(act, 1, 1, row_in)
                    both(act, group, NG // 2 - 1)
                    group(NG // 2 - 1, 0, NG - 2, final=True)
                    group(NG // 2 - 1, 1, NG - 1, final=True)

                @block.tensor
                def _(pe):
                    seen = register(pe, "gin_pe_seen")

                    def cross_product(out, hots, s):
                        for c in range(T):
                            ins = nc.tensor.matmul(out[c // 4][0:WIN, (c % 4) * P:(c % 4 + 1) * P], hots[:, c, :],
                                                   same[:, s, c, :], start=True, stop=True)
                        return ins

                    def total(out_counts, rows, first):
                        for c in range(T):
                            nc.tensor.matmul(totals[c // 4][:, (c % 4) * width:(c % 4 + 1) * width], out_counts[:, c, :],
                                             rows, start=first and c % 4 == 0, stop=True, skip_group_check=True)

                    def group(it, s, g, final=False):
                        pe.wait_ge(equal[s], it + 1)
                        wait(pe, counted[1 - s], before(it, s))
                        cross_product(cross, onehot_b[:, s, :, :], s).then_inc(crossed[s], 1)
                        if not (final and s == 1):
                            spread_src(pe, *slot_after(it, s), row_in, equal, spread)
                        pe.wait_ge(counted[s], it + 1)
                        pe.wait_ge(there[s], 16 * (it + 1))
                        wait(pe, addable[1 - s], before(it, s))
                        total(counts[s], win_x[0:WIN, s, :], True)

                        def window(k):
                            pe.wait_ge(s_xhot, k + 1)
                            cross_product(xcross, onehot_xb, s).then_inc(s_xcross, 1)
                            pe.wait_ge(s_xcount, k + 1)
                            pe.wait_ge(s_xthere, 16 * (k + 1))
                            total(counts_x, win_x[0:WIN, 2, :], False)
                            nc.tensor.matmul(totals[1][:, 0:1], zero_b[:, :], zero_b[:, 0:1], start=False, stop=True,
                                             skip_group_check=True).then_inc(s_xdone, 1)
                        further_windows(pe, g, seen, window)
                        nc.tensor.matmul(totals[1][:, 0:1], zero_b[:, :], zero_b[:, 0:1], start=False, stop=True,
                                         skip_group_check=True).then_inc(totalled[s], 1)
                    pe.sem_inc(s_xdone, 1)
                    spread_src(pe, 0, 0, row_in, equal, spread)
                    both(pe, group, NG // 2 - 1)
                    group(NG // 2 - 1, 0, NG - 2, final=True)
                    group(NG // 2 - 1, 1, NG - 1, final=True)

                @block.vector
                def _(dve):
                    seen = register(dve, "gin_dve_seen")

                    def group(it, s, g):
                        wait(dve, crossed[s], it)
                        is_window(onehot_b[:, s, :, :], group_rel(g))
                        dve.wait_ge(spread[s], it + 1)
                        equal_src(s, same[:, s, :, :]).then_inc(equal[s], 1)
                        dve.wait_ge(equal[s], it + 1)
                        nc.vector.tensor_tensor(earlier[:, :, :], same[:, s, :, :],
                                                lower_b[:, :].unsqueeze(1).to_broadcast([P, T, P]),
                                                ALU.mult).then_inc(s_dup, 1)
                        dve.wait_ge(s_dup, g * 4 + 1)
                        nc.vector.tensor_reduce(dup[:, 0, :], earlier[:, :, :], AX.X, ALU.max).then_inc(s_dup, 1)
                        nc.vector.tensor_scalar(dup[:, 1, :], src_s[:, s, :], -1.0, trash[:, 0:1], ALU.mult,
                                                ALU.add).then_inc(s_dup, 1)
                        dve.wait_ge(s_dup, g * 4 + 3)
                        nc.vector.tensor_tensor(dup[:, 0, :], dup[:, 0, :], dup[:, 1, :], ALU.mult).then_inc(s_dup, 1)
                        dve.wait_ge(s_dup, g * 4 + 4)
                        nc.vector.tensor_tensor(scat_i[:, bass.ds(g, 1), :].rearrange("p a c -> p (a c)"),
                                                dup[:, 0, :], src_s[:, s, :], ALU.add)
                        slot_added(dve, it, s, added)
                        nc.vector.tensor_tensor(idx_s[:, s, :], dup[:, 0, :], src_s[:, s, :], ALU.add).then_inc(index[s], 1)
                        dve.wait_ge(index[s], it + 1)
                        dve.sem_inc(used[s], 1)

                        def second():
                            dve.drain()
                            nc.vector.tensor_scalar(drel[:, :], group_rel(g), float(WIN), None, ALU.subtract)

                        def window(k):
                            dve.drain()
                            dve.wait_ge(s_xdone, k + 1)
                            is_window(onehot_xb[:, :, :], drel[:, :]).then_inc(s_xhot, 1)
                            dve.drain()
                            nc.vector.tensor_scalar(drel[:, :], drel[:, :], float(WIN), None, ALU.subtract)
                        further_windows(dve, g, seen, window, ahead=second)
                    both(dve, group)

        def mean_stage():
            there, rel_in, xrow, turned, filled, filled_o, mixed, relued, back, ready = (
                slots(f"mean_{k}") for k in ("there", "relin", "xrow", "turned", "filled", "filledo", "mixed", "relued",
                                             "back", "ready"))
            row_in, spread, equal, totalled, addable, index = (
                slots(f"mean_{k}") for k in ("rowin", "spread", "equal", "totalled", "addable", "index"))
            added = [slots(f"mean_added{s}") for s in range(2)]
            s_xthere, s_xhot, s_xdone, begun, s_pbegun = (
                edge_sem(f"mean_{k}") for k in ("xthere", "xhot", "xdone", "begun", "pbegun"))
            turn_b, mix_b, back_b, total_b = banks[2:4], banks[4:6], banks[6], banks[7]
            both_in = gath
            mixer = hid
            same32 = [acc[:, q, 0:T * P].rearrange("p (c e) -> p c e", e=P) for q in range(2)]
            relu_t = [acc[0:D, q, T * P:2 * T * P].rearrange("p (c e) -> p c e", e=P) for q in range(2)]
            rows = eattr
            mixer_x = squares
            with nc.Block() as block:
                @block.sync
                def _(sp):
                    seen, start = register(sp, "mean_sp_seen"), register(sp, "mean_sp_start")

                    def group(it, s, g, final=False):
                        at = both_in[:, s, :, 0:D]
                        if final and s == 1:
                            send_last_attributes(sp, at, tab_pre3, turned, there)
                        else:
                            send_attributes(sp, it, s, g, at, turned, there)
                        base = base_of(sp, g)
                        wait(sp, mixed[s], it)
                        window_rows(sp, tab_pre3, D, lhs3[D:P, s, :], base).then_inc(xrow[s], 16)
                        sp.reg_mov(start, base)

                        def window(k):
                            sp.reg_add(start, start, WIN)
                            sp.wait_ge(s_xdone, k + 1)
                            window_rows(sp, tab_pre3, D, lhs3[D:P, 2, :],
                                        sp.snap(start, min_val=0, max_val=NA - WIN)).then_inc(s_xthere, 16)
                        further_windows(sp, g, seen, window)
                    both(sp, group, NG // 2 - 1)
                    group(NG // 2 - 1, 0, NG - 2, final=True)
                    group(NG // 2 - 1, 1, NG - 1, final=True)

                @block.gpsimd
                def _(pool):
                    both(pool, lambda it, s, g: add_rows(pool, it, s, acc_mean, D, index, addable, added, begun))
                    all_added(pool, added)

                @block.scalar
                def _(act):
                    def take_rel(it, s, g):
                        wait(act, turned[s], it)
                        nc.scalar.copy(both_in[:, s, :, D:2 * D],
                                       group_rel(g).unsqueeze(2).to_broadcast([P, T, D])).then_inc(rel_in[s], 1)

                    def fill(it, s):
                        act.wait_ge(turned[s], it + 1)
                        wait(act, mixed[s], it)
                        for q in range(2):
                            ins = nc.scalar.copy(mixer[0:D, s, 4 * q:4 * q + 4, :],
                                                 turn_b[q][0:D, :].rearrange("p (c e) -> p c e", c=4))
                        ins.then_inc(filled[s], 1)

                    def group(it, s, g, final=False):
                        if not final:
                            take_rel(it + 1, s, g + 2)
                        act.wait_ge(mixed[s], it + 1)
                        wait(act, back[s], it)
                        for q in range(2):
                            ins = nc.scalar.activation(relu_t[s][:, 4 * q:4 * q + 4, :],
                                                       mix_b[q][0:D, :].rearrange("p (c e) -> p c e", c=4), ACT.Relu)
                        ins.then_inc(relued[s], 1)
                        if not (final and s == 1):
                            fill(*slot_after(it, s))
                        act.wait_ge(back[s], it + 1)
                        wait(act, totalled[s], it)
                        nc.scalar.copy(rows[:, s, :, :], back_b[:, :].rearrange("p (c f) -> p c f", f=D)).then_inc(ready[s], 1)
                        act.wait_ge(totalled[s], it + 1)
                        slot_added(act, it, s, added)
                        nc.scalar.copy(addend[:, s, :, 0:D], total_b[:, :].rearrange(
                            "p (c f) -> p c f", f=D)).then_inc(addable[s], 1)
                        if not final:
                            take_src(act, s, g + 2, row_in)
                    for s in range(2):
                        take_src(act, s, s, row_in)
                        take_rel(0, s, s)
                    fill(0, 0)
                    both(act, group, NG // 2 - 1)
                    group(NG // 2 - 1, 0, NG - 2, final=True)
                    group(NG // 2 - 1, 1, NG - 1, final=True)

                @block.tensor
                def _(pe):
                    seen = register(pe, "mean_pe_seen")

                    def turn(it, s, last=False):
                        pe.wait_ge(there[s], 16 * it + 16 * (N_LAST if last else 1))
                        pe.wait_ge(rel_in[s], it + 1)
                        wait(pe, filled[1 - s], before(it, s))
                        wait(pe, filled_o[1 - s], before(it, s))
                        for c in range(T):
                            ins = nc.tensor.transpose(turn_b[c // 4][:, (c % 4) * P:(c % 4 + 1) * P],
                                                      both_in[:, s, c, :], ident[:, :])
                        ins.then_inc(turned[s], 1)

                    def mix(lhs, rhs, first):
                        for q in range(2):
                            nc.tensor.matmul(mix_b[q][0:D, :], lhs,
                                             rhs[:, 4 * q:4 * q + 4, :].rearrange("p c e -> p (c e)"),
                                             start=first, stop=True, skip_group_check=True)

                    def group(it, s, g, final=False):
                        pe.wait_ge(filled[s], it + 1)
                        pe.wait_ge(filled_o[s], it + 1)
                        pe.wait_ge(xrow[s], 16 * (it + 1))
                        wait(pe, relued[1 - s], before(it, s))
                        mix(lhs3[:, s, :], mixer[:, s, :, :], True)

                        def window(k):
                            pe.wait_ge(s_xhot, k + 1)
                            pe.wait_ge(s_xthere, 16 * (k + 1))
                            mix(lhs3[:, 2, :], mixer_x[:, :, :], False)
                            nc.tensor.matmul(mix_b[1][0:D, 0:1], zero_b[:, 0:D], zero_b[:, 0:1], start=False, stop=True,
                                             skip_group_check=True).then_inc(s_xdone, 1)
                        further_windows(pe, g, seen, window)
                        nc.tensor.matmul(mix_b[1][0:D, 0:1], zero_b[:, 0:D], zero_b[:, 0:1], start=False, stop=True,
                                         skip_group_check=True).then_inc(mixed[s], 1)
                        if not (final and s == 1):
                            turn(*slot_after(it, s), last=final)
                        pe.wait_ge(relued[s], it + 1)
                        wait(pe, ready[1 - s], before(it, s))
                        pe.sem_inc(s_pbegun, 1)
                        for c in range(T):
                            ins = nc.tensor.transpose(back_b[:, c * D:(c + 1) * D], relu_t[s][:, c, :], ident[0:D, 0:D])
                        ins.then_inc(back[s], 1)
                        if not (final and s == 1):
                            spread_src(pe, *slot_after(it, s), row_in, equal, spread)
                        pe.wait_ge(ready[s], it + 1)
                        pe.wait_ge(equal[s], it + 1)
                        wait(pe, addable[1 - s], before(it, s))
                        for c in range(T):
                            ins = nc.tensor.matmul(total_b[:, c * D:(c + 1) * D], same32[s][:, c, :], rows[:, s, c, :],
                                                   start=True, stop=True)
                        ins.then_inc(totalled[s], 1)
                    pe.sem_inc(s_xdone, 1)
                    turn(0, 0)
                    spread_src(pe, 0, 0, row_in, equal, spread)
                    both(pe, group, NG // 2 - 1)
                    group(NG // 2 - 1, 0, NG - 2, final=True)
                    group(NG // 2 - 1, 1, NG - 1, final=True)

                @block.vector
                def _(dve):
                    seen = register(dve, "mean_dve_seen")

                    def fill_o(out, wcol):
                        for q in range(2):
                            ins = nc.vector.tensor_scalar(out[:, 4 * q:4 * q + 4, :],
                                                          turn_b[q][D:P, :].rearrange("p (c e) -> p c e", c=4),
                                                          wnode[D:P, wcol:wcol + 1], None, ALU.is_equal)
                        return ins

                    def group(it, s, g):
                        dve.wait_ge(turned[s], it + 1)
                        wait(dve, mixed[s], it)
                        fill_o(mixer[D:P, s, :, :], 0).then_inc(filled_o[s], 1)

                        def second():
                            dve.drain()
                            nc.vector.tensor_scalar(wnode[:, 1:2], wnode[:, 0:1], float(WIN), None, ALU.add)

                        def window(k):
                            dve.drain()
                            dve.wait_ge(s_xdone, k + 1)
                            fill_o(mixer_x[D:P, :, :], 1).then_inc(s_xhot, 1)
                            dve.drain()
                            nc.vector.tensor_scalar(wnode[:, 1:2], wnode[:, 1:2], float(WIN), None, ALU.add)
                        further_windows(dve, g, seen, window, ahead=second)
                        dve.wait_ge(spread[s], it + 1)
                        wait(dve, totalled[s], it)
                        equal_src(s, same32[s]).then_inc(equal[s], 1)
                        slot_added(dve, it, s, added)
                        nc.vector.tensor_copy(idx_s[:, s, :], scat_i[:, bass.ds(g, 1), :].rearrange(
                            "p a c -> p (a c)")).then_inc(index[s], 1)
                    nc.vector.memset(mixer_x[0:D, :, :], 0.0)
                    both(dve, group)

        def node_products(pe, lhs_t, rhs, s_m, s_a, first=0):
            for q in range(NCH):
                if q >= 2:
                    pe.wait_ge(s_a, q - 1)
                for k in range(CH):
                    b = CH * q + k
                    ins = nc.tensor.matmul(banks[first + q % 2][:, k * D:(k + 1) * D], lhs_t[:, b * P:(b + 1) * P], rhs,
                                           start=True, stop=True)
                ins.then_inc(s_m, 1)

        def chunk(q, first=0):
            return banks[first + q % 2][:, 0:CH * D].rearrange("p (b f) -> p b f", f=D), slice(CH * q, CH * (q + 1))

        def over_nodes(row):
            return row.unsqueeze(1).to_broadcast([P, CH, D])

        def add_accumulators(sp_or_dve, accs, width, s_ld, s_sm, load):
            size = NB * width
            part = lambda c: acc[:, c % 4 // 2, (c % 2) * (NA // 2):(c % 2) * (NA // 2) + size].rearrange(
                "p (b f) -> p b f", f=width)
            y = node_y[:, :, 0:width]
            if load:
                for c in range(T):
                    if c >= 4:
                        sp_or_dve.wait_ge(s_sm, c - 3)
                    sp_or_dve.dma_start(part(c), node_rows(accs[c][0:NP, :])).then_inc(s_ld[c], 16)
                return
            for c in range(T):
                sp_or_dve.wait_ge(s_ld[c], 16)
                if c == 0:
                    nc.vector.tensor_copy(y, part(0)).then_inc(s_sm, 1)
                else:
                    sp_or_dve.wait_ge(s_sm, c)
                    nc.vector.tensor_tensor(y, y, part(c), ALU.add).then_inc(s_sm, 1)
            sp_or_dve.wait_ge(s_sm, T)

        window_stage("mlp0", tab_pre0, mlp0=True)

        C = lambda i: col[:, i:i + 1]
        s_c, s_sq, s_rt, s_scaled, s_a1, s_st, s_b1, s_lk, s_lk2, s_ms, s_sqs, s_norm, s_m3, s_e3, s_dg, s_dgr, s_di, \
            s_y, s_var, s_std, s_wr, s_gd = (sem(f"bn_{k}") for k in (
                "c sq rt scaled a1 st b1 lk lk2 ms sqs norm m3 e3 dg dgr di y var std wr gd").split())
        with nc.Block() as block:
            @block.tensor
            def _(pe):
                for b in range(NB):
                    ins = nc.tensor.matmul(banks[7][:, b:b + 1], acc[0:1, 1, b * P:(b + 1) * P], ones[0:1, 0:1],
                                           start=True, stop=True)
                ins.then_inc(s_dg, 1)
                for c in range(T):
                    ins = nc.tensor.matmul(banks[6][:, 0:1], sq_sum[:, c, :], ones[:, 0:1], start=(c == 0),
                                           stop=(c == T - 1))
                ins.then_inc(s_gd, 1)
                pe.wait_ge(s_scaled, 1)
                for j in range(2 * NCH):
                    cols = slice(j * CW, (j + 1) * CW)
                    if j >= 2:
                        pe.wait_ge(s_st, j - 1)
                    nc.tensor.matmul(banks[j % 2][:, 0:CW], w0b[:, :], acc[:, 0, cols], start=True,
                                     stop=True).then_inc(s_a1, 1)
                    pe.wait_ge(s_st, j + 1)
                    if j >= 2:
                        pe.wait_ge(s_lk, j - 1)
                    nc.tensor.matmul(banks[2 + j % 2][:, 0:CW], w0cx[:, :], nodes_t[0:D, cols], start=True, stop=False)
                    nc.tensor.matmul(banks[2 + j % 2][:, 0:CW], w0ca[:, :], stage[:, j % 2, :], start=False,
                                     stop=True).then_inc(s_b1, 1)
                pe.wait_ge(s_norm, 1)
                node_products(pe, acc[:, 0, :], w0d[:, :], s_m3, s_e3)

            @block.scalar
            def _(act):
                act.wait_ge(s_sq, 1)
                nc.scalar.activation(C(S1), C(V1), ACT.Sqrt).then_inc(s_rt, 1)
                act.wait_ge(s_dgr, 1)
                nc.scalar.activation(dinv[:, :], ln[:, 0, :], ACT.Sqrt).then_inc(s_di, 1)
                for j in range(2 * NCH):
                    act.wait_ge(s_b1, j + 1)
                    nc.scalar.activation(acc[:, 0, j * CW:(j + 1) * CW], banks[2 + j % 2][:, 0:CW], ACT.Identity,
                                         bias=C(B3)).then_inc(s_lk, 1)
                act.wait_ge(s_ms, 1)
                nc.scalar.activation(acc[:, 1, 0:N], acc[:, 0, 0:N], ACT.Square, bias=C(NM2),
                                     accum_out=C(Q1)).then_inc(s_sqs, 1)
                act.wait_ge(s_sq, 2)
                nc.scalar.activation(C(S1), C(V2), ACT.Sqrt).then_inc(s_rt, 1)
                layer_norm_root(act, s_var, s_std)

            @block.vector
            def _(dve):
                step = stepper(dve, "bn_chain")
                step(nc.vector.tensor_reduce(C(M1), acc[:, 0, 0:N], AX.X, ALU.add))
                step(nc.vector.tensor_scalar(C(M1), C(M1), 1.0 / E, None, ALU.mult))
                step(nc.vector.tensor_tensor(C(Q1), C(M1), C(M1), ALU.mult))
                dve.wait_ge(s_gd, 1)
                step(nc.vector.tensor_scalar(C(V1), banks[6][:, 0:1], 1.0 / E, None, ALU.mult))
                step(nc.vector.tensor_tensor(C(V1), C(V1), C(Q1), ALU.subtract))
                step(nc.vector.tensor_scalar(C(V1), C(V1), 0.0, EPS, ALU.max, ALU.add))
                dve.sem_inc(s_sq, 1)
                dve.wait_ge(s_rt, 1)
                step(nc.vector.reciprocal(C(SC1), C(S1)))
                step(nc.vector.tensor_tensor(C(SC1), C(SC1), C(GB1), ALU.mult))
                step(nc.vector.tensor_tensor(C(SH1), C(M1), C(SC1), ALU.mult))
                step(nc.vector.tensor_tensor(C(SH1), C(GBE1), C(SH1), ALU.subtract))
                step(nc.vector.tensor_scalar(acc[:, 0, 0:NP], acc[:, 0, 0:NP], C(SC1), None, ALU.mult))
                nc.vector.scalar_tensor_tensor(out=acc[:, 0, 0:NP], in0=acc[:, 1, 0:NP], scalar=C(SH1),
                                               in1=acc[:, 0, 0:NP], op0=ALU.mult, op1=ALU.add).then_inc(s_scaled, 1)
                dve.wait_ge(s_dg, 1)
                step(nc.vector.tensor_scalar(ln[:, 0, :], banks[7][:, 0:NB], 1.0, None, ALU.add))
                dve.sem_inc(s_dgr, 1)
                for j in range(2 * NCH):
                    dve.wait_ge(s_a1, j + 1)
                    if j >= 2:
                        dve.wait_ge(s_b1, j - 1)
                    nc.vector.scalar_tensor_tensor(out=stage[:, j % 2, :], in0=acc[:, 1, j * CW:(j + 1) * CW],
                                                   scalar=C(B2), in1=banks[j % 2][:, 0:CW], op0=ALU.mult,
                                                   op1=ALU.add).then_inc(s_st, 1)
                dve.wait_ge(s_di, 1)
                step(nc.vector.reciprocal(dinv[:, :], dinv[:, :]))
                dve.wait_ge(s_lk, 2 * NCH)
                step(nc.vector.scalar_tensor_tensor(out=acc[:, 0, 0:NP], in0=acc[:, 0, 0:NP], scalar=SLOPE,
                                                    in1=acc[:, 0, 0:NP], op0=ALU.mult, op1=ALU.max))
                step(nc.vector.tensor_reduce(C(M2), acc[:, 0, 0:N], AX.X, ALU.add))
                step(nc.vector.tensor_scalar(C(M2), C(M2), 1.0 / N, None, ALU.mult))
                nc.vector.tensor_scalar(C(NM2), C(M2), -1.0, None, ALU.mult).then_inc(s_ms, 1)
                dve.wait_ge(s_sqs, 1)
                nc.vector.tensor_scalar(C(V2), C(Q1), 1.0 / N, EPS, ALU.mult, ALU.add).then_inc(s_sq, 1)
                dve.wait_ge(s_rt, 2)
                step(nc.vector.reciprocal(C(SC2), C(S1)))
                step(nc.vector.tensor_tensor(C(SC2), C(SC2), C(G2), ALU.mult))
                step(nc.vector.tensor_tensor(C(SH2), C(M2), C(SC2), ALU.mult))
                step(nc.vector.tensor_tensor(C(SH2), C(BE2), C(SH2), ALU.subtract))
                nc.vector.tensor_scalar(acc[:, 0, 0:NP], acc[:, 0, 0:NP], C(SC2), C(SH2), ALU.mult,
                                        ALU.add).then_inc(s_norm, 1)
                for q in range(NCH):
                    dve.wait_ge(s_m3, q + 1)
                    got, bl = chunk(q)
                    nc.vector.tensor_tensor(node_y[:, bl, 0:D], got, over_nodes(bc[:, 1, 0:D]), ALU.add).then_inc(s_e3, 1)
                dve.wait_ge(s_e3, NCH)
                y = node_y[:, :, 0:D]
                step(nc.vector.tensor_tensor(y, y, node_x[:, :, :], ALU.add))
                layer_norm(dve, (step, s_var, s_std), y)
                dve.sem_inc(s_y, 1)

            @block.sync
            def _(sp):
                sp.wait_ge(s_y, 1)
                sp.dma_start(node_rows(tab[0]), node_x[:, :, :]).then_inc(s_wr, 16)
                sp.wait_ge(s_wr, 16)

            @block.gpsimd
            def _(pool):
                retire(pool)

        window_stage("conv1", tab[0], mlp0=False)
        s_m, s_r, s_x, s_y, s_tr, s_ev, s_wr = (sem(f"c1_{k}") for k in "m r x y tr ev wr".split())
        with nc.Block() as block:
            @block.tensor
            def _(pe):
                node_products(pe, acc[0:D + 1, 0, :], wc[:, 0, :], s_m, s_r)
                pe.wait_ge(s_y, 1)
                pe.wait_ge(s_r, NCH)
                to_features(pe, acc[:, 0, :], node_y, D, s_tr, s_ev)

            @block.scalar
            def _(act):
                for q in range(NCH):
                    act.wait_ge(s_m, q + 1)
                    got, bl = chunk(q)
                    nc.scalar.activation(node_y[:, bl, 0:D], got, ACT.Relu).then_inc(s_r, 1)
                to_features_copy(act, acc[:, 0, :], D, s_tr, s_ev)

            @block.vector
            def _(dve):
                dve.wait_ge(s_r, NCH)
                nc.vector.tensor_tensor(node_y[:, :, 0:D], node_y[:, :, 0:D],
                                        dinv[:, :].unsqueeze(2).to_broadcast([P, NB, D]), ALU.mult).then_inc(s_y, 1)

            @block.sync
            def _(sp):
                sp.wait_ge(s_y, 1)
                sp.dma_start(node_rows(tab[1]), node_y[:, :, 0:D]).then_inc(s_wr, 16)
                sp.wait_ge(s_wr, 16)

            @block.gpsimd
            def _(pool):
                retire(pool)

        window_stage("conv2", tab[1], mlp0=False)
        s_m2, s_r2, s_y2, s_wr2 = (sem(f"c2_{k}") for k in "m r y wr".split())
        with nc.Block() as block:
            @block.tensor
            def _(pe):
                node_products(pe, acc[0:D, 0, :], wc[0:D, 1, :], s_m2, s_r2)

            @block.vector
            def _(dve):
                step = stepper(dve, "c2_chain")
                for q in range(NCH):
                    dve.wait_ge(s_m2, q + 1)
                    got, bl = chunk(q)
                    nc.vector.tensor_tensor(node_y[:, bl, 0:D], got, dinv[:, bl].unsqueeze(2).to_broadcast([P, CH, D]),
                                            ALU.mult).then_inc(s_r2, 1)
                dve.wait_ge(s_r2, NCH)
                y = node_y[:, :, 0:D]
                step(nc.vector.tensor_tensor(y, y, bc[:, 2, 0:D].unsqueeze(1).to_broadcast([P, NB, D]), ALU.add))
                nc.vector.tensor_scalar(y, y, 0.0, None, ALU.max).then_inc(s_y2, 1)

            @block.sync
            def _(sp):
                sp.wait_ge(s_y2, 1)
                sp.dma_start(node_rows(tab[2]), node_y[:, :, 0:D]).then_inc(s_wr2, 16)
                sp.wait_ge(s_wr2, 16)

            @block.gpsimd
            def _(pool):
                retire(pool)

        window_stage("conv3", tab[2], mlp0=False)
        s_m4, s_r4, s_y4, s_var4, s_std4, s_wr4 = (sem(f"c3_{k}") for k in "m r y var std wr".split())
        with nc.Block() as block:
            @block.tensor
            def _(pe):
                node_products(pe, acc[0:D + 1, 0, :], wc[:, 2, :], s_m4, s_r4)

            @block.scalar
            def _(act):
                layer_norm_root(act, s_var4, s_std4)

            @block.vector
            def _(dve):
                step = stepper(dve, "c3_chain")
                for q in range(NCH):
                    dve.wait_ge(s_m4, q + 1)
                    got, bl = chunk(q)
                    nc.vector.tensor_tensor(node_y[:, bl, 0:D], got, node_x[:, bl, :], ALU.add).then_inc(s_r4, 1)
                dve.wait_ge(s_r4, NCH)
                layer_norm(dve, (step, s_var4, s_std4), node_y[:, :, 0:D])
                step(nc.vector.tensor_copy(node_y[:, :, 0:D], node_x[:, :, :]))
                nc.vector.memset(node_y[:, :, D:D + 1], 1.0).then_inc(s_y4, 1)

            @block.sync
            def _(sp):
                sp.wait_ge(s_y4, 1)
                sp.dma_start(node_rows(tab_gin[0:NP, :]), node_y[:, :, :]).then_inc(s_wr4, 16)
                sp.wait_ge(s_wr4, 16)

            @block.gpsimd
            def _(pool):
                retire(pool)

        gin_stage()
        s_ld5 = [sem(f"g_ld{c}") for c in range(T)]
        s_sm5, s_in5, s_tr5, s_ev5, s_a5, s_h5, s_m5, s_r5, s_var5, s_std5, s_x5, s_tr6, s_ev6, s_m6, s_r6, s_wr5 = (
            sem(f"g_{k}") for k in "sm in tr ev a h m r var std x tr6 ev6 m6 r6 wr".split())
        with nc.Block() as block:
            @block.sync
            def _(sp):
                add_accumulators(sp, acc_gin, D + 1, s_ld5, s_sm5, load=True)
                sp.wait_ge(s_r6, NCH)
                sp.dma_start(node_rows(tab_pre3[0:NP, :]), node_y[:, :, 0:D]).then_inc(s_wr5, 16)
                sp.wait_ge(s_wr5, 16)

            @block.tensor
            def _(pe):
                pe.wait_ge(s_in5, 1)
                to_features(pe, nodes_t, node_y, D, s_tr5, s_ev5)
                pe.wait_ge(s_ev5, (NB + 3) // 4)
                for j in range(2 * NCH):
                    if j >= 2:
                        pe.wait_ge(s_h5, j - 1)
                    nc.tensor.matmul(banks[2 + j % 2][:, 0:CW], wg1[:, :], nodes_t[0:D, j * CW:(j + 1) * CW], start=True,
                                     stop=True).then_inc(s_a5, 1)
                pe.wait_ge(s_h5, 2 * NCH)
                node_products(pe, acc[:, 0, :], wg2[:, :], s_m5, s_r5, first=4)
                pe.wait_ge(s_x5, 1)
                to_features(pe, nodes_t, node_x, D, s_tr6, s_ev6)
                pe.wait_ge(s_ev6, (NB + 3) // 4)
                node_products(pe, nodes_t[0:D, :], w3x[:, :], s_m6, s_r6, first=6)

            @block.scalar
            def _(act):
                to_features_copy(act, nodes_t, D, s_tr5, s_ev5)
                for j in range(2 * NCH):
                    act.wait_ge(s_a5, j + 1)
                    nc.scalar.activation(acc[:, 0, j * CW:(j + 1) * CW], banks[2 + j % 2][:, 0:CW], ACT.Relu,
                                         bias=C(BG1)).then_inc(s_h5, 1)
                layer_norm_root(act, s_var5, s_std5)
                to_features_copy(act, nodes_t, D, s_tr6, s_ev6)

            @block.vector
            def _(dve):
                step = stepper(dve, "g_chain")
                add_accumulators(dve, acc_gin, D + 1, s_ld5, s_sm5, load=False)
                y = node_y[:, :, 0:D]
                step(nc.vector.tensor_copy(count[:, :].unsqueeze(2), node_y[:, :, D:D + 1]))
                nc.vector.tensor_tensor(y, y, node_x[:, :, :], ALU.add).then_inc(s_in5, 1)
                dve.wait_ge(s_tr5, (NB + 3) // 4)
                for q in range(NCH):
                    dve.wait_ge(s_m5, q + 1)
                    got, bl = chunk(q, 4)
                    nc.vector.tensor_tensor(node_y[:, bl, 0:D], got, over_nodes(bc[:, 3, 0:D]), ALU.add).then_inc(s_r5, 1)
                dve.wait_ge(s_r5, NCH)
                step(nc.vector.tensor_tensor(y, y, node_x[:, :, :], ALU.add))
                layer_norm(dve, (step, s_var5, s_std5), y)
                dve.sem_inc(s_x5, 1)
                for q in range(NCH):
                    dve.wait_ge(s_m6, q + 1)
                    got, bl = chunk(q, 6)
                    nc.vector.tensor_tensor(node_y[:, bl, 0:D], got, over_nodes(bc[:, 4, 0:D]), ALU.add).then_inc(s_r6, 1)

            @block.gpsimd
            def _(pool):
                retire(pool)

        mean_stage()
        s_ld7 = [sem(f"m_ld{c}") for c in range(T)]
        s_sm7, s_in7, s_tr7, s_ev7, s_a7, s_st7, s_b7, s_h7, s_m7, s_r7, s_var7, s_std7, s_x7, s_out = (
            sem(f"m_{k}") for k in "sm in tr ev a st b h m r var std x out".split())
        with nc.Block() as block:
            @block.sync
            def _(sp):
                add_accumulators(sp, acc_mean, D, s_ld7, s_sm7, load=True)
                sp.wait_ge(s_x7, 1)
                sp.dma_start(node_rows(out[0:(NB - 1) * P, :]), node_x[:, 0:NB - 1, :]).then_inc(s_out, 16)
                sp.dma_start(out[(NB - 1) * P:N, :], node_x[0:LB, NB - 1, :]).then_inc(s_out, 16)
                sp.wait_ge(s_out, 32)

            @block.tensor
            def _(pe):
                pe.wait_ge(s_in7, 1)
                to_features(pe, acc[:, 0, :], node_y, D + 1, s_tr7, s_ev7)
                pe.wait_ge(s_ev7, (NB + 3) // 4)
                for j in range(2 * NCH):
                    cols = slice(j * CW, (j + 1) * CW)
                    if j >= 2:
                        pe.wait_ge(s_st7, j - 1)
                    nc.tensor.matmul(banks[2 + j % 2][0:D, 0:CW], w3b[:, :], acc[0:D + 1, 0, cols], start=True,
                                     stop=True).then_inc(s_a7, 1)
                    pe.wait_ge(s_st7, j + 1)
                    if j >= 2:
                        pe.wait_ge(s_h7, j - 1)
                    nc.tensor.matmul(banks[4 + j % 2][0:D, 0:CW], w3cx[:, :], nodes_t[0:D, cols], start=True, stop=False)
                    nc.tensor.matmul(banks[4 + j % 2][0:D, 0:CW], w3ca[:, :], stage[0:D, j % 2, :], start=False,
                                     stop=True).then_inc(s_b7, 1)
                pe.wait_ge(s_h7, 2 * NCH)
                node_products(pe, acc[0:D, 1, :], w3d[:, :], s_m7, s_r7, first=6)

            @block.scalar
            def _(act):
                to_features_copy(act, acc[:, 0, :], D + 1, s_tr7, s_ev7)
                for j in range(2 * NCH):
                    act.wait_ge(s_a7, j + 1)
                    nc.scalar.copy(stage[0:D, j % 2, :], banks[2 + j % 2][0:D, 0:CW]).then_inc(s_st7, 1)
                    act.wait_ge(s_b7, j + 1)
                    nc.scalar.activation(acc[0:D, 1, j * CW:(j + 1) * CW], banks[4 + j % 2][0:D, 0:CW], ACT.Relu,
                                         bias=col[0:D, B3A2:B3A2 + 1]).then_inc(s_h7, 1)
                layer_norm_root(act, s_var7, s_std7)

            @block.vector
            def _(dve):
                step = stepper(dve, "m_chain")
                add_accumulators(dve, acc_mean, D, s_ld7, s_sm7, load=False)
                step(nc.vector.tensor_scalar(ln[:, 0, :], count[:, :], 1.0, None, ALU.max))
                step(nc.vector.reciprocal(ln[:, 1, :], ln[:, 0, :]))
                step(nc.vector.tensor_tensor(node_y[:, :, D:D + 1], count[:, :].unsqueeze(2), ln[:, 1, :].unsqueeze(2),
                                             ALU.mult))
                nc.vector.tensor_tensor(node_y[:, :, 0:D], node_y[:, :, 0:D],
                                        ln[:, 1, :].unsqueeze(2).to_broadcast([P, NB, D]), ALU.mult).then_inc(s_in7, 1)
                for q in range(NCH):
                    dve.wait_ge(s_m7, q + 1)
                    got, bl = chunk(q, 6)
                    nc.vector.tensor_tensor(node_y[:, bl, 0:D], got, over_nodes(bc[:, 1, D:2 * D]),
                                            ALU.add).then_inc(s_r7, 1)
                dve.wait_ge(s_r7, NCH)
                y = node_y[:, :, 0:D]
                step(nc.vector.tensor_tensor(y, y, node_x[:, :, :], ALU.add))
                layer_norm(dve, (step, s_var7, s_std7), y)
                dve.sem_inc(s_x7, 1)

            @block.gpsimd
            def _(pool):
                retire(pool)


WEIGHTS = ["L0_gnn_W1", "L0_gnn_b1", "L0_gnn_g1", "L0_gnn_be1", "L0_gnn_W2", "L0_gnn_b2", "L0_gnn_W3", "L0_gnn_b3",
           "L0_gnn_g2", "L0_gnn_be2", "L0_gnn_W4", "L0_gnn_b4", "L1_gnn_W1", "L1_gnn_b1", "L1_gnn_W2", "L1_gnn_b2",
           "L1_gnn_W3", "L1_gnn_b3", "L2_gnn_W1", "L2_gnn_b1", "L2_gnn_W2", "L2_gnn_b2", "L3_gnn_W1a", "L3_gnn_b1a",
           "L3_gnn_W1b", "L3_gnn_b1b", "L3_gnn_W2a", "L3_gnn_b2a", "L3_gnn_W2b", "L3_gnn_b2b"]


def kernel(**inputs):
    import numpy as np
    import concourse.bacc as bacc
    from concourse.bass_utils import run_bass_kernel_spmd

    nc = bacc.Bacc("TRN2", target_bir_lowering=False, num_devices=1)
    arrays, handles = {}, {}
    for name in ["x", "src", "dst", "edge_attr_64"] + WEIGHTS:
        a = np.ascontiguousarray(inputs[name])
        arrays[f"in_{name}"] = a
        handles[name] = nc.dram_tensor(f"in_{name}", a.shape, mybir.dt.from_np(a.dtype), kind="ExternalInput").ap()
    out = nc.dram_tensor("out", (N, D), F32, kind="ExternalOutput").ap()
    build(nc, handles["x"], handles["src"], handles["dst"], handles["edge_attr_64"], {k: handles[k] for k in WEIGHTS}, out)
    return run_bass_kernel_spmd(nc, [arrays], core_ids=[0]).results[0]["out"]
```

```python
from contextlib import ExitStack

import concourse.bass as bass
from concourse import mybir

P = 128
N, E, D, H = 6250, 206250, 64, 128
T = 8
GE = T * P
NG = (E + GE - 1) // GE
LAST = E - (NG - 1) * GE
NB = (N + P - 1) // P
NP = NB * P
LB = N - (NB - 1) * P
WIN = 64
NA = NP + P
CH = 7
NCH = NB // CH
CW = CH * P // 2
CLEAR_STEP = 8
EPS = 1e-5
SLOPE = 0.01
assert (NA // P) % 2 == 0 and 2 + T * CLEAR_STEP < NG // 2 and NG % 2 == 0 and NB % CH == 0 and (2 * NP) % (2 * CW) == 0

F32, I32, U32, BF16 = mybir.dt.float32, mybir.dt.int32, mybir.dt.uint32, mybir.dt.bfloat16
ALU, ACT, AX = mybir.AluOpType, mybir.ActivationFunctionType, mybir.AxisListType


def build(nc, x, src, dst, edge_attr, W, out):
    ctx = ExitStack()
    with ctx:
        def sb(name, shape, dt=F32):
            return ctx.enter_context(nc.sbuf_tensor(name, shape, dt))

        def sem(name):
            return ctx.enter_context(nc.semaphore(name))

        def dram(name, shape, dt=F32):
            return nc.dram_tensor(name, shape, dt, kind="Internal").ap()

        tab_pre0 = dram("tab_pre0", (NA, H))
        tab = [dram(f"tab_{n}", (NA, D)) for n in ("conv1", "conv2", "conv3")]
        tab_gin = dram("tab_gin", (NA, D + 1))
        tab_pre3 = dram("tab_pre3", (NA, D))
        acc_gin = [dram(f"acc_gin{c}", (NA, D + 1)) for c in range(T)]
        acc_mean = [dram(f"acc_mean{c}", (NA, D)) for c in range(T)]
        span_d = dram("span_d", (2, NG), I32)

        ident = sb("ident", [P, P])
        lower = sb("lower", [P, P])
        ones = sb("ones", [P, P])
        iota_i = sb("iota_i", [P, WIN], I32)
        iota_w = sb("iota_w", [P, WIN])
        trash_i = sb("trash_i", [P, 1], I32)
        trash = sb("trash", [P, 1])
        src_i = sb("src_i", [P, NG, T], I32)
        dst_i = sb("dst_i", [P, NG, T], I32)
        src_f = sb("src_f", [P, NG, T])
        dst_rel = sb("dst_rel", [P, NG, T])
        scat_i = dst_i
        span_row = sb("span_row", [1, 2, NG], I32)
        acc = sb("acc", [P, 2, NA])
        nodes_t = sb("nodes_t", [D + 1, NA])
        node_x = sb("node_x", [P, NB, D])
        node_y = sb("node_y", [P, NB, D + 1])
        node_z = sb("node_z", [P, NB, D + 1])
        dinv = sb("dinv", [P, NB])
        ln = sb("ln", [P, 4, NB])
        count = sb("count", [P, NB])
        inv_count = sb("inv_count", [P, NB])
        gath = sb("gath", [P, 2, T, H])
        eattr = sb("eattr", [P, 2, T, D])
        eattr_t = sb("eattr_t", [P, 2, T // 2, P])
        hid = sb("hid", [P, 2, T, H])
        squares = sb("squares", [P, T, H])
        sq_sum = sb("sq_sum", [P, T, H])
        onehot = sb("onehot", [P, 2, T, WIN])
        onehot_b = sb("onehot_b", [P, 2, T, WIN], BF16)
        onehot_x = node_z[:, :, :].rearrange("p b f -> p (b f)")[:, 0:T * WIN].rearrange("p (c n) -> p c n", c=T)
        onehot_xb = sb("onehot_xb", [P, T, WIN], BF16)
        drel = sb("drel", [P, T])
        idx_g = sb("idx_g", [P, 2, T], I32)
        idx_s = sb("idx_s", [P, 2, T], I32)
        same = sb("same", [P, 2, T, P], BF16)
        dup = sb("dup", [P, 2, T])
        addend = node_y[:, :, :].rearrange("p b f -> p (b f)")[:, 0:2 * T * (D + 1)].rearrange(
            "p (s c f) -> p s c f", s=2, c=T)
        zeros = node_y[:, :, :].rearrange("p b f -> p (b f)")[:, 0:(NA // P) // 2 * (D + 1)]
        zero_w = sb("zero_w", [P, H])
        zero_b = sb("zero_b", [P, H], BF16)
        ones_b = sb("ones_b", [P, P], BF16)
        earlier = sb("earlier", [P, T, P], BF16)
        lower_b = sb("lower_b", [P, P], BF16)
        src_s = sb("src_s", [P, 2, T])
        lhs3 = sb("lhs3", [P, 3, D])
        win_x = sb("win_x", [P, 3, D + 1])
        wnode = sb("wnode", [P, 2])
        stage = sb("stage", [P, 2, CW])
        parts = sb("parts", [P, 2 * NCH])
        col = sb("col", [P, 24])
        bc = sb("bc", [P, 5, H])
        w0x = sb("w0x", [D, H])
        w0e = sb("w0e", [P, 2 * H])
        w0b = sb("w0b", [H, H])
        w0cx = sb("w0cx", [D, H])
        w0ca = sb("w0ca", [H, H])
        w0d = sb("w0d", [H, D])
        wc_in = sb("wc_in", [D, 3, D])
        wc = sb("wc", [D + 1, 3, D])
        wg1 = sb("wg1", [D, H])
        wg2 = sb("wg2", [H, D])
        w3x = sb("w3x", [D, D])
        w3b = sb("w3b", [D + 1, D])
        w3cx = sb("w3cx", [D, D])
        w3ca = sb("w3ca", [D, D])
        w3d = sb("w3d", [D, D])

        banks = [ctx.enter_context(nc.psum_tensor(f"bank{i}", [P, 512], F32)) for i in range(8)]

        def node_rows(t):
            return t.rearrange("(b p) f -> p b f", p=P)

        def by_row(t, blocks=slice(0, NB)):
            return t[0:NP, :].rearrange("(p b) f -> p b f", b=NB)[:, blocks, :]

        def row_bc(v):
            return v.rearrange("(a f) -> a f", a=1).to_broadcast([P, v.shape[0]])

        def column(v):
            return v.rearrange("(f a) -> f a", a=1)

        GB1, GBE1, B2, B3, G2, BE2, BG1, B3A2 = range(8)
        M1, V1, SC1, SH1, S1, Q1, M2, V2, SC2, SH2, NM2 = range(8, 19)

        s_fill = sem("s_fill")
        s_par = sem("s_par")
        s_idx = sem("s_idx")
        s_cst = sem("s_cst")
        s_spn = sem("s_spn")
        s_sp0 = sem("s_sp0")
        s_span = sem("s_span")
        s_gm = sem("s_gm")
        with nc.Block() as block:
            ends = acc[:, 1, 0:2 * GE].bitcast(I32)
            QG = NG // 2
            mn, mx = ln[0:QG, 0, 0:2].bitcast(I32), ln[0:QG, 1, 0:2].bitcast(I32)
            base_bc = hid[:, 0, 0:2, :].rearrange("p a b -> p (a b)")[:, 0:NG].bitcast(I32)
            n_param = [0]

            @block.sync
            def _(sp):
                tail = (NG - 2) * GE
                sp.dma_start(ends[0:QG - 1, :], dst[0:tail].rearrange("(q e) -> q e", q=QG - 1)).then_inc(s_gm, 16)
                sp.dma_start(ends[QG - 1:QG, 0:GE + LAST], dst[tail:E].rearrange("(q e) -> q e", q=1)).then_inc(s_gm, 16)
                sp.dma_start(ends[QG - 1:QG, GE + LAST:2 * GE],
                             dst[E - GE + LAST:E].rearrange("(q e) -> q e", q=1)).then_inc(s_gm, 16)
                sp.wait_ge(s_fill, 2)
                full, part = LAST // T, LAST % T
                for t, d in ((src_i, src), (dst_i, dst)):
                    sp.dma_start(t[:, 0:NG - 1, :],
                                 d[0:(NG - 1) * GE].rearrange("(g p c) -> p g c", p=P, c=T)).then_inc(s_idx, 16)
                    sp.dma_start(t[0:full, NG - 1, :],
                                 d[(NG - 1) * GE:(NG - 1) * GE + full * T].rearrange("(p c) -> p c", c=T)).then_inc(s_idx, 16)
                    if part:
                        sp.dma_start(t[full:full + 1, NG - 1, 0:part],
                                     d[(NG - 1) * GE + full * T:E].rearrange("(p c) -> p c", p=1)).then_inc(s_idx, 16)
                sp.wait_ge(s_spn, 1)
                sp.dma_start(span_d[0, :].rearrange("(q r) -> q r", r=2), mn).then_inc(s_sp0, 16)
                sp.dma_start(span_d[1, :].rearrange("(q r) -> q r", r=2), mx).then_inc(s_sp0, 16)
                sp.wait_ge(s_sp0, 32)
                sp.dma_start(span_row[:, :, :], span_d.rearrange("(a t) g -> a t g", a=1)).then_inc(s_span, 16)
                sp.dma_start(base_bc, span_d[0:1, :].to_broadcast([P, NG])).then_inc(s_span, 16)
                sp.wait_ge(s_span, 32)

            @block.scalar
            def _(act):
                def load(dst_ap, src_ap):
                    act.dma_start(dst_ap, src_ap).then_inc(s_par, 16)
                    n_param[0] += 1

                act.wait_ge(s_fill, 4)
                load(node_x[:, 0:NB - 1, :], node_rows(x[0:(NB - 1) * P, :]))
                load(node_x[0:LB, NB - 1, :], x[(NB - 1) * P:N, :])
                load(w0x[:, :], W["L0_gnn_W1"][0:D, :])
                load(w0e[0:D, 0:H], W["L0_gnn_W1"][D:2 * D, :])
                load(w0e[D:P, H:2 * H], W["L0_gnn_W1"][D:2 * D, :])
                load(w0b[:, :], W["L0_gnn_W2"])
                load(w0cx[:, :], W["L0_gnn_W3"][0:D, :])
                load(w0ca[:, :], W["L0_gnn_W3"][D:D + H, :])
                load(w0d[:, :], W["L0_gnn_W4"])
                for i in range(3):
                    load(wc_in[:, i, :], W[f"L1_gnn_W{i + 1}"])
                    load(wc[D:D + 1, i, :], W[f"L1_gnn_b{i + 1}"].rearrange("(a f) -> a f", a=1))
                load(wg1[:, :], W["L2_gnn_W1"])
                load(wg2[:, :], W["L2_gnn_W2"])
                load(w3x[:, :], W["L3_gnn_W1a"][0:D, :])
                for s in range(2):
                    load(lhs3[0:D, s, :], W["L3_gnn_W1a"][D:2 * D, :])
                load(w3b[0:D, :], W["L3_gnn_W1b"])
                load(w3b[D:D + 1, :], W["L3_gnn_b1b"].rearrange("(a f) -> a f", a=1))
                load(w3cx[:, :], W["L3_gnn_W2a"][0:D, :])
                load(w3ca[:, :], W["L3_gnn_W2a"][D:2 * D, :])
                load(w3d[:, :], W["L3_gnn_W2b"])
                for c, name in ((GB1, "L0_gnn_g1"), (GBE1, "L0_gnn_be1"), (B2, "L0_gnn_b2"), (B3, "L0_gnn_b3"),
                                (G2, "L0_gnn_g2"), (BE2, "L0_gnn_be2"), (BG1, "L2_gnn_b1")):
                    load(col[:, c:c + 1], column(W[name]))
                load(col[0:D, B3A2:B3A2 + 1], column(W["L3_gnn_b2a"]))
                for r, name in enumerate(("L0_gnn_b1", "L0_gnn_b4", "L1_gnn_b2", "L2_gnn_b2", "L3_gnn_b1a")):
                    load(bc[:, r, 0:W[name].shape[0]], row_bc(W[name]))
                load(bc[:, 1, D:2 * D], row_bc(W["L3_gnn_b2b"]))
                act.wait_ge(s_par, 16 * n_param[0])

            @block.gpsimd
            def _(pool):
                nc.gpsimd.memset(src_i[:, NG - 1, :], NP + P - 1).then_inc(s_fill, 1)
                nc.gpsimd.memset(dst_i[:, NG - 1, :], N).then_inc(s_fill, 1)
                nc.gpsimd.memset(node_x[:, NB - 1, :], 0.0).then_inc(s_fill, 1)
                nc.gpsimd.memset(w0e[:, :], 0.0).then_inc(s_fill, 1)
                nc.gpsimd.memset(zero_w[:, :], 0.0)
                nc.gpsimd.memset(zero_b[:, :], 0.0)
                nc.gpsimd.memset(ones_b[:, :], 1.0)
                nc.gpsimd.memset(lhs3[:, 2, :], 0.0)
                nc.gpsimd.memset(zeros, 0.0)
                nc.gpsimd.memset(ones[:, :], 1.0).then_inc(s_cst, 1)
                pool.wait_ge(s_cst, 1)
                nc.gpsimd.affine_select(out=ident[:, :], in_=ones[:, :], compare_op=ALU.is_equal, fill=0.0, base=0,
                                        pattern=[[-1, P]], channel_multiplier=1).then_inc(s_cst, 1)
                nc.gpsimd.affine_select(out=lower[:, :], in_=ones[:, :], compare_op=ALU.is_gt, fill=0.0, base=0,
                                        pattern=[[-1, P]], channel_multiplier=1).then_inc(s_cst, 1)
                nc.gpsimd.iota(iota_i[:, :], [[1, WIN]], base=0, channel_multiplier=0).then_inc(s_cst, 1)
                nc.gpsimd.iota(trash_i[:, :], [[0, 1]], base=NP, channel_multiplier=1).then_inc(s_cst, 1)

            @block.vector
            def _(dve):
                s_d, s_row = sem("s_d0"), sem("s_row")
                dve.wait_ge(s_gm, 48)
                e3 = ends[0:QG, :].rearrange("q (r e) -> q r e", r=2)
                nc.vector.tensor_reduce(mn, e3, AX.X, ALU.min).then_inc(s_d, 1)
                nc.vector.tensor_reduce(mx, e3, AX.X, ALU.max).then_inc(s_d, 1)
                dve.wait_ge(s_d, 2)
                nc.vector.tensor_tensor(mx, mx, mn, ALU.subtract).then_inc(s_d, 1)
                dve.wait_ge(s_d, 3)
                nc.vector.tensor_scalar(mx, mx, WIN.bit_length() - 1, None, ALU.arith_shift_right).then_inc(s_d, 1)
                dve.wait_ge(s_d, 4)
                nc.vector.tensor_scalar(mx, mx, 1, None, ALU.add).then_inc(s_spn, 1)
                dve.wait_ge(s_cst, 5)
                nc.vector.tensor_copy(iota_w[:, :], iota_i[:, :])
                nc.vector.tensor_copy(trash[:, :], trash_i[:, :]).then_inc(s_d, 1)
                nc.vector.tensor_copy(lower_b[:, :], lower[:, :])
                dve.wait_ge(s_d, 5)
                nc.vector.tensor_scalar(wnode[:, 0:1], trash[:, :], -float(NP + D), None, ALU.add)
                dve.wait_ge(s_idx, 16 * (6 if LAST % T else 4))
                low, high = (acc[:, 0, k * NG * T:(k + 1) * NG * T].rearrange("p (g c) -> p g c", c=T).bitcast(I32)
                             for k in range(2))
                nc.vector.tensor_scalar(low, src_i[:, :, :], P - 1, None, ALU.bitwise_and)
                nc.vector.tensor_scalar(high, src_i[:, :, :], P.bit_length() - 1, None,
                                        ALU.arith_shift_right).then_inc(s_row, 1)
                dve.wait_ge(s_row, 1)
                nc.vector.scalar_tensor_tensor(out=src_f[:, :, :], in0=low, scalar=float(NB), in1=high, op0=ALU.mult,
                                               op1=ALU.add).then_inc(s_row, 1)
                dve.wait_ge(s_row, 2)
                nc.vector.tensor_copy(src_i[:, :, :], src_f[:, :, :])
                dve.wait_ge(s_span, 32)
                nc.vector.tensor_tensor(dst_rel[:, :, :], dst_i[:, :, :],
                                        base_bc.unsqueeze(2).to_broadcast([P, NG, T]), ALU.subtract).then_inc(s_d, 1)
                dve.wait_ge(s_d, 6)
                nc.vector.scalar_tensor_tensor(out=dst_rel[:, NG - 1, :], in0=dst_i[:, NG - 1, :], scalar=float(N),
                                               in1=dst_rel[:, NG - 1, :], op0=ALU.is_lt, op1=ALU.mult).then_inc(s_d, 1)
                dve.wait_ge(s_d, 7)
                nc.vector.scalar_tensor_tensor(out=dst_rel[:, NG - 1, :], in0=dst_i[:, NG - 1, :], scalar=float(N),
                                               in1=dst_rel[:, NG - 1, :], op0=ALU.is_ge,
                                               op1=ALU.subtract).then_inc(s_d, 1)
                dve.wait_ge(s_d, 8)
                nc.vector.tensor_scalar(dst_rel[:, NG - 1, :], dst_rel[:, NG - 1, :], -1.0, None, ALU.mult)

        def to_features(pe, dst_t, source, width, s_tr, s_ev, src_ready=None):
            for q in range((NB + 3) // 4):
                if q >= 2:
                    pe.wait_ge(s_ev, q - 1)
                for k in range(min(4, NB - 4 * q)):
                    last = nc.tensor.transpose(banks[q % 2][0:width, k * P:(k + 1) * P],
                                               source[:, 4 * q + k, 0:width], ident[:, :])
                last.then_inc(s_tr, 1)

        def to_features_copy(act, dst_t, width, s_tr, s_ev):
            for q in range((NB + 3) // 4):
                act.wait_ge(s_tr, q + 1)
                n = min(4, NB - 4 * q) * P
                nc.scalar.copy(dst_t[0:width, 4 * q * P:4 * q * P + n], banks[q % 2][0:width, 0:n]).then_inc(s_ev, 1)

        def layer_norm(dve, step, q, s_var):
            bl = slice(CH * q, CH * (q + 1))
            y, z = node_y[:, bl, 0:D], node_z[:, bl, 0:D]
            mean, var = ln[:, 0, bl], ln[:, 1, bl]
            step(nc.vector.tensor_reduce(mean, y, AX.X, ALU.add))
            step(nc.vector.tensor_scalar(mean, mean, 1.0 / D, None, ALU.mult))
            step(nc.vector.tensor_tensor(y, y, mean.unsqueeze(2).to_broadcast([P, CH, D]), ALU.subtract))
            step(nc.vector.tensor_tensor(z, y, y, ALU.mult))
            step(nc.vector.tensor_reduce(var, z, AX.X, ALU.add))
            nc.vector.tensor_scalar(var, var, 1.0 / D, EPS, ALU.mult, ALU.add).then_inc(s_var, 1)

        def layer_norm_end(dve, step, q, s_std):
            bl = slice(CH * q, CH * (q + 1))
            dve.wait_ge(s_std, q + 1)
            step(nc.vector.reciprocal(ln[:, 3, bl], ln[:, 2, bl]))
            step(nc.vector.tensor_tensor(node_x[:, bl, :], node_y[:, bl, 0:D],
                                         ln[:, 3, bl].unsqueeze(2).to_broadcast([P, CH, D]), ALU.mult))

        def layer_norm_root(act, q, s_var, s_std):
            act.wait_ge(s_var, q + 1)
            bl = slice(CH * q, CH * (q + 1))
            nc.scalar.activation(ln[:, 2, bl], ln[:, 1, bl], ACT.Sqrt).then_inc(s_std, 1)

        def stepper(dve, name):
            s = sem(name)
            count = [0]

            def step(ins):
                count[0] += 1
                ins.then_inc(s, 1)
                dve.wait_ge(s, count[0])
            return step

        s_t, s_e, s_m, s_a, s_w, s_wt, s_wv = (sem(f"pre_{k}") for k in "temawuv")
        pre = acc[:, 0, 0:NB * H].rearrange("p (b f) -> p b f", f=H)
        with nc.Block() as block:
            @block.tensor
            def _(pe):
                to_features(pe, nodes_t, node_x, D, s_t, s_e)
                for i in range(3):
                    last = nc.tensor.transpose(banks[4][0:D, i * D:(i + 1) * D], wc_in[:, i, :], ident[0:D, 0:D])
                last.then_inc(s_wt, 1)
                pe.wait_ge(s_e, (NB + 3) // 4)
                for q in range((NB + 3) // 4):
                    if q >= 2:
                        pe.wait_ge(s_a, q - 1)
                    for k in range(min(4, NB - 4 * q)):
                        b = 4 * q + k
                        last = nc.tensor.matmul(banks[2 + q % 2][:, k * H:(k + 1) * H], nodes_t[0:D, b * P:(b + 1) * P],
                                                w0x[:, :], start=True, stop=True)
                    last.then_inc(s_m, 1)

            @block.scalar
            def _(act):
                to_features_copy(act, nodes_t, D, s_t, s_e)
                act.wait_ge(s_wt, 1)
                nc.scalar.copy(wc[0:D, :, :], banks[4][0:D, 0:3 * D].rearrange("p (i f) -> p i f", i=3))

            @block.vector
            def _(dve):
                for q in range((NB + 3) // 4):
                    dve.wait_ge(s_m, q + 1)
                    n = min(4, NB - 4 * q)
                    nc.vector.tensor_tensor(pre[:, 4 * q:4 * q + n, :],
                                            banks[2 + q % 2][:, 0:n * H].rearrange("p (b f) -> p b f", f=H),
                                            bc[:, 0, :].unsqueeze(1).to_broadcast([P, n, H]), ALU.add).then_inc(s_a, 1)

            @block.sync
            def _(sp):
                sp.wait_ge(s_a, (NB + 3) // 4)
                sp.dma_start(by_row(tab_pre0), pre).then_inc(s_w, 16)
                sp.dma_start(tab_pre0[NP:NA, :], zero_w[:, :]).then_inc(s_w, 16)
                sp.wait_ge(s_w, 32)

        def both(eng, body, end=NG // 2):
            body(0, 0, 0)
            body(0, 1, 1)
            with eng.Fori(1, end) as it:
                for s in range(2):
                    body(it, s, it * 2 + s)

        def wait(eng, semaphore, value):
            if not isinstance(value, int) or value > 0:
                eng.wait_ge(semaphore, value)

        def send_indices(sp, it, s, g, table, gathered, here):
            wait(sp, gathered[s], 16 * T * it)
            sp.dma_start(idx_g[:, s, :], table[:, bass.ds(g, 1), :].rearrange("p a c -> p (a c)")).then_inc(here[s], 16)

        def send_attributes(sp, it, s, g, at, turned, there):
            wait(sp, turned[s], it)
            sp.dma_start(at, edge_attr[bass.ds(g * GE, GE), :].rearrange("(p c) f -> p c f", p=P)).then_inc(there[s], 16)

        def send_last_attributes(sp, at, filler, turned, there):
            sp.wait_ge(turned[1], NG // 2 - 1)
            full, part = LAST // T, LAST % T
            e0 = (NG - 1) * GE
            sp.dma_start(at[0:full, :, :], edge_attr[e0:e0 + full * T, :].rearrange(
                "(p c) f -> p c f", c=T)).then_inc(there[1], 16)
            if part:
                sp.dma_start(at[full:full + 1, 0:part, :], edge_attr[e0 + full * T:E, :].rearrange(
                    "(p c) f -> p c f", p=1)).then_inc(there[1], 16)
                sp.dma_start(at[full:full + 1, part:T, :], filler[0:T - part, :].rearrange(
                    "(p c) f -> p c f", p=1)).then_inc(there[1], 16)
            first = full + (part > 0)
            sp.dma_start(at[first:P, :, :], filler[0:(P - first) * T, :].rearrange(
                "(p c) f -> p c f", c=T)).then_inc(there[1], 16)

        N_LAST = (3 if LAST % T else 1) + 1

        def gather_rows(pool, it, s, table, width, here, free, gathered, begun):
            indices, used = pool.snap(16 * (it + 1)), pool.snap(it)
            pool.wait_ge(here[s], indices)
            wait(pool, free[s], used)
            pool.sem_inc(begun, 1)
            for c in range(T):
                pool.indirect_dma_start(gath[:, s, c, 0:width], None, table[:, :], bass.IndirectOffsetOnAxis(
                    ap=idx_g[:, s, c:c + 1].bitcast(U32), axis=0)).then_inc(gathered[s], 16)

        edge_sems = []

        def edge_sem(name):
            edge_sems.append(nc.alloc_semaphore(name=name))
            return edge_sems[-1]

        def slots(name):
            return [edge_sem(f"{name}0"), edge_sem(f"{name}1")]

        def retire(pool):
            nc.clear_and_free_semaphores(edge_sems)
            edge_sems.clear()

        def copy_attributes(act, it, s, turned, copied, joined):
            wait(act, joined[s], it)
            act.wait_ge(turned[s], it + 1)
            nc.scalar.copy(eattr_t[:, s, :, :], banks[6][:, :].rearrange("p (q e) -> p q e", e=P)).then_inc(copied[s], 1)

        def slot_after(it, s):
            return (it, 1) if s == 0 else (it + 1, 0)

        def before(it, s):
            return it if s == 0 else it + 1

        def base_of(eng, g):
            return eng.value_load(span_row[0:1, 0, bass.ds(g, 1)], min_val=0, max_val=N - 1)

        def further_windows(eng, g, seen, body, ahead=None):
            windows = eng.value_load(span_row[0:1, 1, bass.ds(g, 1)], min_val=1, max_val=N // WIN + 1)
            with eng.If(windows > 1):
                if ahead is not None:
                    ahead()
                with eng.Fori(1, windows) as w:
                    body(eng.snap(seen, min_val=0, max_val=2 ** 20))
                    eng.reg_add(seen, seen, 1)

        def register(eng, name, value=0):
            reg = eng.alloc_register(name)
            eng.reg_mov(reg, value)
            return reg

        def is_window(out_ap, rel):
            return nc.vector.tensor_tensor(out_ap, iota_w[:, :].unsqueeze(1).to_broadcast([P, T, WIN]),
                                           rel.unsqueeze(2).to_broadcast([P, T, WIN]), ALU.is_equal)

        def group_rel(g):
            return dst_rel[:, bass.ds(g, 1), :].rearrange("p a c -> p (a c)")

        def window_stage(name, table, mlp0):
            width = H if mlp0 else D
            n_acc = 2 if mlp0 else 1
            here, gathered, free, hot, won = (slots(f"{name}_{k}") for k in ("here", "gathered", "free", "hot", "won"))
            s_add, s_xhot, s_xwon = (edge_sem(f"{name}_{k}") for k in ("add", "xhot", "xwon"))
            if mlp0:
                there, turned, copied, joined, summed, ready, hot_b, squared, sq_added = (
                    slots(f"{name}_{k}") for k in ("there", "turned", "copied", "joined", "summed", "ready", "hotb",
                                                   "squared", "sqadded"))
                s_xhot_b, s_closed = edge_sem(f"{name}_xhotb"), edge_sem(f"{name}_closed")
            begun = edge_sem(f"{name}_begun")
            rows = hid if mlp0 else gath
            sums = banks[4]
            with nc.Block() as block:
                @block.sync
                def _(sp):
                    def group(it, s, g):
                        send_indices(sp, it, s, g, src_i, gathered, here)
                        if mlp0:
                            send_attributes(sp, it, s, g, eattr[:, s, :, :], turned, there)

                    def clear(c):
                        for a, f in ((acc_gin[c], D + 1), (acc_mean[c], D)):
                            n = (NA // P) // 2 * f
                            sp.dma_start(a.rearrange("(p h r) f -> p h (r f)", p=P, h=2), zeros[:, 0:n].unsqueeze(
                                1).to_broadcast([P, 2, n])).then_inc(cleared, 16)
                    if not mlp0:
                        both(sp, group)
                        return
                    cleared = sem("cleared")
                    both(sp, group, 2)
                    for c in range(T):
                        clear(c)
                        with sp.Fori(2 + c * CLEAR_STEP, 2 + (c + 1) * CLEAR_STEP if c < T - 1 else NG // 2 - 1) as it:
                            for s in range(2):
                                group(it, s, it * 2 + s)
                    sp.dma_start(tab_gin[NP:NA, :], zeros[:, 0:D + 1]).then_inc(cleared, 16)
                    for t in (tab_pre3, *tab):
                        sp.dma_start(t[NP:NA, :], zeros[:, 0:D]).then_inc(cleared, 16)
                    group(NG // 2 - 1, 0, NG - 2)
                    send_indices(sp, NG // 2 - 1, 1, NG - 1, src_i, gathered, here)
                    sp.wait_ge(cleared, 16 * (2 * T + 2 + len(tab)))
                    send_last_attributes(sp, eattr[:, 1, :, :], acc_mean[0], turned, there)

                @block.gpsimd
                def _(pool):
                    both(pool, lambda it, s, g: gather_rows(pool, it, s, table, width, here, summed if mlp0 else free,
                                                              gathered, begun))

                @block.scalar
                def _(act):
                    if not mlp0:
                        return
                    seen = register(act, f"{name}_act_seen")

                    def group(it, s, g, final=False):
                        act.wait_ge(hot[s], it + 1)
                        nc.scalar.copy(onehot_b[:, s, :, :], onehot[:, s, :, :]).then_inc(hot_b[s], 1)
                        if not (final and s == 1):
                            copy_attributes(act, *slot_after(it, s), turned, copied, joined)
                        act.wait_ge(ready[s], it + 1)
                        wait(act, sq_added[1 - s], before(it, s))
                        nc.scalar.activation(squares[:, :, :], hid[:, s, :, :], ACT.Square).then_inc(squared[s], 1)

                        def window(k):
                            act.wait_ge(s_xhot, k + 1)
                            nc.scalar.copy(onehot_xb[:, :, :], onehot_x[:, :, :]).then_inc(s_xhot_b, 1)
                        further_windows(act, g, seen, window)
                    copy_attributes(act, 0, 0, turned, copied, joined)
                    both(act, group, NG // 2 - 1)
                    group(NG // 2 - 1, 0, NG - 2, final=True)
                    group(NG // 2 - 1, 1, NG - 1, final=True)

                @block.tensor
                def _(pe):
                    seen = register(pe, f"{name}_pe_seen")

                    def turn(it, s, last=False):
                        pe.wait_ge(there[s], 16 * it + 16 * (N_LAST if last else 1))
                        wait(pe, copied[1 - s], before(it, s))
                        for q in range(T // 2):
                            ins = nc.tensor.transpose(banks[6][:, q * P:(q + 1) * P],
                                                      eattr[:, s, 2 * q:2 * q + 2, :].rearrange("p c f -> p (c f)"),
                                                      ident[:, :])
                        ins.then_inc(turned[s], 1)

                    def join(it, s):
                        pe.wait_ge(copied[s], it + 1)
                        wait(pe, summed[s], it)
                        for q in range(T // 2):
                            ins = nc.tensor.matmul(banks[2 * s + q // 2][:, (q % 2) * 2 * H:(q % 2 + 1) * 2 * H],
                                                   eattr_t[:, s, q, :], w0e[:, :], start=True, stop=True)
                        ins.then_inc(joined[s], 1)

                    def window_sums(s, hots, hots_b):
                        for c in range(T):
                            ins = nc.tensor.matmul(sums[0:width, 0:WIN], rows[:, s, c, 0:width], hots[:, c, :],
                                                   start=(c == 0), stop=(c == T - 1))
                        if mlp0:
                            for c in range(T):
                                ins = nc.tensor.matmul(sums[:, WIN:2 * WIN], ones_b[:, :], hots_b[:, c, :],
                                                       start=(c == 0), stop=(c == T - 1))
                        return ins

                    def group(it, s, g, final=False):
                        if mlp0:
                            if not (final and s == 1):
                                turn(*slot_after(it, s), last=final)
                                join(*slot_after(it, s))
                            pe.wait_ge(hot_b[s], it + 1)
                            pe.wait_ge(ready[s], it + 1)
                            wait(pe, s_closed, g)
                        else:
                            pe.wait_ge(hot[s], it + 1)
                            pe.wait_ge(gathered[s], 16 * T * (it + 1))
                        pe.wait_ge(s_add, g + 1)
                        window_sums(s, onehot[:, s, :, :], onehot_b[:, s, :, :]).then_inc(won[s], 1)

                        def window(k):
                            if mlp0:
                                pe.wait_ge(s_xhot_b, k + 1)
                            pe.wait_ge(s_xhot, k + 1)
                            window_sums(s, onehot_x, onehot_xb).then_inc(s_xwon, 1)
                        further_windows(pe, g, seen, window)
                    if mlp0:
                        turn(0, 0)
                        join(0, 0)
                    both(pe, group, NG // 2 - 1)
                    group(NG // 2 - 1, 0, NG - 2, final=True)
                    group(NG // 2 - 1, 1, NG - 1, final=True)

                @block.vector
                def _(dve):
                    seen = register(dve, f"{name}_dve_seen")
                    start = register(dve, f"{name}_dve_start")
                    if mlp0:
                        nc.vector.memset(sq_sum[:, :, :], 0.0)
                        nc.vector.memset(acc[:, :, :], 0.0).then_inc(s_add, 1)
                    elif name != "conv2":
                        nc.vector.memset(acc[D:D + 1, 0, :], 1.0)
                        nc.vector.memset(acc[0:D, 0, :], 0.0).then_inc(s_add, 1)
                    else:
                        nc.vector.memset(acc[0:D, 0, NP:NA], 0.0).then_inc(s_add, 1)

                    def add_window(first):
                        at = acc[0:width, 0:n_acc, bass.ds(first, WIN)]
                        return nc.vector.tensor_tensor(at, at, sums[0:width, 0:n_acc * WIN].rearrange(
                            "p (a n) -> p a n", a=n_acc), ALU.add)

                    def features(it, s, g):
                        wait(dve, won[s], it)
                        is_window(onehot[:, s, :, :], group_rel(g)).then_inc(hot[s], 1)
                        if mlp0:
                            dve.wait_ge(joined[s], it + 1)
                            dve.wait_ge(gathered[s], 16 * T * (it + 1))
                            for q in range(2):
                                ins = nc.vector.tensor_tensor(
                                    hid[:, s, 4 * q:4 * q + 4, :],
                                    banks[2 * s + q][:, :].rearrange("p (c f) -> p c f", f=H),
                                    gath[:, s, 4 * q:4 * q + 4, :], ALU.add)
                            ins.then_inc(summed[s], 1)
                            dve.wait_ge(summed[s], it + 1)
                            nc.vector.scalar_tensor_tensor(out=hid[:, s, :, :], in0=hid[:, s, :, :], scalar=SLOPE,
                                                           in1=hid[:, s, :, :], op0=ALU.mult,
                                                           op1=ALU.max).then_inc(ready[s], 1)

                    def add_squares(it, s):
                        dve.wait_ge(squared[s], it + 1)
                        nc.vector.tensor_tensor(sq_sum[:, :, :], sq_sum[:, :, :], squares[:, :, :],
                                                ALU.add).then_inc(sq_added[s], 1)

                    def add_windows(won_before, s, g):
                        base = base_of(dve, g)
                        dve.wait_ge(won[s], won_before + 1)
                        dve.wait_ge(s_add, g + 1)
                        add_window(base).then_inc(s_add, 1)
                        dve.reg_mov(start, base)

                        def second():
                            dve.drain()
                            nc.vector.tensor_scalar(drel[:, :], group_rel(g), float(WIN), None, ALU.subtract)

                        def window(k):
                            dve.drain()
                            is_window(onehot_x[:, :, :], drel[:, :]).then_inc(s_xhot, 1)
                            dve.reg_add(start, start, WIN)
                            dve.wait_ge(s_xwon, k + 1)
                            nc.vector.tensor_scalar(drel[:, :], drel[:, :], float(WIN), None, ALU.subtract)
                            add_window(dve.snap(start, min_val=0, max_val=NA - WIN))
                            dve.drain()
                        further_windows(dve, g, seen, window, ahead=second)
                        dve.sem_inc(s_closed if mlp0 else free[s], 1)

                    def group(it, s, g):
                        features(it, s, g)
                        if not mlp0:
                            add_windows(it, s, g)
                            return
                        if s == 1:
                            add_windows(it, 0, g - 1)
                        elif not (isinstance(it, int) and it == 0):
                            add_windows(it - 1, 1, g - 1)
                        add_squares(it, s)
                    both(dve, group)
                    if mlp0:
                        add_windows(NG // 2 - 1, 1, NG - 1)

        def add_rows(pool, it, s, accs, width, index, addable, added, begun):
            now = pool.snap(it + 1)
            before_now = pool.snap(16 * (T // 2) * before(it, s))
            pool.wait_ge(index[s], now)
            pool.wait_ge(addable[s], now)
            for h in range(2):
                wait(pool, added[1 - s][h], before_now)
                pool.sem_inc(begun, 1)
                for c in range(h * T // 2, (h + 1) * T // 2):
                    pool.indirect_dma_start(accs[c][:, :], bass.IndirectOffsetOnAxis(
                        ap=idx_s[:, s, c:c + 1].bitcast(U32), axis=0), addend[:, s, c, 0:width], None,
                        bounds_check=NA - 1, compute_op=ALU.add).then_inc(added[s][h], 16)

        def slot_added(eng, it, s, added):
            for h in range(2):
                wait(eng, added[s][h], 16 * (T // 2) * it)

        def all_added(pool, added):
            for s in range(2):
                for h in range(2):
                    pool.wait_ge(added[s][h], 16 * (T // 2) * (NG // 2))

        def spread_src(pe, it, s, row_in, equal, spread):
            pe.wait_ge(row_in[s], it + 1)
            wait(pe, equal[1 - s], before(it, s))
            for c in range(T):
                ins = nc.tensor.transpose(banks[c // 4][:, (c % 4) * P:(c % 4 + 1) * P],
                                          src_s[:, s, c:c + 1].to_broadcast([P, P]), ident[:, :])
            ins.then_inc(spread[s], 1)

        def equal_src(s, out):
            for q in range(2):
                ins = nc.vector.tensor_tensor(out[:, 4 * q:4 * q + 4, :],
                                              banks[q][:, :].rearrange("p (c e) -> p c e", c=4),
                                              src_s[:, s, 4 * q:4 * q + 4].unsqueeze(2).to_broadcast([P, 4, P]),
                                              ALU.is_equal)
            return ins

        def take_src(act, s, g, row_in):
            nc.scalar.copy(src_s[:, s, :], src_f[:, bass.ds(g, 1), :].rearrange("p a c -> p (a c)")).then_inc(row_in[s], 1)

        def window_rows(sp, table, width, at, first):
            return sp.dma_start(at, table[bass.ds(first, WIN), 0:width])

        def gin_stage():
            width = D + 1
            there, row_in, spread, equal, crossed, counted, totalled, addable, index, used = (
                slots(f"gin_{k}") for k in ("there", "rowin", "spread", "equal", "crossed", "counted", "totalled",
                                            "addable", "index", "used"))
            added = [slots(f"gin_added{s}") for s in range(2)]
            s_dup, s_xthere, s_xhot, s_xcross, s_xcount, s_xdone, begun = (
                edge_sem(f"gin_{k}") for k in ("dup", "xthere", "xhot", "xcross", "xcount", "xdone", "begun"))
            cross, xcross, totals = banks[2:4], banks[6:8], banks[4:6]
            counts = [squares[0:WIN, :, :], sq_sum[0:WIN, :, :]]
            counts_x = gath[0:WIN, 0, :, :]
            with nc.Block() as block:
                @block.sync
                def _(sp):
                    seen, start = register(sp, "gin_sp_seen"), register(sp, "gin_sp_start")

                    def group(it, s, g):
                        base = base_of(sp, g)
                        wait(sp, totalled[s], it)
                        window_rows(sp, tab_gin, width, win_x[0:WIN, s, :], base).then_inc(there[s], 16)
                        sp.reg_mov(start, base)

                        def window(k):
                            sp.reg_add(start, start, WIN)
                            sp.wait_ge(s_xdone, k + 1)
                            window_rows(sp, tab_gin, width, win_x[0:WIN, 2, :],
                                        sp.snap(start, min_val=0, max_val=NA - WIN)).then_inc(s_xthere, 16)
                        further_windows(sp, g, seen, window)
                    both(sp, group)

                @block.gpsimd
                def _(pool):
                    both(pool, lambda it, s, g: add_rows(pool, it, s, acc_gin, width, index, addable, added, begun))
                    all_added(pool, added)

                @block.scalar
                def _(act):
                    seen = register(act, "gin_act_seen")

                    def copy_counts(out, cross_banks):
                        for q in range(2):
                            ins = nc.scalar.copy(out[:, 4 * q:4 * q + 4, :],
                                                 cross_banks[q][0:WIN, :].rearrange("p (c e) -> p c e", c=4))
                        return ins

                    def group(it, s, g, final=False):
                        act.wait_ge(crossed[s], it + 1)
                        wait(act, totalled[s], it)
                        copy_counts(counts[s], cross).then_inc(counted[s], 1)

                        def window(k):
                            act.wait_ge(s_xcross, k + 1)
                            copy_counts(counts_x, xcross).then_inc(s_xcount, 1)
                        further_windows(act, g, seen, window)
                        act.wait_ge(totalled[s], it + 1)
                        slot_added(act, it, s, added)
                        for q in range(2):
                            ins = nc.scalar.copy(addend[:, s, 4 * q:4 * q + 4, 0:width],
                                                 totals[q][:, 0:4 * width].rearrange("p (c f) -> p c f", c=4))
                        ins.then_inc(addable[s], 1)
                        if not final:
                            act.wait_ge(used[s], it + 1)
                            take_src(act, s, g + 2, row_in)
                    take_src(act, 0, 0, row_in)
                    take_src(act, 1, 1, row_in)
                    both(act, group, NG // 2 - 1)
                    group(NG // 2 - 1, 0, NG - 2, final=True)
                    group(NG // 2 - 1, 1, NG - 1, final=True)

                @block.tensor
                def _(pe):
                    seen = register(pe, "gin_pe_seen")

                    def cross_product(out, hots, s):
                        for c in range(T):
                            ins = nc.tensor.matmul(out[c // 4][0:WIN, (c % 4) * P:(c % 4 + 1) * P], hots[:, c, :],
                                                   same[:, s, c, :], start=True, stop=True)
                        return ins

                    def total(out_counts, rows, first):
                        for c in range(T):
                            nc.tensor.matmul(totals[c // 4][:, (c % 4) * width:(c % 4 + 1) * width], out_counts[:, c, :],
                                             rows, start=first and c % 4 == 0, stop=True, skip_group_check=True)

                    def group(it, s, g, final=False):
                        pe.wait_ge(equal[s], it + 1)
                        wait(pe, counted[1 - s], before(it, s))
                        cross_product(cross, onehot_b[:, s, :, :], s).then_inc(crossed[s], 1)
                        if not (final and s == 1):
                            spread_src(pe, *slot_after(it, s), row_in, equal, spread)
                        pe.wait_ge(counted[s], it + 1)
                        pe.wait_ge(there[s], 16 * (it + 1))
                        wait(pe, addable[1 - s], before(it, s))
                        total(counts[s], win_x[0:WIN, s, :], True)

                        def window(k):
                            pe.wait_ge(s_xhot, k + 1)
                            cross_product(xcross, onehot_xb, s).then_inc(s_xcross, 1)
                            pe.wait_ge(s_xcount, k + 1)
                            pe.wait_ge(s_xthere, 16 * (k + 1))
                            total(counts_x, win_x[0:WIN, 2, :], False)
                            nc.tensor.matmul(totals[1][:, 0:1], zero_b[:, :], zero_b[:, 0:1], start=False, stop=True,
                                             skip_group_check=True).then_inc(s_xdone, 1)
                        further_windows(pe, g, seen, window)
                        nc.tensor.matmul(totals[1][:, 0:1], zero_b[:, :], zero_b[:, 0:1], start=False, stop=True,
                                         skip_group_check=True).then_inc(totalled[s], 1)
                    pe.sem_inc(s_xdone, 1)
                    spread_src(pe, 0, 0, row_in, equal, spread)
                    both(pe, group, NG // 2 - 1)
                    group(NG // 2 - 1, 0, NG - 2, final=True)
                    group(NG // 2 - 1, 1, NG - 1, final=True)

                @block.vector
                def _(dve):
                    seen = register(dve, "gin_dve_seen")

                    def group(it, s, g):
                        wait(dve, crossed[s], it)
                        is_window(onehot_b[:, s, :, :], group_rel(g))
                        dve.wait_ge(spread[s], it + 1)
                        equal_src(s, same[:, s, :, :]).then_inc(equal[s], 1)
                        dve.wait_ge(equal[s], it + 1)
                        nc.vector.tensor_tensor(earlier[:, :, :], same[:, s, :, :],
                                                lower_b[:, :].unsqueeze(1).to_broadcast([P, T, P]),
                                                ALU.mult).then_inc(s_dup, 1)
                        dve.wait_ge(s_dup, g * 4 + 1)
                        nc.vector.tensor_reduce(dup[:, 0, :], earlier[:, :, :], AX.X, ALU.max).then_inc(s_dup, 1)
                        nc.vector.tensor_scalar(dup[:, 1, :], src_s[:, s, :], -1.0, trash[:, 0:1], ALU.mult,
                                                ALU.add).then_inc(s_dup, 1)
                        dve.wait_ge(s_dup, g * 4 + 3)
                        nc.vector.tensor_tensor(dup[:, 0, :], dup[:, 0, :], dup[:, 1, :], ALU.mult).then_inc(s_dup, 1)
                        dve.wait_ge(s_dup, g * 4 + 4)
                        nc.vector.tensor_tensor(scat_i[:, bass.ds(g, 1), :].rearrange("p a c -> p (a c)"),
                                                dup[:, 0, :], src_s[:, s, :], ALU.add)
                        slot_added(dve, it, s, added)
                        nc.vector.tensor_tensor(idx_s[:, s, :], dup[:, 0, :], src_s[:, s, :], ALU.add).then_inc(index[s], 1)
                        dve.wait_ge(index[s], it + 1)
                        dve.sem_inc(used[s], 1)

                        def second():
                            dve.drain()
                            nc.vector.tensor_scalar(drel[:, :], group_rel(g), float(WIN), None, ALU.subtract)

                        def window(k):
                            dve.drain()
                            dve.wait_ge(s_xdone, k + 1)
                            is_window(onehot_xb[:, :, :], drel[:, :]).then_inc(s_xhot, 1)
                            dve.drain()
                            nc.vector.tensor_scalar(drel[:, :], drel[:, :], float(WIN), None, ALU.subtract)
                        further_windows(dve, g, seen, window, ahead=second)
                    both(dve, group)

        def mean_stage():
            there, rel_in, xrow, turned, filled, filled_o, mixed, relued, back, ready = (
                slots(f"mean_{k}") for k in ("there", "relin", "xrow", "turned", "filled", "filledo", "mixed", "relued",
                                             "back", "ready"))
            row_in, spread, equal, totalled, addable, index = (
                slots(f"mean_{k}") for k in ("rowin", "spread", "equal", "totalled", "addable", "index"))
            added = [slots(f"mean_added{s}") for s in range(2)]
            s_xthere, s_xhot, s_xdone, begun, s_pbegun = (
                edge_sem(f"mean_{k}") for k in ("xthere", "xhot", "xdone", "begun", "pbegun"))
            turn_b, mix_b, back_b, total_b = banks[2:4], banks[4:6], banks[6], banks[7]
            both_in = gath
            mixer = hid
            same32 = [acc[:, q, 0:T * P].rearrange("p (c e) -> p c e", e=P) for q in range(2)]
            relu_t = [acc[0:D, q, T * P:2 * T * P].rearrange("p (c e) -> p c e", e=P) for q in range(2)]
            rows = eattr
            mixer_x = squares
            with nc.Block() as block:
                @block.sync
                def _(sp):
                    seen, start = register(sp, "mean_sp_seen"), register(sp, "mean_sp_start")

                    def group(it, s, g, final=False):
                        at = both_in[:, s, :, 0:D]
                        if final and s == 1:
                            send_last_attributes(sp, at, tab_pre3, turned, there)
                        else:
                            send_attributes(sp, it, s, g, at, turned, there)
                        base = base_of(sp, g)
                        wait(sp, mixed[s], it)
                        window_rows(sp, tab_pre3, D, lhs3[D:P, s, :], base).then_inc(xrow[s], 16)
                        sp.reg_mov(start, base)

                        def window(k):
                            sp.reg_add(start, start, WIN)
                            sp.wait_ge(s_xdone, k + 1)
                            window_rows(sp, tab_pre3, D, lhs3[D:P, 2, :],
                                        sp.snap(start, min_val=0, max_val=NA - WIN)).then_inc(s_xthere, 16)
                        further_windows(sp, g, seen, window)
                    both(sp, group, NG // 2 - 1)
                    group(NG // 2 - 1, 0, NG - 2, final=True)
                    group(NG // 2 - 1, 1, NG - 1, final=True)

                @block.gpsimd
                def _(pool):
                    both(pool, lambda it, s, g: add_rows(pool, it, s, acc_mean, D, index, addable, added, begun))
                    all_added(pool, added)

                @block.scalar
                def _(act):
                    def take_rel(it, s, g):
                        wait(act, turned[s], it)
                        nc.scalar.copy(both_in[:, s, :, D:2 * D],
                                       group_rel(g).unsqueeze(2).to_broadcast([P, T, D])).then_inc(rel_in[s], 1)

                    def fill(it, s):
                        act.wait_ge(turned[s], it + 1)
                        wait(act, mixed[s], it)
                        for q in range(2):
                            ins = nc.scalar.copy(mixer[0:D, s, 4 * q:4 * q + 4, :],
                                                 turn_b[q][0:D, :].rearrange("p (c e) -> p c e", c=4))
                        ins.then_inc(filled[s], 1)

                    def group(it, s, g, final=False):
                        if not final:
                            take_rel(it + 1, s, g + 2)
                        act.wait_ge(mixed[s], it + 1)
                        wait(act, back[s], it)
                        for q in range(2):
                            ins = nc.scalar.activation(relu_t[s][:, 4 * q:4 * q + 4, :],
                                                       mix_b[q][0:D, :].rearrange("p (c e) -> p c e", c=4), ACT.Relu)
                        ins.then_inc(relued[s], 1)
                        if not (final and s == 1):
                            fill(*slot_after(it, s))
                        act.wait_ge(back[s], it + 1)
                        wait(act, totalled[s], it)
                        nc.scalar.copy(rows[:, s, :, :], back_b[:, :].rearrange("p (c f) -> p c f", f=D)).then_inc(ready[s], 1)
                        act.wait_ge(totalled[s], it + 1)
                        slot_added(act, it, s, added)
                        nc.scalar.copy(addend[:, s, :, 0:D], total_b[:, :].rearrange(
                            "p (c f) -> p c f", f=D)).then_inc(addable[s], 1)
                        if not final:
                            take_src(act, s, g + 2, row_in)
                    for s in range(2):
                        take_src(act, s, s, row_in)
                        take_rel(0, s, s)
                    fill(0, 0)
                    both(act, group, NG // 2 - 1)
                    group(NG // 2 - 1, 0, NG - 2, final=True)
                    group(NG // 2 - 1, 1, NG - 1, final=True)

                @block.tensor
                def _(pe):
                    seen = register(pe, "mean_pe_seen")

                    def turn(it, s, last=False):
                        pe.wait_ge(there[s], 16 * it + 16 * (N_LAST if last else 1))
                        pe.wait_ge(rel_in[s], it + 1)
                        wait(pe, filled[1 - s], before(it, s))
                        wait(pe, filled_o[1 - s], before(it, s))
                        for c in range(T):
                            ins = nc.tensor.transpose(turn_b[c // 4][:, (c % 4) * P:(c % 4 + 1) * P],
                                                      both_in[:, s, c, :], ident[:, :])
                        ins.then_inc(turned[s], 1)

                    def mix(lhs, rhs, first):
                        for q in range(2):
                            nc.tensor.matmul(mix_b[q][0:D, :], lhs,
                                             rhs[:, 4 * q:4 * q + 4, :].rearrange("p c e -> p (c e)"),
                                             start=first, stop=True, skip_group_check=True)

                    def group(it, s, g, final=False):
                        pe.wait_ge(filled[s], it + 1)
                        pe.wait_ge(filled_o[s], it + 1)
                        pe.wait_ge(xrow[s], 16 * (it + 1))
                        wait(pe, relued[1 - s], before(it, s))
                        mix(lhs3[:, s, :], mixer[:, s, :, :], True)

                        def window(k):
                            pe.wait_ge(s_xhot, k + 1)
                            pe.wait_ge(s_xthere, 16 * (k + 1))
                            mix(lhs3[:, 2, :], mixer_x[:, :, :], False)
                            nc.tensor.matmul(mix_b[1][0:D, 0:1], zero_b[:, 0:D], zero_b[:, 0:1], start=False, stop=True,
                                             skip_group_check=True).then_inc(s_xdone, 1)
                        further_windows(pe, g, seen, window)
                        nc.tensor.matmul(mix_b[1][0:D, 0:1], zero_b[:, 0:D], zero_b[:, 0:1], start=False, stop=True,
                                         skip_group_check=True).then_inc(mixed[s], 1)
                        if not (final and s == 1):
                            turn(*slot_after(it, s), last=final)
                        pe.wait_ge(relued[s], it + 1)
                        wait(pe, ready[1 - s], before(it, s))
                        pe.sem_inc(s_pbegun, 1)
                        for c in range(T):
                            ins = nc.tensor.transpose(back_b[:, c * D:(c + 1) * D], relu_t[s][:, c, :], ident[0:D, 0:D])
                        ins.then_inc(back[s], 1)
                        if not (final and s == 1):
                            spread_src(pe, *slot_after(it, s), row_in, equal, spread)
                        pe.wait_ge(ready[s], it + 1)
                        pe.wait_ge(equal[s], it + 1)
                        wait(pe, addable[1 - s], before(it, s))
                        for c in range(T):
                            ins = nc.tensor.matmul(total_b[:, c * D:(c + 1) * D], same32[s][:, c, :], rows[:, s, c, :],
                                                   start=True, stop=True)
                        ins.then_inc(totalled[s], 1)
                    pe.sem_inc(s_xdone, 1)
                    turn(0, 0)
                    spread_src(pe, 0, 0, row_in, equal, spread)
                    both(pe, group, NG // 2 - 1)
                    group(NG // 2 - 1, 0, NG - 2, final=True)
                    group(NG // 2 - 1, 1, NG - 1, final=True)

                @block.vector
                def _(dve):
                    seen = register(dve, "mean_dve_seen")

                    def fill_o(out, wcol):
                        for q in range(2):
                            ins = nc.vector.tensor_scalar(out[:, 4 * q:4 * q + 4, :],
                                                          turn_b[q][D:P, :].rearrange("p (c e) -> p c e", c=4),
                                                          wnode[D:P, wcol:wcol + 1], None, ALU.is_equal)
                        return ins

                    def group(it, s, g):
                        dve.wait_ge(turned[s], it + 1)
                        wait(dve, mixed[s], it)
                        fill_o(mixer[D:P, s, :, :], 0).then_inc(filled_o[s], 1)

                        def second():
                            dve.drain()
                            nc.vector.tensor_scalar(wnode[:, 1:2], wnode[:, 0:1], float(WIN), None, ALU.add)

                        def window(k):
                            dve.drain()
                            dve.wait_ge(s_xdone, k + 1)
                            fill_o(mixer_x[D:P, :, :], 1).then_inc(s_xhot, 1)
                            dve.drain()
                            nc.vector.tensor_scalar(wnode[:, 1:2], wnode[:, 1:2], float(WIN), None, ALU.add)
                        further_windows(dve, g, seen, window, ahead=second)
                        dve.wait_ge(spread[s], it + 1)
                        wait(dve, totalled[s], it)
                        equal_src(s, same32[s]).then_inc(equal[s], 1)
                        slot_added(dve, it, s, added)
                        nc.vector.tensor_copy(idx_s[:, s, :], scat_i[:, bass.ds(g, 1), :].rearrange(
                            "p a c -> p (a c)")).then_inc(index[s], 1)
                    nc.vector.memset(mixer_x[0:D, :, :], 0.0)
                    both(dve, group)

        def node_products(pe, q, lhs_t, rhs, s_m, s_a, first=0):
            if q >= 2:
                pe.wait_ge(s_a, q - 1)
            for k in range(CH):
                ins = nc.tensor.matmul(banks[first + q % 2][:, k * D:(k + 1) * D], lhs_t[:, k * P:(k + 1) * P], rhs,
                                       start=True, stop=True)
            ins.then_inc(s_m, 1)

        def chunk_nodes(q):
            return slice(q * CH * P, (q + 1) * CH * P)

        HALVES = ((0, 4), (4, CH))

        def chunk_to_features(pe, q, source, width, s_tr):
            for h, (b0, b1) in enumerate(HALVES):
                for k in range(b0, b1):
                    ins = nc.tensor.transpose(banks[h][0:width, (k - b0) * P:(k - b0 + 1) * P],
                                              source[:, CH * q + k, 0:width], ident[:, :])
            ins.then_inc(s_tr, 1)

        def chunk_to_features_copy(act, q, dst_t, width, s_tr, s_ev):
            act.wait_ge(s_tr, q + 1)
            for h, (b0, b1) in enumerate(HALVES):
                ins = nc.scalar.copy(dst_t[0:width, b0 * P:b1 * P], banks[h][0:width, 0:(b1 - b0) * P])
            ins.then_inc(s_ev, 1)

        def chunk(q, first=0):
            return banks[first + q % 2][:, 0:CH * D].rearrange("p (b f) -> p b f", f=D), slice(CH * q, CH * (q + 1))

        def over_nodes(row):
            return row.unsqueeze(1).to_broadcast([P, CH, D])

        def accumulator_chunk(q, width):
            return acc[:, q % 2, 0:T * CH * width].rearrange("p (c b f) -> p c b f", c=T, f=width)

        def load_accumulators(eng, tiles, accs, width, s_ld, s_sm):
            for q in range(NCH):
                if q >= 2:
                    eng.wait_ge(s_sm, q - 1)
                for c in tiles:
                    eng.dma_start(accumulator_chunk(q, width)[:, c], by_row(accs[c], slice(CH * q, CH * (q + 1)))
                                  ).then_inc(s_ld[q % 2], 16)

        def add_accumulators(dve, step, q, width, s_ld, s_sm):
            dve.wait_ge(s_ld[q % 2], 16 * T * (q // 2 + 1))
            a = accumulator_chunk(q, width)
            step(nc.vector.tensor_tensor(a[:, 0:4], a[:, 0:4], a[:, 4:8], ALU.add))
            step(nc.vector.tensor_tensor(a[:, 0:2], a[:, 0:2], a[:, 2:4], ALU.add))
            step(nc.vector.tensor_tensor(node_y[:, CH * q:CH * (q + 1), 0:width], a[:, 0], a[:, 1], ALU.add))
            dve.sem_inc(s_sm, 1)

        window_stage("mlp0", tab_pre0, mlp0=True)

        def write_chunks(sp, to, what, s_ready, s_written):
            for q in range(NCH):
                sp.wait_ge(s_ready, q + 1)
                bl = slice(CH * q, CH * (q + 1))
                sp.dma_start(to(bl), what(bl)).then_inc(s_written, 16)
            sp.wait_ge(s_written, 16 * NCH)

        C = lambda i: col[:, i:i + 1]
        HALF = 2 * NCH
        half = lambda j: slice(j * CW, (j + 1) * CW)
        in_half = lambda j: slice(j * CW, min((j + 1) * CW, N))
        s_sq, s_rt, s_scaled, s_a1, s_st, s_b1, s_lk, s_ms, s_sqs, s_norm, s_m3, s_e3, s_dg, s_dgr, s_di, s_y, s_var, \
            s_std, s_wr, s_gd = (sem(f"bn_{k}") for k in (
                "sq rt scaled a1 st b1 lk ms sqs norm m3 e3 dg dgr di y var std wr gd").split())
        with nc.Block() as block:
            @block.tensor
            def _(pe):
                for c in range(T):
                    ins = nc.tensor.matmul(banks[6][:, 0:1], sq_sum[:, c, :], ones[:, 0:1], start=(c == 0),
                                           stop=(c == T - 1))
                ins.then_inc(s_gd, 1)
                for j in range(HALF + 1):
                    if j < HALF:
                        pe.wait_ge(s_scaled, j + 1)
                        if j >= 2:
                            pe.wait_ge(s_st, j - 1)
                        nc.tensor.matmul(banks[j % 2][:, 0:CW], w0b[:, :], acc[:, 0, half(j)], start=True,
                                         stop=True).then_inc(s_a1, 1)
                    if j >= 1:
                        pe.wait_ge(s_st, j)
                        if j >= 3:
                            pe.wait_ge(s_lk, j - 2)
                        out_b = banks[2 + (j - 1) % 2][:, 0:CW]
                        nc.tensor.matmul(out_b, w0cx[:, :], nodes_t[0:D, half(j - 1)], start=True, stop=False)
                        nc.tensor.matmul(out_b, w0ca[:, :], stage[:, (j - 1) % 2, :], start=False,
                                         stop=True).then_inc(s_b1, 1)
                for q in range(NCH):
                    pe.wait_ge(s_norm, q + 1)
                    node_products(pe, q, acc[:, 0, chunk_nodes(q)], w0d[:, :], s_m3, s_e3)
                    for b in range(CH * q, CH * (q + 1)):
                        ins = nc.tensor.matmul(banks[7][:, b:b + 1], acc[0:1, 1, b * P:(b + 1) * P], ones[0:1, 0:1],
                                               start=True, stop=True)
                ins.then_inc(s_dg, 1)

            @block.scalar
            def _(act):
                act.wait_ge(s_sq, 1)
                nc.scalar.activation(C(S1), C(V1), ACT.Sqrt).then_inc(s_rt, 1)
                for j in range(HALF):
                    act.wait_ge(s_b1, j + 1)
                    nc.scalar.activation(acc[:, 0, half(j)], banks[2 + j % 2][:, 0:CW], ACT.Identity,
                                         bias=C(B3)).then_inc(s_lk, 1)
                act.wait_ge(s_ms, 1)
                for j in range(HALF):
                    nodes = in_half(j)
                    if j >= 2:
                        act.wait_ge(s_sqs, j - 1)
                    nc.scalar.activation(squares[:, (j % 2) * 4:(j % 2) * 4 + 4, :].rearrange("p c f -> p (c f)")[
                        :, 0:nodes.stop - nodes.start], acc[:, 0, nodes], ACT.Square, bias=C(NM2),
                        accum_out=parts[:, j:j + 1]).then_inc(s_sqs, 1)
                act.wait_ge(s_sq, 2)
                nc.scalar.activation(C(S1), C(V2), ACT.Sqrt).then_inc(s_rt, 1)
                for q in range(NCH):
                    layer_norm_root(act, q, s_var, s_std)
                act.wait_ge(s_dgr, 1)
                nc.scalar.activation(dinv[:, :], dinv[:, :], ACT.Sqrt).then_inc(s_di, 1)

            @block.vector
            def _(dve):
                step = stepper(dve, "bn_chain")
                step(nc.vector.tensor_reduce(C(M1), acc[:, 0, 0:N], AX.X, ALU.add))
                step(nc.vector.tensor_scalar(C(M1), C(M1), 1.0 / E, None, ALU.mult))
                step(nc.vector.tensor_tensor(C(Q1), C(M1), C(M1), ALU.mult))
                dve.wait_ge(s_gd, 1)
                step(nc.vector.tensor_scalar(C(V1), banks[6][:, 0:1], 1.0 / E, None, ALU.mult))
                step(nc.vector.tensor_tensor(C(V1), C(V1), C(Q1), ALU.subtract))
                step(nc.vector.tensor_scalar(C(V1), C(V1), 0.0, EPS, ALU.max, ALU.add))
                dve.sem_inc(s_sq, 1)
                dve.wait_ge(s_rt, 1)
                step(nc.vector.reciprocal(C(SC1), C(S1)))
                step(nc.vector.tensor_tensor(C(SC1), C(SC1), C(GB1), ALU.mult))
                step(nc.vector.tensor_tensor(C(SH1), C(M1), C(SC1), ALU.mult))
                step(nc.vector.tensor_tensor(C(SH1), C(GBE1), C(SH1), ALU.subtract))
                for j in range(HALF + 2):
                    if j < HALF:
                        step(nc.vector.tensor_scalar(acc[:, 0, half(j)], acc[:, 0, half(j)], C(SC1), None, ALU.mult))
                        nc.vector.scalar_tensor_tensor(out=acc[:, 0, half(j)], in0=acc[:, 1, half(j)], scalar=C(SH1),
                                                       in1=acc[:, 0, half(j)], op0=ALU.mult,
                                                       op1=ALU.add).then_inc(s_scaled, 1)
                    if 1 <= j <= HALF:
                        dve.wait_ge(s_a1, j)
                        if j >= 3:
                            dve.wait_ge(s_b1, j - 2)
                        nc.vector.scalar_tensor_tensor(out=stage[:, (j - 1) % 2, :], in0=acc[:, 1, half(j - 1)],
                                                       scalar=C(B2), in1=banks[(j - 1) % 2][:, 0:CW], op0=ALU.mult,
                                                       op1=ALU.add).then_inc(s_st, 1)
                    if j >= 2:
                        dve.wait_ge(s_lk, j - 1)
                        step(nc.vector.scalar_tensor_tensor(out=acc[:, 0, half(j - 2)], in0=acc[:, 0, half(j - 2)],
                                                            scalar=SLOPE, in1=acc[:, 0, half(j - 2)], op0=ALU.mult,
                                                            op1=ALU.max))
                        step(nc.vector.tensor_reduce(parts[:, j - 2:j - 1], acc[:, 0, in_half(j - 2)], AX.X, ALU.add))
                step(nc.vector.tensor_reduce(C(M2), parts[:, :], AX.X, ALU.add))
                step(nc.vector.tensor_scalar(C(M2), C(M2), 1.0 / N, None, ALU.mult))
                nc.vector.tensor_scalar(C(NM2), C(M2), -1.0, None, ALU.mult).then_inc(s_ms, 1)
                dve.wait_ge(s_sqs, HALF)
                step(nc.vector.tensor_reduce(C(Q1), parts[:, :], AX.X, ALU.add))
                nc.vector.tensor_scalar(C(V2), C(Q1), 1.0 / N, EPS, ALU.mult, ALU.add).then_inc(s_sq, 1)
                dve.wait_ge(s_rt, 2)
                step(nc.vector.reciprocal(C(SC2), C(S1)))
                step(nc.vector.tensor_tensor(C(SC2), C(SC2), C(G2), ALU.mult))
                step(nc.vector.tensor_tensor(C(SH2), C(M2), C(SC2), ALU.mult))
                step(nc.vector.tensor_tensor(C(SH2), C(BE2), C(SH2), ALU.subtract))
                for q in range(NCH + 3):
                    if q < NCH:
                        at = acc[:, 0, chunk_nodes(q)]
                        nc.vector.tensor_scalar(at, at, C(SC2), C(SH2), ALU.mult, ALU.add).then_inc(s_norm, 1)
                    if 2 <= q < NCH + 2:
                        dve.wait_ge(s_m3, q - 1)
                        got, bl = chunk(q - 2)
                        y = node_y[:, bl, 0:D]
                        step(nc.vector.tensor_tensor(y, got, over_nodes(bc[:, 1, 0:D]), ALU.add))
                        dve.sem_inc(s_e3, 1)
                        step(nc.vector.tensor_tensor(y, y, node_x[:, bl, :], ALU.add))
                        layer_norm(dve, step, q - 2, s_var)
                    if q >= 3:
                        layer_norm_end(dve, step, q - 3, s_std)
                        dve.sem_inc(s_y, 1)
                dve.wait_ge(s_dg, 1)
                nc.vector.tensor_scalar(dinv[:, :], banks[7][:, 0:NB], 1.0, None, ALU.add).then_inc(s_dgr, 1)
                dve.wait_ge(s_di, 1)
                nc.vector.reciprocal(dinv[:, :], dinv[:, :])

            @block.sync
            def _(sp):
                write_chunks(sp, lambda bl: by_row(tab[0], bl), lambda bl: node_x[:, bl, :], s_y, s_wr)

            @block.gpsimd
            def _(pool):
                retire(pool)

        window_stage("conv1", tab[0], mlp0=False)
        s_m, s_r, s_y, s_tr, s_ev, s_wr = (sem(f"c1_{k}") for k in "m r y tr ev wr".split())
        with nc.Block() as block:
            @block.tensor
            def _(pe):
                for q in range(NCH + 2):
                    if q < NCH:
                        node_products(pe, q, acc[0:D + 1, 0, chunk_nodes(q)], wc[:, 0, :], s_m, s_r, first=2)
                    if q >= 2:
                        pe.wait_ge(s_y, q - 1)
                        if q >= 3:
                            pe.wait_ge(s_ev, q - 2)
                        chunk_to_features(pe, q - 2, node_y, D, s_tr)

            @block.scalar
            def _(act):
                for q in range(NCH + 2):
                    if q < NCH:
                        act.wait_ge(s_m, q + 1)
                        got, bl = chunk(q, 2)
                        nc.scalar.activation(node_y[:, bl, 0:D], got, ACT.Relu).then_inc(s_r, 1)
                    if q >= 2:
                        chunk_to_features_copy(act, q - 2, acc[:, 0, chunk_nodes(q - 2)], D, s_tr, s_ev)

            @block.vector
            def _(dve):
                for q in range(NCH):
                    dve.wait_ge(s_r, q + 1)
                    bl = slice(CH * q, CH * (q + 1))
                    nc.vector.tensor_tensor(node_y[:, bl, 0:D], node_y[:, bl, 0:D],
                                            dinv[:, bl].unsqueeze(2).to_broadcast([P, CH, D]), ALU.mult).then_inc(s_y, 1)

            @block.sync
            def _(sp):
                write_chunks(sp, lambda bl: by_row(tab[1], bl), lambda bl: node_y[:, bl, 0:D], s_y, s_wr)

            @block.gpsimd
            def _(pool):
                retire(pool)

        window_stage("conv2", tab[1], mlp0=False)
        s_m2, s_r2, s_y2, s_wr2 = (sem(f"c2_{k}") for k in "m r y wr".split())
        with nc.Block() as block:
            @block.tensor
            def _(pe):
                for q in range(NCH):
                    node_products(pe, q, acc[0:D, 0, chunk_nodes(q)], wc[0:D, 1, :], s_m2, s_r2)

            @block.vector
            def _(dve):
                step = stepper(dve, "c2_chain")
                for q in range(NCH):
                    dve.wait_ge(s_m2, q + 1)
                    got, bl = chunk(q)
                    y = node_y[:, bl, 0:D]
                    step(nc.vector.tensor_tensor(y, got, dinv[:, bl].unsqueeze(2).to_broadcast([P, CH, D]), ALU.mult))
                    dve.sem_inc(s_r2, 1)
                    step(nc.vector.tensor_tensor(y, y, over_nodes(bc[:, 2, 0:D]), ALU.add))
                    nc.vector.tensor_scalar(y, y, 0.0, None, ALU.max).then_inc(s_y2, 1)

            @block.sync
            def _(sp):
                write_chunks(sp, lambda bl: by_row(tab[2], bl), lambda bl: node_y[:, bl, 0:D], s_y2, s_wr2)

            @block.gpsimd
            def _(pool):
                retire(pool)

        window_stage("conv3", tab[2], mlp0=False)
        s_m4, s_r4, s_y4, s_var4, s_std4, s_wr4 = (sem(f"c3_{k}") for k in "m r y var std wr".split())
        with nc.Block() as block:
            @block.tensor
            def _(pe):
                for q in range(NCH):
                    node_products(pe, q, acc[0:D + 1, 0, chunk_nodes(q)], wc[:, 2, :], s_m4, s_r4)

            @block.scalar
            def _(act):
                for q in range(NCH):
                    layer_norm_root(act, q, s_var4, s_std4)

            @block.vector
            def _(dve):
                step = stepper(dve, "c3_chain")
                nc.vector.memset(node_y[:, :, D:D + 1], 1.0)
                for q in range(NCH + 1):
                    if q < NCH:
                        dve.wait_ge(s_m4, q + 1)
                        got, bl = chunk(q)
                        step(nc.vector.tensor_tensor(node_y[:, bl, 0:D], got, node_x[:, bl, :], ALU.add))
                        dve.sem_inc(s_r4, 1)
                        layer_norm(dve, step, q, s_var4)
                    if q >= 1:
                        layer_norm_end(dve, step, q - 1, s_std4)
                        bl = slice(CH * (q - 1), CH * q)
                        nc.vector.tensor_copy(node_y[:, bl, 0:D], node_x[:, bl, :]).then_inc(s_y4, 1)

            @block.sync
            def _(sp):
                write_chunks(sp, lambda bl: node_rows(tab_gin[0:NP, :])[:, bl, :], lambda bl: node_y[:, bl, :],
                             s_y4, s_wr4)

            @block.gpsimd
            def _(pool):
                retire(pool)

        gin_stage()
        s_ld5 = [sem(f"g_ld{k}") for k in range(2)]
        s_sm5, s_in5, s_tr5, s_ev5, s_a5, s_h5, s_m5, s_r5, s_var5, s_std5, s_x5, s_tr6, s_ev6, s_m6, s_r6, s_wr5 = (
            sem(f"g_{k}") for k in "sm in tr ev a h m r var std x tr6 ev6 m6 r6 wr".split())
        with nc.Block() as block:
            @block.sync
            def _(sp):
                load_accumulators(sp, range(T), acc_gin, D + 1, s_ld5, s_sm5)
                write_chunks(sp, lambda bl: node_rows(tab_pre3[0:NP, :])[:, bl, :], lambda bl: node_y[:, bl, 0:D],
                             s_r6, s_wr5)

            @block.tensor
            def _(pe):
                for q in range(NCH + 4):
                    if q < NCH:
                        pe.wait_ge(s_in5, q + 1)
                        if q >= 5:
                            pe.wait_ge(s_ev6, q - 4)
                        elif q >= 1:
                            pe.wait_ge(s_ev5, q)
                        chunk_to_features(pe, q, node_y, D, s_tr5)
                        pe.wait_ge(s_ev5, q + 1)
                        for h in range(2):
                            j = 2 * q + h
                            if j >= 2:
                                pe.wait_ge(s_h5, j - 1)
                            nc.tensor.matmul(banks[2 + h][:, 0:CW], wg1[:, :], nodes_t[0:D, j * CW:(j + 1) * CW],
                                             start=True, stop=True).then_inc(s_a5, 1)
                        pe.wait_ge(s_h5, 2 * q + 2)
                        node_products(pe, q, stage[:, :, :].rearrange("p h n -> p (h n)"), wg2[:, :], s_m5, s_r5, first=4)
                    if q >= 4:
                        pe.wait_ge(s_x5, q - 3)
                        pe.wait_ge(s_ev5, min(q + 1, NCH))
                        if q >= 5:
                            pe.wait_ge(s_ev6, q - 4)
                        chunk_to_features(pe, q - 4, node_x, D, s_tr6)
                        pe.wait_ge(s_ev6, q - 3)
                        node_products(pe, q - 4, nodes_t[0:D, chunk_nodes(q - 4)], w3x[:, :], s_m6, s_r6, first=6)

            @block.scalar
            def _(act):
                for q in range(NCH + 4):
                    if q < NCH:
                        chunk_to_features_copy(act, q, nodes_t[:, chunk_nodes(q)], D, s_tr5, s_ev5)
                        for h in range(2):
                            j = 2 * q + h
                            act.wait_ge(s_a5, j + 1)
                            if q >= 1:
                                act.wait_ge(s_m5, q)
                            nc.scalar.activation(stage[:, h, :], banks[2 + h][:, 0:CW], ACT.Relu,
                                                 bias=C(BG1)).then_inc(s_h5, 1)
                    if 2 <= q < NCH + 2:
                        layer_norm_root(act, q - 2, s_var5, s_std5)
                    if q >= 4:
                        chunk_to_features_copy(act, q - 4, nodes_t[:, chunk_nodes(q - 4)], D, s_tr6, s_ev6)

            @block.vector
            def _(dve):
                step = stepper(dve, "g_chain")
                for q in range(NCH + 5):
                    if q < NCH:
                        bl = slice(CH * q, CH * (q + 1))
                        y = node_y[:, bl, 0:D]
                        add_accumulators(dve, step, q, D + 1, s_ld5, s_sm5)
                        nc.vector.tensor_copy(count[:, bl].unsqueeze(2), node_y[:, bl, D:D + 1])
                        nc.vector.tensor_tensor(y, y, node_x[:, bl, :], ALU.add).then_inc(s_in5, 1)
                    if 2 <= q < NCH + 2:
                        dve.wait_ge(s_m5, q - 1)
                        got, bl = chunk(q - 2, 4)
                        y = node_y[:, bl, 0:D]
                        step(nc.vector.tensor_tensor(y, got, over_nodes(bc[:, 3, 0:D]), ALU.add))
                        dve.sem_inc(s_r5, 1)
                        step(nc.vector.tensor_tensor(y, y, node_x[:, bl, :], ALU.add))
                        layer_norm(dve, step, q - 2, s_var5)
                    if 3 <= q < NCH + 3:
                        layer_norm_end(dve, step, q - 3, s_std5)
                        dve.sem_inc(s_x5, 1)
                    if q >= 5:
                        dve.wait_ge(s_m6, q - 4)
                        got, bl = chunk(q - 5, 6)
                        nc.vector.tensor_tensor(node_y[:, bl, 0:D], got, over_nodes(bc[:, 4, 0:D]),
                                                ALU.add).then_inc(s_r6, 1)

            @block.gpsimd
            def _(pool):
                retire(pool)

        mean_stage()
        s_ld7 = [sem(f"m_ld{k}") for k in range(2)]
        s_sm7, s_in7, s_tr7, s_ev7, s_a7, s_st7, s_b7, s_h7, s_m7, s_r7, s_var7, s_std7, s_x7, s_out = (
            sem(f"m_{k}") for k in "sm in tr ev a st b h m r var std x out".split())
        mean_t = onehot[:, :, :, :].rearrange("p s c n -> p (s c n)")[:, 0:CH * P]
        upd_t = squares[:, :, :].rearrange("p c f -> p (c f)")[0:D, 0:CH * P]
        with nc.Block() as block:
            @block.sync
            def _(sp):
                load_accumulators(sp, range(T), acc_mean, D, s_ld7, s_sm7)
                for q in range(NCH - 1):
                    sp.wait_ge(s_x7, q + 1)
                    sp.dma_start(node_rows(out[q * CH * P:(q + 1) * CH * P, :]),
                                 node_x[:, CH * q:CH * (q + 1), :]).then_inc(s_out, 16)
                sp.wait_ge(s_x7, NCH)
                sp.dma_start(node_rows(out[(NB - CH) * P:(NB - 1) * P, :]), node_x[:, NB - CH:NB - 1, :]).then_inc(s_out, 16)
                sp.dma_start(out[(NB - 1) * P:N, :], node_x[0:LB, NB - 1, :]).then_inc(s_out, 16)
                sp.wait_ge(s_out, 16 * (NCH + 1))

            @block.tensor
            def _(pe):
                for q in range(NCH):
                    pe.wait_ge(s_in7, q + 1)
                    if q >= 1:
                        pe.wait_ge(s_ev7, q)
                    chunk_to_features(pe, q, node_y, D + 1, s_tr7)
                    pe.wait_ge(s_ev7, q + 1)
                    for h in range(2):
                        if q >= 1:
                            pe.wait_ge(s_st7, 2 * q - 1 + h)
                        nc.tensor.matmul(banks[2 + h][0:D, 0:CW], w3b[:, :], mean_t[0:D + 1, h * CW:(h + 1) * CW],
                                         start=True, stop=True).then_inc(s_a7, 1)
                    for h in range(2):
                        j = 2 * q + h
                        pe.wait_ge(s_st7, j + 1)
                        if j >= 2:
                            pe.wait_ge(s_h7, j - 1)
                        nc.tensor.matmul(banks[4 + h][0:D, 0:CW], w3cx[:, :], nodes_t[0:D, j * CW:(j + 1) * CW],
                                         start=True, stop=False)
                        nc.tensor.matmul(banks[4 + h][0:D, 0:CW], w3ca[:, :], stage[0:D, h, :], start=False,
                                         stop=True).then_inc(s_b7, 1)
                    pe.wait_ge(s_h7, 2 * q + 2)
                    node_products(pe, q, upd_t, w3d[:, :], s_m7, s_r7, first=6)

            @block.scalar
            def _(act):
                for q in range(NCH + 2):
                    if q < NCH:
                        if q >= 1:
                            act.wait_ge(s_a7, 2 * q)
                        chunk_to_features_copy(act, q, mean_t, D + 1, s_tr7, s_ev7)
                        for h in range(2):
                            j = 2 * q + h
                            act.wait_ge(s_a7, j + 1)
                            if j >= 2:
                                act.wait_ge(s_b7, j - 1)
                            nc.scalar.copy(stage[0:D, h, :], banks[2 + h][0:D, 0:CW]).then_inc(s_st7, 1)
                        for h in range(2):
                            j = 2 * q + h
                            act.wait_ge(s_b7, j + 1)
                            if q >= 1:
                                act.wait_ge(s_m7, q)
                            nc.scalar.activation(upd_t[:, h * CW:(h + 1) * CW], banks[4 + h][0:D, 0:CW], ACT.Relu,
                                                 bias=col[0:D, B3A2:B3A2 + 1]).then_inc(s_h7, 1)
                    if q >= 2:
                        layer_norm_root(act, q - 2, s_var7, s_std7)

            @block.vector
            def _(dve):
                step = stepper(dve, "m_chain")
                step(nc.vector.tensor_scalar(inv_count[:, :], count[:, :], 1.0, None, ALU.max))
                step(nc.vector.reciprocal(inv_count[:, :], inv_count[:, :]))
                for q in range(NCH + 3):
                    if q < NCH:
                        bl = slice(CH * q, CH * (q + 1))
                        y, inv = node_y[:, bl, 0:D], inv_count[:, bl].unsqueeze(2)
                        add_accumulators(dve, step, q, D, s_ld7, s_sm7)
                        nc.vector.tensor_tensor(node_y[:, bl, D:D + 1], count[:, bl].unsqueeze(2), inv, ALU.mult)
                        nc.vector.tensor_tensor(y, y, inv.to_broadcast([P, CH, D]), ALU.mult).then_inc(s_in7, 1)
                    if 2 <= q < NCH + 2:
                        dve.wait_ge(s_m7, q - 1)
                        got, bl = chunk(q - 2, 6)
                        y = node_y[:, bl, 0:D]
                        step(nc.vector.tensor_tensor(y, got, over_nodes(bc[:, 1, D:2 * D]), ALU.add))
                        dve.sem_inc(s_r7, 1)
                        step(nc.vector.tensor_tensor(y, y, node_x[:, bl, :], ALU.add))
                        layer_norm(dve, step, q - 2, s_var7)
                    if q >= 3:
                        layer_norm_end(dve, step, q - 3, s_std7)
                        dve.sem_inc(s_x7, 1)

            @block.gpsimd
            def _(pool):
                retire(pool)


WEIGHTS = ["L0_gnn_W1", "L0_gnn_b1", "L0_gnn_g1", "L0_gnn_be1", "L0_gnn_W2", "L0_gnn_b2", "L0_gnn_W3", "L0_gnn_b3",
           "L0_gnn_g2", "L0_gnn_be2", "L0_gnn_W4", "L0_gnn_b4", "L1_gnn_W1", "L1_gnn_b1", "L1_gnn_W2", "L1_gnn_b2",
           "L1_gnn_W3", "L1_gnn_b3", "L2_gnn_W1", "L2_gnn_b1", "L2_gnn_W2", "L2_gnn_b2", "L3_gnn_W1a", "L3_gnn_b1a",
           "L3_gnn_W1b", "L3_gnn_b1b", "L3_gnn_W2a", "L3_gnn_b2a", "L3_gnn_W2b", "L3_gnn_b2b"]


def kernel(**inputs):
    import numpy as np
    import concourse.bacc as bacc
    from concourse.bass_utils import run_bass_kernel_spmd

    nc = bacc.Bacc("TRN2", target_bir_lowering=False, num_devices=1)
    arrays, handles = {}, {}
    for name in ["x", "src", "dst", "edge_attr_64"] + WEIGHTS:
        a = np.ascontiguousarray(inputs[name])
        arrays[f"in_{name}"] = a
        handles[name] = nc.dram_tensor(f"in_{name}", a.shape, mybir.dt.from_np(a.dtype), kind="ExternalInput").ap()
    out = nc.dram_tensor("out", (N, D), F32, kind="ExternalOutput").ap()
    build(nc, handles["x"], handles["src"], handles["dst"], handles["edge_attr_64"], {k: handles[k] for k in WEIGHTS}, out)
    return run_bass_kernel_spmd(nc, [arrays], core_ids=[0]).results[0]["out"]
```
